# Optimizing a Trainium2 kernel written in Bass

```python
import numpy as np
import jax
import jax.numpy as jnp

def _softmax(x, axis=-1):
    return jax.nn.softmax(x, axis=axis)

def _gelu(x):
    return jax.nn.gelu(x, approximate=True)

def _silu(x):
    return jax.nn.silu(x)

def _sigmoid(x):
    return jax.nn.sigmoid(x)

def _layernorm(x, axis=-1, eps=1e-05):
    m = jnp.mean(x, axis=axis, keepdims=True)
    v = jnp.var(x, axis=axis, keepdims=True)
    return (x - m) / jnp.sqrt(v + eps)

def _scatter_add(tgt, idx, src, axis=0):
    return tgt.at[idx].add(src)

def _segment_sum(src, seg, n):
    return jax.ops.segment_sum(src, seg, n)
kernel_name = 'mk_recurrent_d1_jaxref_r8_f6d5a3'

def setup_inputs(seed: int=0):
    np.random.seed(seed)
    _w = jnp.asarray

    def _L0_attn_setup():
        import jax, jax.numpy as jnp
        import numpy as np
        NF4 = jnp.array([-1.0, -0.6961928009986877, -0.5250730514526367, -0.39491748809814453, -0.28444138169288635, -0.18477343022823334, -0.09105003625154495, 0.0, 0.07958029955625534, 0.16093020141124725, 0.24611230194568634, 0.33791524171829224, 0.44070982933044434, 0.5626170039176941, 0.7229568362236023, 1.0], dtype=jnp.float32)
        BLOCK = 64

        def _dequant(codes, scales):
            w = NF4[codes]
            O, I = w.shape
            w = w.reshape(O, I // BLOCK, BLOCK) * scales[:, :, None]
            return w.reshape(O, I)

        def _lin_lora(x, W, A, B):
            base = jnp.einsum('bsh,oh->bso', x, W)
            lora = jnp.einsum('bsr,or->bso', jnp.einsum('bsh,rh->bsr', x, A), B)
            return base + lora
        H, I, R, BT, S = (512, 1792, 16, 2, 256)
        key = jax.random.key(seed)
        ks = jax.random.split(key, 12)
        x = jax.random.normal(ks[0], (BT, S, H), jnp.float32)
        codes_attn = jax.random.randint(ks[1], (4, H, H), 0, 16, jnp.int32)
        scales_attn = jax.random.uniform(ks[2], (4, H, H // BLOCK), jnp.float32) * 0.02
        codes_gu = jax.random.randint(ks[3], (2, I, H), 0, 16, jnp.int32)
        scales_gu = jax.random.uniform(ks[4], (2, I, H // BLOCK), jnp.float32) * 0.02
        codes_down = jax.random.randint(ks[5], (H, I), 0, 16, jnp.int32)
        scales_down = jax.random.uniform(ks[6], (H, I // BLOCK), jnp.float32) * 0.02
        lora_A_h = jax.random.normal(ks[7], (6, R, H), jnp.float32) * 0.02
        lora_A_down = jax.random.normal(ks[8], (R, I), jnp.float32) * 0.02
        lora_B_attn = jax.random.normal(ks[9], (4, H, R), jnp.float32) * 0.02
        lora_B_gu = jax.random.normal(ks[10], (2, I, R), jnp.float32) * 0.02
        lora_B_down = jax.random.normal(ks[11], (H, R), jnp.float32) * 0.02
        return dict(x=x, codes_attn=codes_attn, scales_attn=scales_attn, codes_gu=codes_gu, scales_gu=scales_gu, codes_down=codes_down, scales_down=scales_down, lora_A_h=lora_A_h, lora_A_down=lora_A_down, lora_B_attn=lora_B_attn, lora_B_gu=lora_B_gu, lora_B_down=lora_B_down)
    _L0_attn_in = _L0_attn_setup()

    def _L0_ffn_setup():
        import jax, jax.numpy as jnp
        import numpy as np
        HID, INTER = (512, 1792)
        B, S = (2, 256)

        def _binary_diff_weight(w, base):
            d = w - base
            coeff = jnp.mean(jnp.abs(d))
            return base + coeff * jnp.sign(d)
        key = jax.random.key(seed)
        ks = jax.random.split(key, 7)
        return {'hidden_states': jax.random.normal(ks[0], (B, S, HID), dtype=jnp.float32), 'w1': jax.random.normal(ks[1], (INTER, HID), dtype=jnp.float32) * 0.02, 'mean_w1': jax.random.normal(ks[2], (INTER, HID), dtype=jnp.float32) * 0.02, 'w2': jax.random.normal(ks[3], (HID, INTER), dtype=jnp.float32) * 0.02, 'mean_w2': jax.random.normal(ks[4], (HID, INTER), dtype=jnp.float32) * 0.02, 'w3': jax.random.normal(ks[5], (INTER, HID), dtype=jnp.float32) * 0.02, 'mean_w3': jax.random.normal(ks[6], (INTER, HID), dtype=jnp.float32) * 0.02}
    _L0_ffn_in = _L0_ffn_setup()
    _d = {'L0_attn_x': _L0_attn_in['x'], 'L0_attn_codes_attn': _L0_attn_in['codes_attn'], 'L0_attn_scales_attn': _L0_attn_in['scales_attn'], 'L0_attn_codes_gu': _L0_attn_in['codes_gu'], 'L0_attn_scales_gu': _L0_attn_in['scales_gu'], 'L0_attn_codes_down': _L0_attn_in['codes_down'], 'L0_attn_scales_down': _L0_attn_in['scales_down'], 'L0_attn_lora_A_h': _L0_attn_in['lora_A_h'], 'L0_attn_lora_A_down': _L0_attn_in['lora_A_down'], 'L0_attn_lora_B_attn': _L0_attn_in['lora_B_attn'], 'L0_attn_lora_B_gu': _L0_attn_in['lora_B_gu'], 'L0_attn_lora_B_down': _L0_attn_in['lora_B_down'], 'L0_ffn_w1': _L0_ffn_in['w1'], 'L0_ffn_mean_w1': _L0_ffn_in['mean_w1'], 'L0_ffn_w2': _L0_ffn_in['w2'], 'L0_ffn_mean_w2': _L0_ffn_in['mean_w2'], 'L0_ffn_w3': _L0_ffn_in['w3'], 'L0_ffn_mean_w3': _L0_ffn_in['mean_w3']}
    _x0 = _d['L0_attn_x']
    _d['L0_attn_x'] = jax.random.normal(jax.random.fold_in(jax.random.key(seed), 1), (4, 256, 512), dtype=_x0.dtype)
    del _x0
    return _d

def reference(L0_attn_x, L0_attn_codes_attn, L0_attn_scales_attn, L0_attn_codes_gu, L0_attn_scales_gu, L0_attn_codes_down, L0_attn_scales_down, L0_attn_lora_A_h, L0_attn_lora_A_down, L0_attn_lora_B_attn, L0_attn_lora_B_gu, L0_attn_lora_B_down, L0_ffn_w1, L0_ffn_mean_w1, L0_ffn_w2, L0_ffn_mean_w2, L0_ffn_w3, L0_ffn_mean_w3):

    def _L0_attn_ref(x, codes_attn, scales_attn, codes_gu, scales_gu, codes_down, scales_down, lora_A_h, lora_A_down, lora_B_attn, lora_B_gu, lora_B_down):
        import jax, jax.numpy as jnp
        import numpy as np
        NF4 = jnp.array([-1.0, -0.6961928009986877, -0.5250730514526367, -0.39491748809814453, -0.28444138169288635, -0.18477343022823334, -0.09105003625154495, 0.0, 0.07958029955625534, 0.16093020141124725, 0.24611230194568634, 0.33791524171829224, 0.44070982933044434, 0.5626170039176941, 0.7229568362236023, 1.0], dtype=jnp.float32)
        BLOCK = 64

        def _dequant(codes, scales):
            w = NF4[codes]
            O, I = w.shape
            w = w.reshape(O, I // BLOCK, BLOCK) * scales[:, :, None]
            return w.reshape(O, I)

        def _lin_lora(x, W, A, B):
            base = jnp.einsum('bsh,oh->bso', x, W)
            lora = jnp.einsum('bsr,or->bso', jnp.einsum('bsh,rh->bsr', x, A), B)
            return base + lora
        q = _lin_lora(x, _dequant(codes_attn[0], scales_attn[0]), lora_A_h[0], lora_B_attn[0])
        k = _lin_lora(x, _dequant(codes_attn[1], scales_attn[1]), lora_A_h[1], lora_B_attn[1])
        v = _lin_lora(x, _dequant(codes_attn[2], scales_attn[2]), lora_A_h[2], lora_B_attn[2])
        attn = (q + k + v) / 3.0
        o = _lin_lora(attn, _dequant(codes_attn[3], scales_attn[3]), lora_A_h[3], lora_B_attn[3])
        x1 = x + o
        g = _lin_lora(x1, _dequant(codes_gu[0], scales_gu[0]), lora_A_h[4], lora_B_gu[0])
        u = _lin_lora(x1, _dequant(codes_gu[1], scales_gu[1]), lora_A_h[5], lora_B_gu[1])
        h = jax.nn.silu(g) * u
        d = _lin_lora(h, _dequant(codes_down, scales_down), lora_A_down, lora_B_down)
        return x1 + d

    def _L0_ffn_ref(hidden_states, w1, mean_w1, w2, mean_w2, w3, mean_w3):
        import jax, jax.numpy as jnp
        import numpy as np
        HID, INTER = (512, 1792)
        B, S = (2, 256)

        def _binary_diff_weight(w, base):
            d = w - base
            coeff = jnp.mean(jnp.abs(d))
            return base + coeff * jnp.sign(d)
        W1 = _binary_diff_weight(w1, mean_w1)
        W2 = _binary_diff_weight(w2, mean_w2)
        W3 = _binary_diff_weight(w3, mean_w3)
        gate = jnp.einsum('bsh,ih->bsi', hidden_states, W1)
        up = jnp.einsum('bsh,ih->bsi', hidden_states, W3)
        h = jax.nn.silu(gate) * up
        return jnp.einsum('bsi,hi->bsh', h, W2)
    x = L0_attn_x
    xn = _layernorm(x, axis=-1)
    s = _L0_attn_ref(xn, L0_attn_codes_attn, L0_attn_scales_attn, L0_attn_codes_gu, L0_attn_scales_gu, L0_attn_codes_down, L0_attn_scales_down, L0_attn_lora_A_h, L0_attn_lora_A_down, L0_attn_lora_B_attn, L0_attn_lora_B_gu, L0_attn_lora_B_down)
    g = _silu(_L0_ffn_ref(xn, L0_ffn_w1, L0_ffn_mean_w1, L0_ffn_w2, L0_ffn_mean_w2, L0_ffn_w3, L0_ffn_mean_w3))
    x = x + s * g
    return x

_drawn_inputs = setup_inputs


def setup_inputs(seed=0):
    import zlib

    import numpy as np

    out = dict(_drawn_inputs(seed))
    spreads = {}
    factors = {'L0_attn_scales_attn': 8.0,
     'L0_attn_scales_gu': 8.0,
     'L0_attn_scales_down': 8.0,
     'L0_attn_lora_A_h': 8.0,
     'L0_attn_lora_A_down': 8.0,
     'L0_attn_lora_B_attn': 8.0,
     'L0_attn_lora_B_gu': 8.0,
     'L0_attn_lora_B_down': 8.0}
    for name, (base, spread) in spreads.items():
        noise = np.random.default_rng([zlib.crc32(name.encode()), seed]).standard_normal(out[name].shape)
        drawn = base * np.exp(spread * noise) if base else spread * noise
        out[name] = jnp.asarray(drawn.astype(out[name].dtype))
    for name, factor in factors.items():
        out[name] = (out[name] * factor).astype(out[name].dtype)
    return out
```

```python
import concourse.bass as bass
from concourse import mybir
from contextlib import ExitStack

P = 128
TOKENS, HID, INTER, RANK = 1024, 512, 1792, 16
BLOCK = 64
EPS = 1e-5
CHUNKS = INTER // P
HC = HID // P
TT = TOKENS // P
HALF = TOKENS // 2
TRIO = 3 * HID
PAIRS = CHUNKS // 2
SCAN = 1792
SCANS = INTER * HID // P // SCAN
SCAN_SLOTS = 3

NF4_STEP = 0.30380719900131226
NF4_OFFSET = 3.2915611267089844
NF4_RAMPS = [
    (0.4722318649291992, -0.5077152252197266, 6.19162654876709),
    (0.16412925720214844, -0.3930339813232422, 1.7030200958251953),
    (0.05514240264892578, -0.24013614654541016, 0.39171409606933594),
    (0.02811431884765625, -0.18800067901611328, 0.09946441650390625),
    (0.036876678466796875, -0.27657508850097656, 0.031052589416503906),
]
RAMPS = len(NF4_RAMPS)
GATE, UP, DOWN = 0, 1, 2
HI, LO = 0, 1
PASSES = [(HI, HI), (HI, LO), (LO, HI)]


def block_kernel(nc, x, codes_attn, scales_attn, codes_gu, scales_gu, codes_down, scales_down,
                 lora_A_h, lora_A_down, lora_B_attn, lora_B_gu, lora_B_down,
                 w1, mean_w1, w2, mean_w2, w3, mean_w3, out):
    f32, f32r, i32 = mybir.dt.float32, mybir.dt.float32r, mybir.dt.int32
    ALU, ACT, AX = mybir.AluOpType, mybir.ActivationFunctionType, mybir.AxisListType
    ds = bass.ds

    x_v = x.rearrange("b s h -> (b s) h").rearrange("(t p) h -> p t h", p=P)
    out_v = out.rearrange("b s h -> (b s) h").rearrange("(t p) h -> p t h", p=P)
    scan_v = [m.rearrange("(p a) n -> p (a n)", p=P) for m in (w1, mean_w1, w3, mean_w3, w2, mean_w2)]
    w2_v, mean_w2_v = (m.rearrange("(q p) i -> p q i", p=P) for m in (w2, mean_w2))
    codes_gu_v = codes_gu.rearrange("m i h -> i m h")
    codes_down_v = codes_down.rearrange("(q p) i -> p q i", p=P)
    codes_attn_v = codes_attn.rearrange("w o h -> o w h")

    ctx = ExitStack()
    with ctx:
        def sb(name, shape, dt=f32):
            return ctx.enter_context(nc.sbuf_tensor(name, shape, dt))

        def sem(name):
            return ctx.enter_context(nc.semaphore(name))

        ident = sb("ident", [P, P])
        ones = sb("ones", [P, P])
        stats = sb("stats", [P, TT, 6])
        moments = sb("moments", [P, TT, 2])
        ln = sb("ln", [P, 5, TT])
        inv_std = sb("inv_std", [P, TT])
        ramp_bias = sb("ramp_bias", [P, RAMPS])
        abs_sums = sb("abs_sums", [P, 3 * SCANS])
        abs_part = sb("abs_part", [P, 3])
        coeff = sb("coeff", [P, 3])
        xT = sb("xT", [P, 2, HC, TOKENS], f32r)
        h_split = sb("h_split", [P, 2, 2, TOKENS], f32r)
        staging = sb("staging", [P, TOKENS])
        downT = sb("downT", [P, 2, 2, HID], f32r)
        guT = sb("guT", [P, 2, 2, 2, HID], f32r)
        raw = sb("raw", [P, 2, TRIO])
        base = sb("base", [P, 2, TRIO])
        weight = sb("weight", [P, 2, TRIO])
        ramp = sb("ramp", [P, 2 * TRIO])
        silu_gate = sb("silu_gate", [P, TOKENS])
        y = sb("y", [P, TT, HID])
        scale_raw = sb("scale_raw", [P, CHUNKS, 2, 8])
        scale_down_raw = sb("scale_down_raw", [P, HC, 2 * CHUNKS])
        scale_trio = sb("scale_trio", [P, CHUNKS, 24])
        scale_attn_raw = sb("scale_attn_raw", [P, 4, 4, 8])
        scale_attn = sb("scale_attn", [P, 4, 4, 8])
        A_gu = sb("A_gu", [P, 2, HID], f32r)
        B_downT = sb("B_downT", [P, HID], f32r)
        A_down_now = sb("A_down_now", [P, 2, P], f32r)
        with nc.sbuf_tensor("scan", [P, SCAN_SLOTS, 2, SCAN], f32) as scan:
            pass
        with nc.sbuf_tensor("attn_codes", [P, 4, HID], f32) as attn_codes, \
                nc.sbuf_tensor("attn_sum", [P, 4, HID], f32) as attn_sum, \
                nc.sbuf_tensor("w_qkv", [P, 4, HID], f32) as w_qkv, \
                nc.sbuf_tensor("w_o", [P, 4, HID], f32) as w_o, \
                nc.sbuf_tensor("x1", [P, TT, HID], f32) as x1:
            pass
        MT = sb("MT", [P, 2, HC, HID], f32r)
        A_down = sb("A_down", [P, INTER], f32r)
        B_guT = sb("B_guT", [P, INTER], f32r)
        sb("x1_space", [P, 32 * 256 - 4 * HID * 2 - 2 * INTER + TT * HID])
        A_attn = x1[:, 0, :]
        B_qkvT = x1[:, 1, :]
        B_oT = x1[:, 2, :]
        B_attn_raw = x1[:, 3, 0:256].rearrange("p (j w r) -> p j w r", j=4, w=4)
        B_qkv_nat = x1[:, 4, 0:256].rearrange("p (j r) -> p j r", j=4)
        B_o_nat = x1[:, 4, 256:512].rearrange("p (j r) -> p j r", j=4)
        qkv_split = h_split[:, :, :, :].rearrange("p a b t -> p (a b t)").rearrange(
            "p (m s h) -> p m s h", m=4, s=2)
        oT_split = guT[:, :, :, :, :].rearrange("p a b c h -> p (a b c h)").rearrange(
            "p (s m h) -> p s m h", s=2, m=4)
        B_down_nat = ramp[:, 0:256].rearrange("p (j s r) -> p j s r", j=4, s=4)
        B_down_raw = ramp[:, 256:320].rearrange("p (j r) -> p j r", j=4)
        B_gu_raw = ramp[:, 320:768].rearrange("p (c m r) -> p c m r", c=CHUNKS, m=2)
        A_gu_raw = ramp[:, 768:1280]
        A_down_raw = ramp[:, 1280:1280 + INTER]
        HALF_CHUNKS = CHUNKS // 2
        B_gu_nat = [t[:, 0:HALF_CHUNKS * P].rearrange("p (c m s r) -> p c m s r", c=HALF_CHUNKS, m=2, s=4)
                    for t in (silu_gate, staging)]

        def pb(name):
            return ctx.enter_context(nc.psum_tensor(name, [P, 2, HALF], f32))

        gate_ps, up_ps, tr_ps, sum_ps = pb("gate_ps"), pb("up_ps"), pb("tr_ps"), pb("sum_ps")
        down_ps = [sum_ps[:, 0, :], sum_ps[:, 1, :], gate_ps[:, 0, :], gate_ps[:, 1, :],
                   sum_ps[:, 0, :], sum_ps[:, 1, :], up_ps[:, 0, :], up_ps[:, 1, :]]
        four_ps = [gate_ps[:, 0, :], gate_ps[:, 1, :], up_ps[:, 0, :], up_ps[:, 1, :]]

        x_loaded = [sem("x_loaded0"), sem("x_loaded1")]
        const_ready = sem("const_ready")
        ln_step = sem("ln_step")
        root_done = sem("root_done")
        xn_ready = sem("xn_ready")
        xT_tr = sem("xT_tr")
        xT_hi = sem("xT_hi")
        xT_lo = sem("xT_lo")
        scan_loaded = [sem(f"scan_loaded{n}") for n in range(SCAN_SLOTS)]
        scan_diff = sem("scan_diff")
        scan_abs = sem("scan_abs")
        part_ready = sem("part_ready")
        total_ready = sem("total_ready")
        coeff_ready = sem("coeff_ready")
        scales_loaded = sem("scales_loaded")
        scales_ready = sem("scales_ready")
        chunk_loaded = [sem("chunk_loaded0"), sem("chunk_loaded1")]
        diff_ready = sem("diff_ready")
        sign_ready = sem("sign_ready")
        ffn_weight = sem("ffn_weight")
        nf4_start = sem("nf4_start")
        nf4_ramp = sem("nf4_ramp")
        nf4_sum = sem("nf4_sum")
        nf4_weight = sem("nf4_weight")
        A_down_ready = sem("A_down_ready")
        tr_done = sem("tr_done")
        w_hi = sem("w_hi")
        w_lo = sem("w_lo")
        gate_done = sem("gate_done")
        up_done = sem("up_done")
        silu_done = sem("silu_done")
        h_done = sem("h_done")
        h_hi = sem("h_hi")
        h_lo = sem("h_lo")
        down_done = sem("down_done")
        y_done = sem("y_done")
        attn_loaded = sem("attn_loaded")
        gpsimd_passed = sem("gpsimd_passed")
        attn_start = sem("attn_start")
        attn_ramp = sem("attn_ramp")
        attn_acc = sem("attn_acc")
        attn_scaled = sem("attn_scaled")
        fold_loaded = sem("fold_loaded")
        B_nat_ready = sem("B_nat_ready")
        B_tr = sem("B_tr")
        B_T_ready = sem("B_T_ready")
        lora_qkv = sem("lora_qkv")
        qkv_full = sem("qkv_full")
        qkv_hi = sem("qkv_hi")
        qkv_lo = sem("qkv_lo")
        oT_tr = sem("oT_tr")
        oT_hi = sem("oT_hi")
        oT_lo = sem("oT_lo")
        MT_done = sem("MT_done")
        MT_hi = sem("MT_hi")
        MT_lo = sem("MT_lo")
        x_again = [sem("x_again0"), sem("x_again1")]
        xn_again = sem("xn_again")
        x1_sum = sem("x1_sum")
        x1_ready = sem("x1_ready")
        x1_tr = sem("x1_tr")
        x1_hi = sem("x1_hi")
        x1_lo = sem("x1_lo")
        lora_loaded = sem("lora_loaded")
        lora_zero = sem("lora_zero")
        lora_hi = sem("lora_hi")
        lora_lo = sem("lora_lo")
        A_low = sem("A_low")
        lora_tr = sem("lora_tr")
        lora_T = sem("lora_T")
        ffn_silu = sem("ffn_silu")
        x_last = sem("x_last")
        s_full = sem("s_full")
        gated = sem("gated")
        out_ready = sem("out_ready")
        out_stored = sem("out_stored")

        block = ctx.enter_context(nc.Block())

        def unit_index(block_no, c, kind):
            if block_no == 0 and isinstance(c, int) and c < 2:
                return {(0, GATE): 0, (0, UP): 1, (1, GATE): 2, (1, UP): 3, (0, DOWN): 4, (1, DOWN): 5}[c, kind]
            return 3 * (CHUNKS * block_no + c) + kind

        def slot_free(c):
            return {2: 5, 3: 6}[c] if isinstance(c, int) and c < 4 else 3 * c - 3

        def unit_bank(block_no, c_par, kind, first=False):
            if first:
                return c_par if kind == DOWN else kind
            return (3 * c_par + kind) % 2

        @block.sync
        def _(sp):
            for n in range(2):
                sp.dma_start(y[:, 4 * n:4 * n + 4, :], x_v[:, 4 * n:4 * n + 4, :]).then_inc(x_loaded[n], 16)

            def load_scan(k):
                m, part = k // SCANS, k % SCANS
                if k >= SCAN_SLOTS:
                    sp.wait_ge(scan_abs, k - SCAN_SLOTS + 1)
                for which in range(2):
                    sp.dma_start(scan[:, k % SCAN_SLOTS, which, :],
                                 scan_v[2 * m + which][:, part * SCAN:(part + 1) * SCAN]
                                 ).then_inc(scan_loaded[k % SCAN_SLOTS], 16)

            def load_ffn(c, par):
                if not (isinstance(c, int) and c < 2):
                    sp.wait_ge(ffn_weight, slot_free(c))
                for dst, gate, up, down in ((raw, w1, w3, w2_v), (base, mean_w1, mean_w3, mean_w2_v)):
                    sp.dma_start(dst[:, par, 0:HID], gate[ds(c * P, P), :]).then_inc(chunk_loaded[par], 16)
                    sp.dma_start(dst[:, par, HID:2 * HID], up[ds(c * P, P), :]).then_inc(chunk_loaded[par], 16)
                    sp.dma_start(dst[:, par, 2 * HID:].rearrange("p (q i) -> p q i", q=HC),
                                 down[:, :, ds(c * P, P)]).then_inc(chunk_loaded[par], 16)

            def load_nf4(k, par):
                if isinstance(k, int) and k < 2:
                    sp.wait_ge(ffn_weight, 3 * (CHUNKS - 2 + k) + 3)
                else:
                    sp.wait_ge(nf4_ramp, RAMPS * (k - 1))
                sp.dma_start(raw[:, par, 0:2 * HID].bitcast(i32).rearrange("p (m h) -> p m h", m=2),
                             codes_gu_v[ds(k * P, P), :, :]).then_inc(chunk_loaded[par], 16)
                sp.dma_start(raw[:, par, 2 * HID:].bitcast(i32).rearrange("p (q i) -> p q i", q=HC),
                             codes_down_v[:, :, ds(k * P, P)]).then_inc(chunk_loaded[par], 16)

            def load_attn(m):
                if not isinstance(m, int):
                    sp.wait_ge(attn_ramp, 2 * RAMPS * m)
                sp.dma_start(attn_codes[:, :, :].bitcast(i32), codes_attn_v[ds(m * P, P), :, :]
                             ).then_inc(attn_loaded, 16)

            for k in range(2 * SCANS):
                load_scan(k)
            load_ffn(0, 0)
            load_ffn(1, 1)
            for k in range(2 * SCANS, 3 * SCANS):
                load_scan(k)
            load_ffn(2, 0)
            load_ffn(3, 1)
            sp.wait_ge(scan_abs, 3 * SCANS)
            load_attn(0)
            sp.dma_start(A_attn[0:4 * RANK, :], lora_A_h[0:4].rearrange("w r h -> (w r) h")
                         ).then_inc(fold_loaded, 16)
            for j in range(4):
                sp.dma_start(B_attn_raw[:, j, :, :],
                             lora_B_attn[:, j * P:(j + 1) * P, :].rearrange("w p r -> p w r")
                             ).then_inc(fold_loaded, 16)
            load_ffn(4, 0)
            load_ffn(5, 1)
            with sp.Fori(1, 4) as i:
                load_ffn(2 * i + 4, 0)
                load_ffn(2 * i + 5, 1)
                load_attn(i)
            load_ffn(12, 0)
            load_ffn(13, 1)
            load_nf4(0, 0)
            load_nf4(1, 1)
            sp.wait_ge(nf4_sum, 2 * RAMPS)
            for m in range(2):
                for copy in range(4):
                    sp.dma_start(A_gu_raw[64 * m + 16 * copy:64 * m + 16 * copy + 16, :], lora_A_h[4 + m]
                                 ).then_inc(lora_loaded, 16)
                sp.dma_start(B_gu_raw[:, :, m, :], lora_B_gu[m].rearrange("(c p) r -> p c r", p=P)
                             ).then_inc(lora_loaded, 16)
            for copy in range(4):
                sp.dma_start(A_down_raw[16 * copy:16 * copy + 16, :], lora_A_down).then_inc(lora_loaded, 16)
            sp.dma_start(B_down_raw, lora_B_down.rearrange("(j p) r -> p j r", p=P)).then_inc(lora_loaded, 16)
            load_nf4(2, 0)
            load_nf4(3, 1)
            sp.wait_ge(oT_tr, 4)
            sp.wait_ge(lora_qkv, 4)
            for n in range(2):
                sp.dma_start(x1[:, 4 * n:4 * n + 4, :], x_v[:, 4 * n:4 * n + 4, :]).then_inc(x_again[n], 16)
            with sp.Fori(1, 6) as i:
                load_nf4(2 * i + 2, 0)
                load_nf4(2 * i + 3, 1)
            sp.wait_ge(nf4_sum, RAMPS * CHUNKS)
            sp.wait_ge(nf4_weight, CHUNKS)
            for n in range(2):
                for which, dst in enumerate((raw, base)):
                    t = 4 * n + 2 * which
                    sp.dma_start(dst[:, n, 0:2 * HID].rearrange("p (t h) -> p t h", t=2), x_v[:, t:t + 2, :]
                                 ).then_inc(x_last, 16)
            for t in range(TT):
                sp.wait_ge(out_ready, t + 1)
                sp.dma_start(out_v[:, t, :], y[:, t, :]).then_inc(out_stored, 16)
            sp.wait_ge(out_stored, 16 * TT)

        def last_x(t):
            buf = (raw, base)[(t % 4) // 2]
            return buf[:, t // 4, (t % 2) * HID:(t % 2 + 1) * HID]

        @block.gpsimd
        def _(pool):
            nc.gpsimd.memset(ident[:], 0.0).then_inc(const_ready, 1)
            nc.gpsimd.memset(ones[:], 1.0).then_inc(const_ready, 1)
            pool.wait_ge(const_ready, 2)
            nc.gpsimd.affine_select(out=ident[:], in_=ident[:], compare_op=ALU.not_equal, fill=1.0, base=0,
                                    pattern=[[-1, P]], channel_multiplier=1).then_inc(const_ready, 1)
            nc.gpsimd.memset(A_gu[:, :, :].bitcast(f32), 0.0).then_inc(lora_zero, 1)
            nc.gpsimd.memset(B_downT[:, :].bitcast(f32), 0.0).then_inc(lora_zero, 1)
            pool.wait_ge(scales_loaded, 16 * (2 + 4 + 1))
            nc.gpsimd.tensor_scalar(scale_trio[:, :, 0:16], scale_raw[:, :, :, :].rearrange("p c m b -> p c (m b)"),
                                    -NF4_STEP, 0.0, ALU.mult, ALU.add).then_inc(scales_ready, 1)
            for q in range(HC):
                nc.gpsimd.tensor_scalar(scale_trio[:, :, 16 + 2 * q:18 + 2 * q],
                                        scale_down_raw[:, q, :].rearrange("p (c b) -> p c b", b=2),
                                        -NF4_STEP, 0.0, ALU.mult, ALU.add).then_inc(scales_ready, 1)
            nc.gpsimd.tensor_scalar(scale_attn[:, :, 0:3, :], scale_attn_raw[:, :, 0:3, :],
                                    -NF4_STEP / 3.0, 0.0, ALU.mult, ALU.add).then_inc(scales_ready, 1)
            nc.gpsimd.tensor_scalar(scale_attn[:, :, 3, :], scale_attn_raw[:, :, 3, :],
                                    -NF4_STEP, 0.0, ALU.mult, ALU.add).then_inc(scales_ready, 1)
            pool.wait_ge(scales_ready, 3 + HC)
            nc.gpsimd.memset(ln[:, 4, 0:1], 0.0).then_inc(attn_scaled, 1)

            def counted(semaphore, count):
                pool.wait_ge(semaphore, count)
                pool.sem_inc(gpsimd_passed, 1)

            def ffn_diff_at(i, par):
                counted(chunk_loaded[par], 96 * i + 96)
                nc.gpsimd.tensor_tensor(raw[:, par, :], raw[:, par, :], base[:, par, :], ALU.subtract
                                        ).then_inc(diff_ready, 1)

            def nf4_scale(k, par):
                counted(nf4_sum, RAMPS * k + RAMPS)
                counted(tr_done, 3 * (CHUNKS + k) - 3)
                nc.gpsimd.tensor_tensor(
                    weight[:, par, :].rearrange("p (b n) -> p b n", n=BLOCK),
                    base[:, par, :].rearrange("p (b n) -> p b n", n=BLOCK),
                    scale_trio[:, ds(k, 1), :].rearrange("p a b -> p (a b)").unsqueeze(2).to_broadcast([P, 24, BLOCK]),
                    ALU.mult).then_inc(nf4_weight, 1)

            def A_down_chunk(k, par):
                counted(tr_done, 3 * (CHUNKS + k) - 3)
                nc.gpsimd.tensor_copy(A_down_now[:, par, :], A_down[:, ds(k * P, P)].bitcast(f32)
                                      ).then_inc(A_down_ready, 1)

            def attn_begin(m):
                counted(attn_loaded, 16 * m + 16)
                counted(attn_scaled, 5 * m + 1)
                nc.gpsimd.tensor_scalar(attn_sum[:, :, :], attn_codes[:, :, :].bitcast(i32), -1.0, NF4_OFFSET,
                                        ALU.mult, ALU.add).then_inc(attn_start, 1)

            def attn_scale(dst, m, w0, w1_):
                n = (w1_ - w0) * HID // BLOCK
                nc.gpsimd.tensor_tensor(
                    dst.rearrange("p w (b n) -> p (w b) n", n=BLOCK),
                    attn_sum[:, w0:w1_, :].rearrange("p w (b n) -> p (w b) n", n=BLOCK),
                    scale_attn[:, ds(m, 1), w0:w1_, :].rearrange("p a w b -> p (a w b)").unsqueeze(2)
                    .to_broadcast([P, n, BLOCK]), ALU.mult).then_inc(attn_scaled, 1)

            def attn_finish(m, half):
                counted(attn_acc, 2 + 2 * RAMPS * m + RAMPS * (half + 1))
                if half == 0:
                    attn_scale(attn_sum[:, 0:2, :], m, 0, 2)
                    counted(attn_scaled, 5 * m + 2)
                    nc.gpsimd.tensor_tensor(w_qkv[:, ds(m, 1), :], attn_sum[:, 0:1, :], attn_sum[:, 1:2, :],
                                            ALU.add).then_inc(attn_scaled, 1)
                else:
                    attn_scale(attn_sum[:, 2:3, :], m, 2, 3)
                    attn_scale(w_o[:, ds(m, 1), :], m, 3, 4)
                    counted(attn_scaled, 5 * m + 5)
                    nc.gpsimd.tensor_tensor(w_qkv[:, ds(m, 1), :], w_qkv[:, ds(m, 1), :], attn_sum[:, 2:3, :],
                                            ALU.add).then_inc(attn_scaled, 1)

            def make_nf4(k):
                for par in range(2):
                    nf4_scale(k + par, par)
                    A_down_chunk(k + par, par)

            ffn_diff_at(0, 0)
            ffn_diff_at(0, 1)
            for i in (1, 2):
                for par in range(2):
                    ffn_diff_at(i, par)
            with pool.Fori(1, 5) as i:
                attn_begin(i - 1)
                ffn_diff_at(i + 2, 0)
                attn_finish(i - 1, 0)
                ffn_diff_at(i + 2, 1)
                attn_finish(i - 1, 1)
            pool.wait_ge(scan_abs, 3 * SCANS)
            nc.gpsimd.memset(x1[:, 4, :], 0.0).then_inc(B_nat_ready, 1)
            pool.wait_ge(fold_loaded, 16 * 5)
            pool.wait_ge(B_nat_ready, 1)
            nc.gpsimd.tensor_copy(B_qkv_nat[:, :, 0:48].rearrange("p j (w r) -> p j w r", w=3),
                                  B_attn_raw[:, :, 0:3, :]).then_inc(B_nat_ready, 1)
            nc.gpsimd.tensor_copy(B_o_nat[:, :, 48:64], B_attn_raw[:, :, 3, :]).then_inc(B_nat_ready, 1)
            for par in range(2):
                nf4_scale(par, par)

            for m in range(4):
                pool.wait_ge(qkv_hi, m + 1)
                nc.gpsimd.tensor_tensor(qkv_split[:, m, LO, :], w_qkv[:, m, :],
                                        qkv_split[:, m, HI, :].bitcast(f32), ALU.subtract).then_inc(qkv_lo, 1)
            pool.wait_ge(lora_loaded, 16 * 15)
            for n in range(2):
                for s in (1, 3):
                    pool.wait_ge(lora_hi, 2 + 2 * n + 2)
                    nc.gpsimd.tensor_tensor(B_gu_nat[n][:, :, :, s, :],
                                            B_gu_raw[:, n * HALF_CHUNKS:(n + 1) * HALF_CHUNKS, :, :],
                                            B_gu_nat[n][:, :, :, 0, :], ALU.subtract).then_inc(lora_lo, 1)
            for s in (1, 3):
                pool.wait_ge(lora_hi, 8)
                nc.gpsimd.tensor_tensor(B_down_nat[:, :, s, :], B_down_raw, B_down_nat[:, :, 0, :],
                                        ALU.subtract).then_inc(lora_lo, 1)
            pool.wait_ge(A_low, 3)
            pool.wait_ge(lora_zero, 3)
            A_down_chunk(0, 0)
            A_down_chunk(1, 1)
            with pool.Fori(0, PAIRS - 1) as i:
                make_nf4(2 * i + 2)
            for t in range(TT):
                pool.wait_ge(x_last, 16 * 4)
                pool.wait_ge(gated, t + 1)
                nc.gpsimd.tensor_tensor(y[:, t, :], y[:, t, :], last_x(t), ALU.add).then_inc(out_ready, 1)

        @block.scalar
        def _(act):
            act.dma_start(scale_raw[:, :, 0, :], scales_gu[0].rearrange("(c p) b -> p c b", p=P)
                          ).then_inc(scales_loaded, 16)
            act.dma_start(scale_raw[:, :, 1, :], scales_gu[1].rearrange("(c p) b -> p c b", p=P)
                          ).then_inc(scales_loaded, 16)
            act.dma_start(scale_down_raw[:, :, :], scales_down.rearrange("(q p) b -> p q b", p=P)
                          ).then_inc(scales_loaded, 16)
            for m in range(4):
                act.dma_start(scale_attn_raw[:, m, :, :],
                              scales_attn[:, m * P:(m + 1) * P, :].rearrange("w p b -> p w b")
                              ).then_inc(scales_loaded, 16)
            act.wait_ge(ln_step, TT + 1)
            nc.scalar.activation(ln[:, 1, :], ln[:, 0, :], ACT.Sqrt).then_inc(root_done, 1)
            for t in range(TT):
                act.wait_ge(xT_tr, t + 1)
                nc.scalar.activation(xT[:, HI, :, t * P:(t + 1) * P],
                                     tr_ps[:, t % 2, :].rearrange("p (c t) -> p c t", c=HC), ACT.Copy
                                     ).then_inc(xT_hi, 1)

            def scan_sum(k):
                act.wait_ge(scan_diff, k + 1)
                nc.scalar.activation(scan[:, k % SCAN_SLOTS, 0, :], scan[:, k % SCAN_SLOTS, 0, :], ACT.Abs,
                                     accum_out=abs_sums[:, k:k + 1]).then_inc(scan_abs, 1)

            def ffn_sign(c, par):
                act.wait_ge(diff_ready, c + 1)
                nc.scalar.activation(raw[:, par, :], raw[:, par, :], ACT.Sign).then_inc(sign_ready, 1)

            def w_high(block_no, c, par, kind, first=False):
                act.wait_ge(tr_done, unit_index(block_no, c, kind) + 1)
                dst = downT[:, par, HI, :] if kind == DOWN else guT[:, par, kind, HI, :]
                nc.scalar.activation(dst, tr_ps[:, unit_bank(block_no, par, kind, first), :], ACT.Copy
                                     ).then_inc(w_hi, 1)

            def silu(n, th, first=False):
                act.wait_ge(gate_done, 2 * n + th + 1)
                if not first:
                    act.wait_ge(h_done, 2 * n + th - 1)
                nc.scalar.activation(silu_gate[:, th * HALF:(th + 1) * HALF], gate_ps[:, th, :], ACT.Silu
                                     ).then_inc(silu_done, 1)

            def h_high(n, par, th):
                act.wait_ge(h_done, 2 * n + th + 1)
                sl = slice(th * HALF, (th + 1) * HALF)
                nc.scalar.activation(h_split[:, par, HI, sl], up_ps[:, th, :], ACT.Copy).then_inc(h_hi, 1)

            def nf4_begin(k, par):
                act.wait_ge(chunk_loaded[par], 96 * PAIRS + 16 * (k - par) + 32)
                if isinstance(k, int) and k < 2:
                    act.wait_ge(ffn_weight, 3 * (CHUNKS - 2 + k) + 3)
                else:
                    act.wait_ge(nf4_weight, k - 1)
                nc.scalar.activation(base[:, par, :], raw[:, par, :].bitcast(i32), ACT.Copy, bias=NF4_OFFSET,
                                     scale=-1.0).then_inc(nf4_start, 1)

            def nf4_ramp_step(k, step):
                par, j = step // RAMPS, step % RAMPS
                slope, start, _ = NF4_RAMPS[j]
                r = RAMPS * k + step
                if j == 0:
                    nf4_begin(k + par, par)
                if not (isinstance(k, int) and r < 2):
                    act.wait_ge(nf4_sum, r - 1)
                nc.scalar.activation(ramp[:, (step % 2) * TRIO:(step % 2 + 1) * TRIO],
                                     raw[:, par, :].bitcast(i32), ACT.Relu, bias=ramp_bias[:, j:j + 1], scale=slope
                                     ).then_inc(nf4_ramp, 1)

            def attn_ramp_step(m, step):
                half, j = step // RAMPS, step % RAMPS
                slope, start, _ = NF4_RAMPS[j]
                if step == 0:
                    act.wait_ge(attn_start, m + 1)
                act.wait_ge(attn_acc, 2 * RAMPS * m + step + 1)
                nc.scalar.activation(ramp[:, (step % 2) * TRIO:(step % 2) * TRIO + 2 * HID],
                                     attn_codes[:, 2 * half:2 * half + 2, :].bitcast(i32).rearrange("p w h -> p (w h)"),
                                     ACT.Relu, bias=ramp_bias[:, j:j + 1], scale=slope).then_inc(attn_ramp, 1)

            def make(step, i, make_ffn, attn, make_nf4):
                if make_ffn and step == 6:
                    ffn_sign(2 * i + 4, 0)
                if attn is not None:
                    attn_ramp_step(attn, step)
                if make_nf4 is not None:
                    nf4_ramp_step(2 * make_nf4, step)

            def iteration(block_no, i, make_ffn=False, attn=None, make_nf4=None, last=False):
                n, a, b = CHUNKS * block_no + 2 * i, 2 * i, 2 * i + 1
                bg = (i, make_ffn, attn, make_nf4)
                w_high(block_no, a, 0, DOWN)
                make(0, *bg)
                make(1, *bg)
                silu(n, 0)
                w_high(block_no, b, 1, GATE)
                make(2, *bg)
                silu(n, 1)
                w_high(block_no, b, 1, UP)
                make(3, *bg)
                h_high(n, 0, 0)
                w_high(block_no, b, 1, DOWN)
                make(4, *bg)
                h_high(n, 0, 1)
                make(5, *bg)
                silu(n + 1, 0)
                make(6, *bg)
                silu(n + 1, 1)
                make(7, *bg)
                h_high(n + 1, 1, 0)
                make(8, *bg)
                h_high(n + 1, 1, 1)
                make(9, *bg)
                if not last:
                    w_high(block_no, a + 2, 0, GATE)
                if make_ffn:
                    ffn_sign(b + 4, 1)
                if not last:
                    w_high(block_no, a + 2, 0, UP)

            for k in range(2 * SCANS):
                scan_sum(k)
            ffn_sign(0, 0)
            ffn_sign(1, 1)
            act.wait_ge(xT_lo, TT)
            for c in range(2):
                for kind in (GATE, UP):
                    w_high(0, c, c, kind, first=True)
                if c == 0:
                    silu(0, 0, first=True)
                    silu(0, 1, first=True)
            scan_sum(2 * SCANS)
            h_high(0, 0, 0)
            scan_sum(2 * SCANS + 1)
            h_high(0, 0, 1)
            silu(1, 0)
            scan_sum(2 * SCANS + 2)
            silu(1, 1)
            h_high(1, 1, 0)
            h_high(1, 1, 1)
            scan_sum(2 * SCANS + 3)
            for c in range(2):
                w_high(0, c, c, DOWN, first=True)
            ffn_sign(2, 0)
            ffn_sign(3, 1)
            for kind in (GATE, UP):
                w_high(0, 2, 0, kind)
            ffn_sign(4, 0)
            ffn_sign(5, 1)
            with act.Fori(1, 5) as i:
                iteration(0, i, make_ffn=True, attn=i - 1)
            iteration(0, 5)
            act.wait_ge(attn_acc, 2 + 8 * RAMPS)
            iteration(0, 6, make_nf4=0, last=True)

            act.wait_ge(B_tr, 2)
            nc.scalar.activation(B_qkvT[0:64, :], tr_ps[0:64, 0, :], ACT.Copy, scale=1.0 / 3.0).then_inc(B_T_ready, 1)
            nc.scalar.activation(B_oT[0:64, :], tr_ps[0:64, 1, :], ACT.Copy).then_inc(B_T_ready, 1)
            for m in range(4):
                act.wait_ge(qkv_full, m + 1)
                nc.scalar.activation(qkv_split[:, m, HI, :], w_qkv[:, m, :], ACT.Copy).then_inc(qkv_hi, 1)
                act.wait_ge(oT_tr, m + 1)
                nc.scalar.activation(oT_split[:, HI, :, m * P:(m + 1) * P],
                                     tr_ps[:, m % 2, :].rearrange("p (c o) -> p c o", c=4), ACT.Copy
                                     ).then_inc(oT_hi, 1)
            act.wait_ge(lora_loaded, 16 * 15)
            act.wait_ge(lora_zero, 2)
            for m in range(2):
                rows = slice(64 * m, 64 * m + 64)
                nc.scalar.activation(A_gu[rows, m, :], A_gu_raw[rows, :], ACT.Copy).then_inc(lora_hi, 1)
            act.wait_ge(h_done, 4 * PAIRS)
            for n in range(2):
                for s in (0, 2):
                    nc.scalar.activation(B_gu_nat[n][:, :, :, s, :].bitcast(f32r),
                                         B_gu_raw[:, n * HALF_CHUNKS:(n + 1) * HALF_CHUNKS, :, :], ACT.Copy
                                         ).then_inc(lora_hi, 1)
            for s in (0, 2):
                nc.scalar.activation(B_down_nat[:, :, s, :].bitcast(f32r), B_down_raw, ACT.Copy).then_inc(lora_hi, 1)
            act.wait_ge(qkv_hi, 4)
            act.wait_ge(qkv_lo, 4)
            nc.scalar.activation(A_down[0:64, :], A_down_raw[0:64, :], ACT.Copy).then_inc(lora_hi, 1)
            for c in range(HC):
                act.wait_ge(MT_done, c + 1)
                nc.scalar.activation(MT[:, HI, c, :], four_ps[c], ACT.Copy).then_inc(MT_hi, 1)
            for n in range(5):
                act.wait_ge(lora_tr, n + 1)
                if n < 4:
                    w = min(4, CHUNKS - 4 * n) * P
                    nc.scalar.activation(B_guT[:, 4 * n * P:4 * n * P + w], tr_ps[:, n % 2, 0:w], ACT.Copy
                                         ).then_inc(lora_T, 1)
                else:
                    nc.scalar.activation(B_downT[0:64, :], tr_ps[0:64, n % 2, :], ACT.Copy).then_inc(lora_T, 1)
            for t in range(TT):
                act.wait_ge(x1_tr, t + 1)
                nc.scalar.activation(xT[:, HI, :, t * P:(t + 1) * P],
                                     tr_ps[:, t % 2, :].rearrange("p (c t) -> p c t", c=HC), ACT.Copy
                                     ).then_inc(x1_hi, 1)
            for kind in (GATE, UP):
                w_high(1, 0, 0, kind)
            act.wait_ge(y_done, TT * PAIRS)
            nc.scalar.activation(y[:, :, :].rearrange("p t h -> p (t h)"), y[:, :, :].rearrange("p t h -> p (t h)"),
                                 ACT.Silu).then_inc(ffn_silu, 1)
            with act.Fori(0, 6) as i:
                iteration(1, i, make_nf4=i + 1)
            iteration(1, 6, last=True)

        @block.vector
        def _(dve):
            for j, (_, start, _) in enumerate(NF4_RAMPS):
                nc.vector.memset(ramp_bias[:, j:j + 1], start)
            for t in range(TT):
                dve.wait_ge(x_loaded[t // 4], 16)
                nc.vector.bn_stats(stats[:, t, :], y[:, t, :]).then_inc(ln_step, 1)
            ln_count = TT
            dve.wait_ge(ln_step, TT)
            for t in range(TT):
                last = nc.vector.bn_aggr(moments[:, t, :], stats[:, t, :])
            last.then_inc(xn_ready, 1)
            dve.wait_ge(xn_ready, 1)
            nc.vector.tensor_scalar(ln[:, 0, :], moments[:, :, 1], EPS, None, ALU.add).then_inc(ln_step, 1)
            dve.wait_ge(root_done, 1)
            nc.vector.reciprocal(ln[:, 2, :], ln[:, 1, :]).then_inc(xn_ready, 1)
            dve.wait_ge(xn_ready, 2)
            nc.vector.tensor_tensor(ln[:, 2, :], ln[:, 2, :], ln[:, 0, :], ALU.mult).then_inc(xn_ready, 1)
            dve.wait_ge(xn_ready, 3)
            nc.vector.tensor_tensor(ln[:, 2, :], ln[:, 2, :], ln[:, 1, :], ALU.add).then_inc(xn_ready, 1)
            dve.wait_ge(xn_ready, 4)
            nc.vector.tensor_scalar(ln[:, 3, :], ln[:, 2, :], 0.5, None, ALU.mult).then_inc(xn_ready, 1)
            dve.wait_ge(xn_ready, 5)
            nc.vector.reciprocal(inv_std[:, :], ln[:, 3, :]).then_inc(xn_ready, 1)
            dve.wait_ge(xn_ready, 6)

            def normalise(buf, t, done):
                nc.vector.tensor_scalar(buf[:, t, :], buf[:, t, :], moments[:, t, 0:1], inv_std[:, t:t + 1],
                                        ALU.subtract, ALU.mult).then_inc(done, 1)

            def scan_subtract(k):
                dve.wait_ge(scan_loaded[k % SCAN_SLOTS], 32 * (k // SCAN_SLOTS) + 32)
                nc.vector.tensor_tensor(scan[:, k % SCAN_SLOTS, 0, :], scan[:, k % SCAN_SLOTS, 0, :],
                                        scan[:, k % SCAN_SLOTS, 1, :], ALU.subtract).then_inc(scan_diff, 1)

            for t in range(TT):
                normalise(y, t, xn_ready)
            for t in range(TT):
                dve.wait_ge(xT_hi, t + 1)
                nc.vector.tensor_tensor(xT[:, LO, :, t * P:(t + 1) * P],
                                        tr_ps[:, t % 2, :].rearrange("p (c t) -> p c t", c=HC),
                                        xT[:, HI, :, t * P:(t + 1) * P].bitcast(f32), ALU.subtract
                                        ).then_inc(xT_lo, 1)

            def sum_part(m):
                dve.wait_ge(scan_abs, SCANS * (m + 1))
                nc.vector.tensor_reduce(abs_part[:, m:m + 1], abs_sums[:, SCANS * m:SCANS * (m + 1)],
                                        axis=AX.X, op=ALU.add).then_inc(part_ready, 1)

            def take_coeff(m0, m1, count):
                dve.wait_ge(total_ready, count)
                nc.vector.tensor_scalar(coeff[:, m0:m1], sum_ps[:, 0, m0:m1], 1.0 / (INTER * HID), None, ALU.mult
                                        ).then_inc(coeff_ready, 1)
                dve.wait_ge(coeff_ready, count)

            def ffn_make(c, par, kind):
                dve.wait_ge(sign_ready, c + 1)
                if not (isinstance(c, int) and c < 2):
                    dve.wait_ge(tr_done, slot_free(c))
                sl = slice(kind * HID, (kind + 1) * HID)
                nc.vector.scalar_tensor_tensor(weight[:, par, sl], raw[:, par, sl], coeff[:, kind:kind + 1],
                                               base[:, par, sl], ALU.mult, ALU.add).then_inc(ffn_weight, 1)

            def w_low(block_no, c, par, kind, first=False):
                dve.wait_ge(w_hi, unit_index(block_no, c, kind) + 1)
                buf = downT[:, par] if kind == DOWN else guT[:, par, kind]
                nc.vector.tensor_tensor(buf[:, LO, :], tr_ps[:, unit_bank(block_no, par, kind, first), :],
                                        buf[:, HI, :].bitcast(f32), ALU.subtract).then_inc(w_lo, 1)

            def h_make(n, th):
                dve.wait_ge(silu_done, 2 * n + th + 1)
                dve.wait_ge(up_done, 2 * n + th + 1)
                nc.vector.tensor_tensor(up_ps[:, th, :], silu_gate[:, th * HALF:(th + 1) * HALF], up_ps[:, th, :],
                                        ALU.mult).then_inc(h_done, 1)

            def h_low(n, par, th):
                dve.wait_ge(h_hi, 2 * n + th + 1)
                sl = slice(th * HALF, (th + 1) * HALF)
                nc.vector.tensor_tensor(h_split[:, par, LO, sl], up_ps[:, th, :],
                                        h_split[:, par, HI, sl].bitcast(f32), ALU.subtract).then_inc(h_lo, 1)

            def nf4_add(k, step):
                par, j = step // RAMPS, step % RAMPS
                r = RAMPS * k + step
                dve.wait_ge(nf4_ramp, r + 1)
                if not (isinstance(k, int) and r < 1):
                    dve.wait_ge(nf4_sum, r)
                nc.vector.scalar_tensor_tensor(base[:, par, :], ramp[:, (step % 2) * TRIO:(step % 2 + 1) * TRIO],
                                               NF4_RAMPS[j][2], base[:, par, :], ALU.min, ALU.add
                                               ).then_inc(nf4_sum, 1)

            def attn_add(m, step):
                half, j = step // RAMPS, step % RAMPS
                dve.wait_ge(attn_ramp, 2 * RAMPS * m + step + 1)
                dve.wait_ge(attn_acc, 2 * RAMPS * m + step + 2)
                dst = attn_sum[:, 2 * half:2 * half + 2, :].rearrange("p w h -> p (w h)")
                nc.vector.scalar_tensor_tensor(dst, ramp[:, (step % 2) * TRIO:(step % 2) * TRIO + 2 * HID],
                                               NF4_RAMPS[j][2], dst, ALU.min, ALU.add).then_inc(attn_acc, 1)

            def y_add(block_no, i, t, first=False, last=False):
                done = TT * (PAIRS * block_no + i) + t
                dve.wait_ge(down_done, done + 1)
                if block_no == 0:
                    if first:
                        nc.vector.tensor_copy(y[:, t, :], down_ps[t]).then_inc(y_done, 1)
                    else:
                        dve.wait_ge(y_done, done - TT + 1)
                        nc.vector.tensor_tensor(y[:, t, :], y[:, t, :], down_ps[t], ALU.add
                                                ).then_inc(y_done, 1)
                else:
                    if isinstance(i, int) and i == 0:
                        dve.wait_ge(x1_ready, t + 1)
                    else:
                        dve.wait_ge(y_done, done - TT + 1)
                    nc.vector.tensor_tensor(x1[:, t, :], x1[:, t, :], down_ps[t], ALU.add
                                            ).then_inc(y_done, 1)
                    if last:
                        dve.wait_ge(y_done, done + 1)
                        if t == 0:
                            dve.wait_ge(ffn_silu, 1)
                        nc.vector.tensor_tensor(y[:, t, :], x1[:, t, :], y[:, t, :], ALU.mult).then_inc(gated, 1)

            def make(step, i, make_ffn, attn, make_nf4):
                if make_ffn and step % RAMPS == 0:
                    for kind in (GATE, UP, DOWN):
                        ffn_make(2 * i + 2 + step // RAMPS, step // RAMPS, kind)
                if attn is not None:
                    attn_add(attn, step)
                if make_nf4 is not None:
                    nf4_add(2 * make_nf4, step)

            def iteration(block_no, i, make_ffn=False, attn=None, make_nf4=None, last=False):
                n, a, b = CHUNKS * block_no + 2 * i, 2 * i, 2 * i + 1
                bg = (i, make_ffn, attn, make_nf4)
                w_low(block_no, a, 0, DOWN)
                make(0, *bg)
                make(1, *bg)
                w_low(block_no, b, 1, GATE)
                make(2, *bg)
                w_low(block_no, b, 1, UP)
                make(3, *bg)
                h_make(n, 0)
                w_low(block_no, b, 1, DOWN)
                h_low(n, 0, 0)
                h_make(n, 1)
                make(4, *bg)
                h_low(n, 0, 1)
                make(5, *bg)
                make(6, *bg)
                make(7, *bg)
                h_make(n + 1, 0)
                h_low(n + 1, 1, 0)
                h_make(n + 1, 1)
                h_low(n + 1, 1, 1)
                for t in range(TT):
                    y_add(block_no, i, t, last=last and block_no == 1)
                    if t == 0:
                        make(8, *bg)
                    if t == 2:
                        make(9, *bg)
                    if t == 3 and not last:
                        w_low(block_no, a + 2, 0, GATE)
                    if t == 5 and not last:
                        w_low(block_no, a + 2, 0, UP)

            for k in range(2 * SCANS):
                scan_subtract(k)
            sum_part(0)
            sum_part(1)
            take_coeff(0, 2, 1)
            for c in range(2):
                ffn_make(c, c, GATE)
                ffn_make(c, c, UP)
            for c in range(2):
                for kind in (GATE, UP):
                    w_low(0, c, c, kind, first=True)
            scan_subtract(2 * SCANS)
            h_make(0, 0)
            scan_subtract(2 * SCANS + 1)
            h_low(0, 0, 0)
            h_make(0, 1)
            scan_subtract(2 * SCANS + 2)
            h_low(0, 0, 1)
            h_make(1, 0)
            h_low(1, 1, 0)
            scan_subtract(2 * SCANS + 3)
            h_make(1, 1)
            h_low(1, 1, 1)
            nc.vector.memset(ln[:, 2, 0:1], 0.0).then_inc(attn_acc, 1)
            nc.vector.memset(ln[:, 2, 1:2], 0.0).then_inc(attn_acc, 1)
            sum_part(2)
            take_coeff(2, 3, 2)
            for c in range(2):
                ffn_make(c, c, DOWN)
            for c in range(2):
                w_low(0, c, c, DOWN, first=True)
            for t in range(TT):
                y_add(0, 0, t, first=True)
                if t == 3:
                    for kind in (GATE, UP, DOWN):
                        ffn_make(2, 0, kind)
                    w_low(0, 2, 0, GATE)
                if t == 5:
                    w_low(0, 2, 0, UP)
            for kind in (GATE, UP, DOWN):
                ffn_make(3, 1, kind)
            with dve.Fori(1, 5) as i:
                iteration(0, i, make_ffn=True, attn=i - 1)
            iteration(0, 5, make_ffn=True)
            iteration(0, 6, make_nf4=0, last=True)

            for m in range(4):
                dve.wait_ge(lora_qkv, m + 1)
                dve.wait_ge(attn_scaled, 5 * 4 + 1)
                nc.vector.tensor_tensor(w_qkv[:, m, :], w_qkv[:, m, :], four_ps[m], ALU.add).then_inc(qkv_full, 1)
                dve.wait_ge(oT_hi, m + 1)
                nc.vector.tensor_tensor(oT_split[:, LO, :, m * P:(m + 1) * P],
                                        tr_ps[:, m % 2, :].rearrange("p (c o) -> p c o", c=4),
                                        oT_split[:, HI, :, m * P:(m + 1) * P].bitcast(f32), ALU.subtract
                                        ).then_inc(oT_lo, 1)
            for t in range(TT):
                dve.wait_ge(x_again[t // 4], 16)
                normalise(x1, t, xn_again)
            dve.wait_ge(oT_tr, 4)
            dve.wait_ge(qkv_lo, 4)
            nc.vector.memset(A_down[64:128, :].bitcast(f32), 0.0).then_inc(lora_zero, 1)
            for m in range(2):
                rows = slice(64 * m + 32, 64 * m + 64)
                dve.wait_ge(lora_hi, m + 1)
                nc.vector.tensor_tensor(A_gu[rows, m, :], A_gu_raw[rows, :], A_gu[rows, m, :].bitcast(f32),
                                        ALU.subtract).then_inc(A_low, 1)
            dve.wait_ge(lora_hi, 9)
            nc.vector.tensor_tensor(A_down[32:64, :], A_down_raw[32:64, :], A_down[32:64, :].bitcast(f32),
                                    ALU.subtract).then_inc(A_low, 1)
            for c in range(HC):
                dve.wait_ge(MT_hi, c + 1)
                nc.vector.tensor_tensor(MT[:, LO, c, :], four_ps[c], MT[:, HI, c, :].bitcast(f32), ALU.subtract
                                        ).then_inc(MT_lo, 1)
            for t in range(TT + 1):
                if t < TT:
                    dve.wait_ge(x1_sum, t + 1)
                    dve.wait_ge(xn_again, t + 1)
                    nc.vector.tensor_tensor(x1[:, t, :], x1[:, t, :], sum_ps[:, t % 2, :], ALU.add
                                            ).then_inc(x1_ready, 1)
                if t > 0:
                    u = t - 1
                    dve.wait_ge(x1_hi, u + 1)
                    nc.vector.tensor_tensor(xT[:, LO, :, u * P:(u + 1) * P],
                                            tr_ps[:, u % 2, :].rearrange("p (c t) -> p c t", c=HC),
                                            xT[:, HI, :, u * P:(u + 1) * P].bitcast(f32), ALU.subtract
                                            ).then_inc(x1_lo, 1)
            for kind in (GATE, UP):
                w_low(1, 0, 0, kind)
            with dve.Fori(0, 6) as i:
                iteration(1, i, make_nf4=i + 1)
            iteration(1, 6, last=True)

        @block.tensor
        def _(pe):
            def transpose4(bank, src, accumulate=False):
                for c in range(HC):
                    last = nc.tensor.matmul(tr_ps[:, bank, c * P:(c + 1) * P], src(c), ident[:], is_transpose=True,
                                            start=(c == 0), stop=(c == HC - 1 and not accumulate))
                return last

            pe.wait_ge(const_ready, 3)
            for t in range(TT):
                pe.wait_ge(xn_ready, 6 + t + 1)
                if t >= 2:
                    pe.wait_ge(xT_lo, t - 1)
                transpose4(t % 2, lambda c: y[:, t, c * P:(c + 1) * P]).then_inc(xT_tr, 1)
            pe.wait_ge(part_ready, 2)
            nc.tensor.matmul(sum_ps[:, 0, 0:2], ones[:], abs_part[:, 0:2], start=True, stop=True
                             ).then_inc(total_ready, 1)
            pe.wait_ge(xT_lo, TT)

            def unit(block_no, c, par, kind, first=False):
                index = unit_index(block_no, c, kind)
                bank = unit_bank(block_no, par, kind, first)
                if not (isinstance(index, int) and index < 2):
                    pe.wait_ge(w_hi, index - 1)
                    pe.wait_ge(w_lo, index - 1)
                if block_no == 0:
                    pe.wait_ge(ffn_weight, index + 1)
                else:
                    pe.wait_ge(nf4_weight, c + 1)
                last = transpose4(bank, lambda n: weight[:, par, kind * HID + n * P:kind * HID + (n + 1) * P],
                                  accumulate=block_no == 1)
                if block_no == 1 and kind == DOWN:
                    pe.wait_ge(A_down_ready, c + 1)
                    last = nc.tensor.matmul(tr_ps[:, bank, :], A_down_now[:, par, :], B_downT[:, :],
                                            start=False, stop=True)
                elif block_no == 1:
                    for n in range(HC):
                        last = nc.tensor.matmul(tr_ps[:, bank, n * P:(n + 1) * P], A_gu[:, kind, n * P:(n + 1) * P],
                                                B_guT[:, ds(c * P, P)], start=False, stop=(n == HC - 1))
                last.then_inc(tr_done, 1)

            def project(block_no, c, par, kind, th, first=False):
                n = CHUNKS * block_no + c
                if th == 0:
                    pe.wait_ge(w_lo, unit_index(block_no, c, kind) + 1)
                if par == 1:
                    pe.wait_ge(silu_done if kind == GATE else h_lo, 2 * n + th - 1)
                elif not first:
                    pe.wait_ge(y_done, TT // 2 * n + (3 if kind == GATE else 7) + th - TT)
                ps = (gate_ps if kind == GATE else up_ps)[:, th, :]
                for hc in range(HC):
                    for w_part, x_part in PASSES:
                        last = nc.tensor.matmul(ps, guT[:, par, kind, w_part, hc * P:(hc + 1) * P],
                                                xT[:, x_part, hc, th * HALF:(th + 1) * HALF],
                                                start=(hc == 0 and w_part == x_part == HI),
                                                stop=(hc == HC - 1 and w_part == LO))
                last.then_inc(gate_done if kind == GATE else up_done, 1)

            def down(block_no, i, t, first=False):
                q = PAIRS * block_no + i
                done = TT * q + t
                if t == 0:
                    pe.wait_ge(w_lo, 6 * q + 6)
                    pe.wait_ge(h_lo, 4 * q + 3)
                if t == TT // 2:
                    pe.wait_ge(h_lo, 4 * q + 4)
                if t in (2, 3):
                    pe.wait_ge(silu_done, 4 * q + 1 + t)
                elif t < 6 and not (first and t < 2):
                    pe.wait_ge(y_done, done - 3)
                for par in range(2):
                    for h_part, w_part in PASSES:
                        last = nc.tensor.matmul(down_ps[t], h_split[:, par, h_part, t * P:(t + 1) * P],
                                                downT[:, par, w_part, :],
                                                start=(par == 0 and h_part == w_part == HI),
                                                stop=(par == 1 and h_part == LO))
                last.then_inc(down_done, 1)

            def iteration(block_no, i, last=False):
                a, b = 2 * i, 2 * i + 1
                unit(block_no, a, 0, DOWN)
                project(block_no, a, 0, GATE, 0)
                unit(block_no, b, 1, GATE)
                project(block_no, a, 0, GATE, 1)
                unit(block_no, b, 1, UP)
                project(block_no, a, 0, UP, 0)
                unit(block_no, b, 1, DOWN)
                project(block_no, a, 0, UP, 1)
                for kind in (GATE, UP):
                    for th in range(2):
                        project(block_no, b, 1, kind, th)
                for t in range(TT):
                    down(block_no, i, t)
                    if t == 3 and not last:
                        unit(block_no, a + 2, 0, GATE)
                    if t == 5 and not last:
                        unit(block_no, a + 2, 0, UP)

            unit(0, 0, 0, GATE, first=True)
            unit(0, 0, 0, UP, first=True)
            project(0, 0, 0, GATE, 0, first=True)
            unit(0, 1, 1, GATE, first=True)
            project(0, 0, 0, GATE, 1, first=True)
            unit(0, 1, 1, UP, first=True)
            for th in range(2):
                project(0, 0, 0, UP, th, first=True)
            for kind in (GATE, UP):
                for th in range(2):
                    project(0, 1, 1, kind, th)
            pe.wait_ge(part_ready, 3)
            nc.tensor.matmul(sum_ps[:, 0, 2:3], ones[:], abs_part[:, 2:3], start=True, stop=True
                             ).then_inc(total_ready, 1)
            unit(0, 0, 0, DOWN, first=True)
            unit(0, 1, 1, DOWN, first=True)
            pe.wait_ge(coeff_ready, 2)
            for t in range(TT):
                down(0, 0, t, first=True)
                if t == 3:
                    unit(0, 2, 0, GATE)
                if t == 5:
                    unit(0, 2, 0, UP)
            with pe.Fori(1, 5) as i:
                iteration(0, i)
            iteration(0, 5)
            iteration(0, 6, last=True)

            pe.wait_ge(w_lo, 3 * CHUNKS)
            pe.wait_ge(B_nat_ready, 3)
            for bank, nat in enumerate((B_qkv_nat, B_o_nat)):
                for j in range(4):
                    last = nc.tensor.matmul(tr_ps[0:64, bank, j * P:(j + 1) * P], nat[:, j, :], ident[:],
                                            is_transpose=True, start=(j == 0), stop=(j == 3))
                last.then_inc(B_tr, 1)
            pe.wait_ge(B_T_ready, 2)
            pe.wait_ge(silu_done, 2 * CHUNKS)
            pe.wait_ge(h_lo, 2 * CHUNKS)
            pe.wait_ge(fold_loaded, 16 * 5)
            pe.wait_ge(y_done, TT * PAIRS)
            for m in range(4):
                nc.tensor.matmul(four_ps[m], B_qkvT[0:64, m * P:(m + 1) * P], A_attn[0:64, :], start=True, stop=True
                                 ).then_inc(lora_qkv, 1)
            pe.wait_ge(attn_scaled, 5 * 4 + 1)
            for j in range(4):
                if j >= 2:
                    pe.wait_ge(oT_lo, j - 1)
                transpose4(j % 2, lambda c: w_o[:, j, c * P:(c + 1) * P], accumulate=True)
                for c in range(4):
                    last = nc.tensor.matmul(tr_ps[:, j % 2, c * P:(c + 1) * P], A_attn[0:64, c * P:(c + 1) * P],
                                            B_oT[0:64, j * P:(j + 1) * P], start=False, stop=(c == 3))
                last.then_inc(oT_tr, 1)
            pe.wait_ge(qkv_full, 4)
            pe.wait_ge(qkv_lo, 4)
            pe.wait_ge(oT_lo, 4)
            for hc in range(HC):
                for m in range(4):
                    for a_part, b_part in PASSES:
                        last = nc.tensor.matmul(four_ps[hc], qkv_split[:, m, a_part, hc * P:(hc + 1) * P],
                                                oT_split[:, b_part, m, :],
                                                start=(m == 0 and a_part == b_part == HI),
                                                stop=(m == 3 and a_part == LO))
                last.then_inc(MT_done, 1)
            for n in range(5):
                if n < 4:
                    pe.wait_ge(lora_lo, 2 if 4 * n + 4 <= HALF_CHUNKS else 4)
                else:
                    pe.wait_ge(lora_lo, 6)
                if n >= 2:
                    pe.wait_ge(lora_T, n - 1)
                if n < 4:
                    chunks = range(4 * n, min(4 * n + 4, CHUNKS))
                    for c in chunks:
                        nat = B_gu_nat[c // HALF_CHUNKS][:, c % HALF_CHUNKS, :, :, :].rearrange("p m s r -> p (m s r)")
                        last = nc.tensor.matmul(tr_ps[:, n % 2, (c - 4 * n) * P:(c - 4 * n + 1) * P], nat, ident[:],
                                                is_transpose=True, start=(c == 4 * n), stop=(c == chunks[-1]))
                else:
                    for j in range(4):
                        last = nc.tensor.matmul(tr_ps[0:64, n % 2, j * P:(j + 1) * P],
                                                B_down_nat[:, j, :, :].rearrange("p s r -> p (s r)"), ident[:],
                                                is_transpose=True, start=(j == 0), stop=(j == 3))
                last.then_inc(lora_tr, 1)
            pe.wait_ge(MT_lo, HC)
            pe.wait_ge(y_done, TT * PAIRS)

            def x1_transpose(t):
                pe.wait_ge(x1_ready, t + 1)
                if t < 2:
                    pe.wait_ge(lora_T, 5)
                else:
                    pe.wait_ge(x1_lo, t - 1)
                transpose4(t % 2, lambda c: x1[:, t, c * P:(c + 1) * P]).then_inc(x1_tr, 1)

            for t in range(TT):
                if t >= 2:
                    pe.wait_ge(x1_ready, t - 1)
                for hc in range(HC):
                    for x_part, m_part in PASSES:
                        last = nc.tensor.matmul(sum_ps[:, t % 2, :], xT[:, x_part, hc, t * P:(t + 1) * P],
                                                MT[:, m_part, hc, :],
                                                start=(hc == 0 and x_part == m_part == HI),
                                                stop=(hc == HC - 1 and x_part == LO))
                last.then_inc(x1_sum, 1)
                if t > 0:
                    x1_transpose(t - 1)
            x1_transpose(TT - 1)
            pe.wait_ge(x1_lo, TT)
            pe.wait_ge(A_low, 2)
            unit(1, 0, 0, GATE)
            unit(1, 0, 0, UP)
            with pe.Fori(0, 6) as i:
                iteration(1, i)
            iteration(1, 6, last=True)


_INS = ["L0_attn_x", "L0_attn_codes_attn", "L0_attn_scales_attn", "L0_attn_codes_gu", "L0_attn_scales_gu",
        "L0_attn_codes_down", "L0_attn_scales_down", "L0_attn_lora_A_h", "L0_attn_lora_A_down",
        "L0_attn_lora_B_attn", "L0_attn_lora_B_gu", "L0_attn_lora_B_down",
        "L0_ffn_w1", "L0_ffn_mean_w1", "L0_ffn_w2", "L0_ffn_mean_w2", "L0_ffn_w3", "L0_ffn_mean_w3"]


def kernel(**inputs):
    import numpy as np
    import concourse.bacc as bacc
    from concourse.bass_utils import run_bass_kernel_spmd

    nc = bacc.Bacc("TRN2", target_bir_lowering=False, num_devices=1)
    arrays, args = {}, []
    for name in _INS:
        a = np.ascontiguousarray(inputs[name])
        arrays[name] = a
        args.append(nc.dram_tensor(name, a.shape, mybir.dt.from_np(a.dtype), kind="ExternalInput").ap())
    shape = inputs["L0_attn_x"].shape
    args.append(nc.dram_tensor("out", shape, mybir.dt.float32, kind="ExternalOutput").ap())
    block_kernel(nc, *args)
    result = run_bass_kernel_spmd(nc, [arrays], core_ids=[0])
    return result.results[0]["out"]
```

```python
import concourse.bass as bass
from concourse import mybir
from contextlib import ExitStack

P = 128
TOKENS, HID, INTER, RANK = 1024, 512, 1792, 16
BLOCK = 64
EPS = 1e-5
CHUNKS = INTER // P
HC = HID // P
TT = TOKENS // P
HALF = TOKENS // 2
TRIO = 3 * HID
PAIRS = CHUNKS // 2
FIRST = 4
FIRST_UNITS = 3 * FIRST
SECTIONS = 6
SCAN = INTER - FIRST * P
SCANS = HID // P
SUMS = SCANS + FIRST
SCAN_SLOTS = 4
GROUPS = PAIRS - 1

NF4_STEP = 0.30380719900131226
NF4_OFFSET = 3.2915611267089844
NF4_RAMPS = [
    (0.4722318649291992, -0.5077152252197266, 6.19162654876709),
    (0.16412925720214844, -0.3930339813232422, 1.7030200958251953),
    (0.05514240264892578, -0.24013614654541016, 0.39171409606933594),
    (0.02811431884765625, -0.18800067901611328, 0.09946441650390625),
    (0.036876678466796875, -0.27657508850097656, 0.031052589416503906),
]
RAMPS = len(NF4_RAMPS)
GATE, UP, DOWN = 0, 1, 2
HI, LO = 0, 1
PASSES = [(HI, HI), (HI, LO), (LO, HI)]


def block_kernel(nc, x, codes_attn, scales_attn, codes_gu, scales_gu, codes_down, scales_down,
                 lora_A_h, lora_A_down, lora_B_attn, lora_B_gu, lora_B_down,
                 w1, mean_w1, w2, mean_w2, w3, mean_w3, out):
    f32, f32r, i32 = mybir.dt.float32, mybir.dt.float32r, mybir.dt.int32
    ALU, ACT, AX = mybir.AluOpType, mybir.ActivationFunctionType, mybir.AxisListType
    ds = bass.ds

    x_v = x.rearrange("b s h -> (b s) h").rearrange("(t p) h -> p t h", p=P)
    out_v = out.rearrange("b s h -> (b s) h").rearrange("(t p) h -> p t h", p=P)
    w2_v, mean_w2_v = (m.rearrange("(q p) i -> p q i", p=P) for m in (w2, mean_w2))
    scan_v = [m[FIRST * P:, :].rearrange("(p a) n -> p (a n)", p=P).rearrange("p (k s) -> p k s", s=SCAN)
              for m in (w1, mean_w1, w3, mean_w3)] + [m[:, :, FIRST * P:] for m in (w2_v, mean_w2_v)]
    codes_gu_v = codes_gu.rearrange("m i h -> i m h")
    codes_down_v = codes_down.rearrange("(q p) i -> p q i", p=P)
    codes_attn_v = codes_attn.rearrange("w o h -> o w h")

    ctx = ExitStack()
    with ctx:
        def sb(name, shape, dt=f32):
            return ctx.enter_context(nc.sbuf_tensor(name, shape, dt))

        def sem(name):
            return ctx.enter_context(nc.semaphore(name))

        ident = sb("ident", [P, P])
        ones = sb("ones", [P, P])
        stats = sb("stats", [P, TT, 6])
        moments = sb("moments", [P, TT, 2])
        ln = sb("ln", [P, 5, TT])
        inv_std = sb("inv_std", [P, TT])
        ramp_bias = sb("ramp_bias", [P, RAMPS])
        abs_sums = sb("abs_sums", [P, 3 * SUMS])
        abs_part = sb("abs_part", [P, 3])
        coeff = sb("coeff", [P, 3])
        xT = sb("xT", [P, 2, HC, TOKENS], f32r)
        h_split = sb("h_split", [P, 2, 2, TOKENS], f32r)
        staging = sb("staging", [P, TOKENS])
        downT = sb("downT", [P, 2, 2, HID], f32r)
        guT = sb("guT", [P, 2, 2, 2, HID], f32r)
        raw = sb("raw", [P, 2, TRIO])
        base = sb("base", [P, 2, TRIO])
        weight = sb("weight", [P, 2, TRIO])
        ramp = sb("ramp", [P, 2 * TRIO])
        silu_gate = sb("silu_gate", [P, TOKENS])
        with nc.sbuf_tensor("y", [P, TT, HID], f32) as y:
            pass
        h_more = sb("h_more", [P, TT, HID], f32r)
        scale_raw = sb("scale_raw", [P, CHUNKS, 2, 8])
        scale_down_raw = sb("scale_down_raw", [P, HC, 2 * CHUNKS])
        scale_trio = sb("scale_trio", [P, CHUNKS, 24])
        scale_attn_raw = sb("scale_attn_raw", [P, 4, 4, 8])
        scale_attn = sb("scale_attn", [P, 4, 4, 8])
        A_gu = sb("A_gu", [P, 2, HID], f32r)
        B_downT = sb("B_downT", [P, HID], f32r)
        A_down_now = sb("A_down_now", [P, 2, P], f32r)
        with nc.sbuf_tensor("scan", [P, SCAN_SLOTS, 2, SCAN], f32) as scan:
            pass
        with nc.sbuf_tensor("attn_codes", [P, 4, HID], f32) as attn_codes, \
                nc.sbuf_tensor("attn_sum", [P, 4, HID], f32) as attn_sum, \
                nc.sbuf_tensor("w_qkv", [P, 4, HID], f32) as w_qkv, \
                nc.sbuf_tensor("w_o", [P, 4, HID], f32) as w_o, \
                nc.sbuf_tensor("x1", [P, TT, HID], f32) as x1:
            pass
        with nc.sbuf_tensor("downT_more_space", [P, 4, HID], f32), \
                nc.sbuf_tensor("downT_more", [P, 2, 2, HID], f32r) as downT_more:
            pass
        MT = sb("MT", [P, 2, HC, HID], f32r)
        A_down = sb("A_down", [P, INTER], f32r)
        B_guT = sb("B_guT", [P, INTER], f32r)
        sb("x1_space", [P, 32 * 256 - 4 * HID * 2 - 2 * INTER + TT * HID])
        A_attn = x1[:, 0, :]
        B_qkvT = x1[:, 1, :]
        B_oT = x1[:, 2, :]
        B_attn_raw = x1[:, 3, 0:256].rearrange("p (j w r) -> p j w r", j=4, w=4)
        B_qkv_nat = x1[:, 4, 0:256].rearrange("p (j r) -> p j r", j=4)
        B_o_nat = x1[:, 4, 256:512].rearrange("p (j r) -> p j r", j=4)
        qkv_split = h_split[:, :, :, :].rearrange("p a b t -> p (a b t)").rearrange(
            "p (m s h) -> p m s h", m=4, s=2)
        oT_split = guT[:, :, :, :, :].rearrange("p a b c h -> p (a b c h)").rearrange(
            "p (s m h) -> p s m h", s=2, m=4)
        B_down_nat = ramp[:, 0:256].rearrange("p (j s r) -> p j s r", j=4, s=4)
        B_down_raw = ramp[:, 256:320].rearrange("p (j r) -> p j r", j=4)
        B_gu_raw = ramp[:, 320:768].rearrange("p (c m r) -> p c m r", c=CHUNKS, m=2)
        A_gu_raw = ramp[:, 768:1280]
        A_down_raw = ramp[:, 1280:1280 + INTER]
        HALF_CHUNKS = CHUNKS // 2
        B_gu_nat = [t[:, 0:HALF_CHUNKS * P].rearrange("p (c m s r) -> p c m s r", c=HALF_CHUNKS, m=2, s=4)
                    for t in (silu_gate, staging)]

        raw_s, base_s, weight_s = (t[:, :, :].rearrange("p a (k h) -> p (a k) h", h=HID) for t in (raw, base, weight))
        silu_first = [silu_gate[:, :], staging[:, :], ramp[:, 0:TOKENS], ramp[:, TOKENS:2 * TOKENS]]
        abs_out = ramp[:, 2 * TOKENS:2 * TOKENS + HID]

        def first_w(n):
            if n < 2 * FIRST:
                return guT[:, n % FIRST // 2, n % 2]
            c = n - 2 * FIRST
            return downT[:, c] if c < 2 else downT_more[:, c - 2]

        def first_h(c, part, t0, t1):
            if c < 2:
                return h_split[:, c, part, t0 * P:t1 * P].rearrange("p (t n) -> p t n", n=P)
            k = 2 * (c - 2) + part
            return h_more[:, t0:t1, k * P:(k + 1) * P]

        def pb(name):
            return ctx.enter_context(nc.psum_tensor(name, [P, 2, HALF], f32))

        gate_ps, up_ps, tr_ps, sum_ps = pb("gate_ps"), pb("up_ps"), pb("tr_ps"), pb("sum_ps")
        down_ps = [sum_ps[:, 0, :], sum_ps[:, 1, :], gate_ps[:, 0, :], gate_ps[:, 1, :],
                   sum_ps[:, 0, :], sum_ps[:, 1, :], up_ps[:, 0, :], up_ps[:, 1, :]]
        four_ps = [gate_ps[:, 0, :], gate_ps[:, 1, :], up_ps[:, 0, :], up_ps[:, 1, :]]

        x_loaded = [sem("x_loaded0"), sem("x_loaded1")]
        const_ready = sem("const_ready")
        ln_step = sem("ln_step")
        root_done = sem("root_done")
        xn_ready = sem("xn_ready")
        xT_tr = sem("xT_tr")
        xT_hi = sem("xT_hi")
        xT_lo = sem("xT_lo")
        scan_loaded = [sem(f"scan_loaded{n}") for n in range(SCAN_SLOTS)]
        scan_diff = sem("scan_diff")
        scan_abs = sem("scan_abs")
        first_loaded = [sem(f"first_loaded{n}") for n in range(SECTIONS)]
        first_abs = sem("first_abs")
        part_ready = sem("part_ready")
        total_ready = sem("total_ready")
        coeff_ready = sem("coeff_ready")
        scales_loaded = sem("scales_loaded")
        scales_ready = sem("scales_ready")
        chunk_loaded = [sem("chunk_loaded0"), sem("chunk_loaded1")]
        diff_ready = sem("diff_ready")
        sign_ready = sem("sign_ready")
        ffn_weight = sem("ffn_weight")
        nf4_start = sem("nf4_start")
        nf4_ramp = sem("nf4_ramp")
        nf4_sum = sem("nf4_sum")
        nf4_weight = sem("nf4_weight")
        A_down_ready = sem("A_down_ready")
        tr_done = sem("tr_done")
        w_hi = sem("w_hi")
        w_lo = sem("w_lo")
        gate_done = sem("gate_done")
        up_done = sem("up_done")
        silu_done = sem("silu_done")
        h_done = sem("h_done")
        h_hi = sem("h_hi")
        h_lo = sem("h_lo")
        down_done = sem("down_done")
        y_done = sem("y_done")
        attn_loaded = sem("attn_loaded")
        gpsimd_passed = sem("gpsimd_passed")
        attn_start = sem("attn_start")
        attn_ramp = sem("attn_ramp")
        attn_acc = sem("attn_acc")
        attn_scaled = sem("attn_scaled")
        fold_loaded = sem("fold_loaded")
        B_nat_ready = sem("B_nat_ready")
        B_tr = sem("B_tr")
        B_T_ready = sem("B_T_ready")
        lora_qkv = sem("lora_qkv")
        qkv_full = sem("qkv_full")
        qkv_hi = sem("qkv_hi")
        qkv_lo = sem("qkv_lo")
        oT_tr = sem("oT_tr")
        oT_hi = sem("oT_hi")
        oT_lo = sem("oT_lo")
        MT_done = sem("MT_done")
        MT_hi = sem("MT_hi")
        MT_lo = sem("MT_lo")
        x_again = [sem("x_again0"), sem("x_again1")]
        xn_again = sem("xn_again")
        x1_sum = sem("x1_sum")
        x1_ready = sem("x1_ready")
        x1_tr = sem("x1_tr")
        x1_hi = sem("x1_hi")
        x1_lo = sem("x1_lo")
        lora_loaded = sem("lora_loaded")
        lora_zero = sem("lora_zero")
        lora_hi = sem("lora_hi")
        lora_lo = sem("lora_lo")
        A_low = sem("A_low")
        lora_tr = sem("lora_tr")
        lora_T = sem("lora_T")
        ffn_silu = sem("ffn_silu")
        x_last = sem("x_last")
        s_full = sem("s_full")
        gated = sem("gated")
        out_ready = sem("out_ready")
        out_stored = sem("out_stored")

        block = ctx.enter_context(nc.Block())

        def unit_index(block_no, c, kind):
            return 3 * (CHUNKS * block_no + c) + kind

        @block.sync
        def _(sp):
            for n in range(2):
                sp.dma_start(y[:, 4 * n:4 * n + 4, :], x_v[:, 4 * n:4 * n + 4, :]).then_inc(x_loaded[n], 16)

            def load_scan(k):
                m, part = k // SCANS, k % SCANS
                if k >= SCAN_SLOTS:
                    sp.wait_ge(scan_abs, k - SCAN_SLOTS + 1)
                for which in range(2):
                    sp.dma_start(scan[:, k % SCAN_SLOTS, which, :], scan_v[2 * m + which][:, part, :]
                                 ).then_inc(scan_loaded[k % SCAN_SLOTS], 16)

            def load_first(n):
                kind, c = n // FIRST, n % FIRST
                if n >= SECTIONS:
                    sp.wait_ge(ffn_weight, n - SECTIONS + 1)
                for dst, src in ((raw_s, (w1, w3, w2_v)[kind]), (base_s, (mean_w1, mean_w3, mean_w2_v)[kind])):
                    if kind == DOWN:
                        sp.dma_start(dst[:, n % SECTIONS, :].rearrange("p (q i) -> p q i", q=HC),
                                     src[:, :, c * P:(c + 1) * P]).then_inc(first_loaded[n % SECTIONS], 16)
                    else:
                        sp.dma_start(dst[:, n % SECTIONS, :], src[c * P:(c + 1) * P, :]
                                     ).then_inc(first_loaded[n % SECTIONS], 16)

            def load_ffn(c, par):
                sp.wait_ge(ffn_weight, 3 * c - 3)
                for dst, gate, up, down in ((raw, w1, w3, w2_v), (base, mean_w1, mean_w3, mean_w2_v)):
                    sp.dma_start(dst[:, par, 0:HID], gate[ds(c * P, P), :]).then_inc(chunk_loaded[par], 16)
                    sp.dma_start(dst[:, par, HID:2 * HID], up[ds(c * P, P), :]).then_inc(chunk_loaded[par], 16)
                    sp.dma_start(dst[:, par, 2 * HID:].rearrange("p (q i) -> p q i", q=HC),
                                 down[:, :, ds(c * P, P)]).then_inc(chunk_loaded[par], 16)

            def load_nf4(k, par):
                if isinstance(k, int) and k < 2:
                    sp.wait_ge(ffn_weight, 3 * (CHUNKS - 2 + k) + 3)
                else:
                    sp.wait_ge(nf4_ramp, RAMPS * (k - 1))
                sp.dma_start(raw[:, par, 0:2 * HID].bitcast(i32).rearrange("p (m h) -> p m h", m=2),
                             codes_gu_v[ds(k * P, P), :, :]).then_inc(chunk_loaded[par], 16)
                sp.dma_start(raw[:, par, 2 * HID:].bitcast(i32).rearrange("p (q i) -> p q i", q=HC),
                             codes_down_v[:, :, ds(k * P, P)]).then_inc(chunk_loaded[par], 16)

            def load_attn(m):
                if not isinstance(m, int):
                    sp.wait_ge(attn_ramp, 2 * RAMPS * m)
                sp.dma_start(attn_codes[:, :, :].bitcast(i32), codes_attn_v[ds(m * P, P), :, :]
                             ).then_inc(attn_loaded, 16)

            for m in range(3):
                for half in range(2):
                    for k in range(2):
                        load_scan(SCANS * m + 2 * half + k)
                    for k in range(2):
                        load_first(FIRST * m + 2 * half + k)
            for m in range(2):
                sp.dma_start(scale_raw[:, :, m, :], scales_gu[m].rearrange("(c p) b -> p c b", p=P)
                             ).then_inc(scales_loaded, 16)
            sp.dma_start(scale_down_raw[:, :, :], scales_down.rearrange("(q p) b -> p q b", p=P)
                         ).then_inc(scales_loaded, 16)
            for m in range(4):
                sp.dma_start(scale_attn_raw[:, m, :, :],
                             scales_attn[:, m * P:(m + 1) * P, :].rearrange("w p b -> p w b")
                             ).then_inc(scales_loaded, 16)
            load_ffn(4, 0)
            load_ffn(5, 1)
            sp.wait_ge(scan_abs, 3 * SCANS)
            load_attn(0)
            sp.dma_start(A_attn[0:4 * RANK, :], lora_A_h[0:4].rearrange("w r h -> (w r) h")
                         ).then_inc(fold_loaded, 16)
            for j in range(4):
                sp.dma_start(B_attn_raw[:, j, :, :],
                             lora_B_attn[:, j * P:(j + 1) * P, :].rearrange("w p r -> p w r")
                             ).then_inc(fold_loaded, 16)
            load_ffn(6, 0)
            load_ffn(7, 1)
            with sp.Fori(2, 5) as i:
                load_ffn(2 * i + 4, 0)
                load_ffn(2 * i + 5, 1)
                load_attn(i - 1)
            load_nf4(0, 0)
            load_nf4(1, 1)
            sp.wait_ge(nf4_sum, 2 * RAMPS)
            for m in range(2):
                for copy in range(4):
                    sp.dma_start(A_gu_raw[64 * m + 16 * copy:64 * m + 16 * copy + 16, :], lora_A_h[4 + m]
                                 ).then_inc(lora_loaded, 16)
                sp.dma_start(B_gu_raw[:, :, m, :], lora_B_gu[m].rearrange("(c p) r -> p c r", p=P)
                             ).then_inc(lora_loaded, 16)
            for copy in range(4):
                sp.dma_start(A_down_raw[16 * copy:16 * copy + 16, :], lora_A_down).then_inc(lora_loaded, 16)
            sp.dma_start(B_down_raw, lora_B_down.rearrange("(j p) r -> p j r", p=P)).then_inc(lora_loaded, 16)
            load_nf4(2, 0)
            load_nf4(3, 1)
            sp.wait_ge(oT_tr, 4)
            sp.wait_ge(lora_qkv, 4)
            for n in range(2):
                sp.dma_start(x1[:, 4 * n:4 * n + 4, :], x_v[:, 4 * n:4 * n + 4, :]).then_inc(x_again[n], 16)
            with sp.Fori(1, 6) as i:
                load_nf4(2 * i + 2, 0)
                load_nf4(2 * i + 3, 1)
            sp.wait_ge(nf4_sum, RAMPS * CHUNKS)
            sp.wait_ge(nf4_weight, CHUNKS)
            for n in range(2):
                for which, dst in enumerate((raw, base)):
                    t = 4 * n + 2 * which
                    sp.dma_start(dst[:, n, 0:2 * HID].rearrange("p (t h) -> p t h", t=2), x_v[:, t:t + 2, :]
                                 ).then_inc(x_last, 16)
            for t in range(TT):
                sp.wait_ge(out_ready, t + 1)
                sp.dma_start(out_v[:, t, :], y[:, t, :]).then_inc(out_stored, 16)
            sp.wait_ge(out_stored, 16 * TT)

        def last_x(t):
            buf = (raw, base)[(t % 4) // 2]
            return buf[:, t // 4, (t % 2) * HID:(t % 2 + 1) * HID]

        @block.gpsimd
        def _(pool):
            nc.gpsimd.memset(ident[:], 0.0).then_inc(const_ready, 1)
            nc.gpsimd.memset(ones[:], 1.0).then_inc(const_ready, 1)
            pool.wait_ge(const_ready, 2)
            nc.gpsimd.affine_select(out=ident[:], in_=ident[:], compare_op=ALU.not_equal, fill=1.0, base=0,
                                    pattern=[[-1, P]], channel_multiplier=1).then_inc(const_ready, 1)
            nc.gpsimd.memset(A_gu[:, :, :].bitcast(f32), 0.0).then_inc(lora_zero, 1)
            nc.gpsimd.memset(B_downT[:, :].bitcast(f32), 0.0).then_inc(lora_zero, 1)
            def counted(semaphore, count):
                pool.wait_ge(semaphore, count)
                pool.sem_inc(gpsimd_passed, 1)

            def ffn_diff_at(i, par):
                counted(chunk_loaded[par], 96 * i - 96)
                nc.gpsimd.tensor_tensor(raw[:, par, :], raw[:, par, :], base[:, par, :], ALU.subtract
                                        ).then_inc(diff_ready, 1)

            def nf4_scale(k, par):
                counted(nf4_sum, RAMPS * k + RAMPS)
                counted(tr_done, 3 * (CHUNKS + k) - 3)
                nc.gpsimd.tensor_tensor(
                    weight[:, par, :].rearrange("p (b n) -> p b n", n=BLOCK),
                    base[:, par, :].rearrange("p (b n) -> p b n", n=BLOCK),
                    scale_trio[:, ds(k, 1), :].rearrange("p a b -> p (a b)").unsqueeze(2).to_broadcast([P, 24, BLOCK]),
                    ALU.mult).then_inc(nf4_weight, 1)

            def A_down_chunk(k, par):
                counted(tr_done, 3 * (CHUNKS + k) - 3)
                nc.gpsimd.tensor_copy(A_down_now[:, par, :], A_down[:, ds(k * P, P)].bitcast(f32)
                                      ).then_inc(A_down_ready, 1)

            def attn_begin(m):
                counted(attn_loaded, 16 * m + 16)
                counted(attn_scaled, 5 * m + 1)
                nc.gpsimd.tensor_scalar(attn_sum[:, :, :], attn_codes[:, :, :].bitcast(i32), -1.0, NF4_OFFSET,
                                        ALU.mult, ALU.add).then_inc(attn_start, 1)

            def attn_scale(dst, m, w0, w1_):
                n = (w1_ - w0) * HID // BLOCK
                nc.gpsimd.tensor_tensor(
                    dst.rearrange("p w (b n) -> p (w b) n", n=BLOCK),
                    attn_sum[:, w0:w1_, :].rearrange("p w (b n) -> p (w b) n", n=BLOCK),
                    scale_attn[:, ds(m, 1), w0:w1_, :].rearrange("p a w b -> p (a w b)").unsqueeze(2)
                    .to_broadcast([P, n, BLOCK]), ALU.mult).then_inc(attn_scaled, 1)

            def attn_finish(m, half):
                counted(attn_acc, 2 + 2 * RAMPS * m + RAMPS * (half + 1))
                if half == 0:
                    attn_scale(attn_sum[:, 0:2, :], m, 0, 2)
                    counted(attn_scaled, 5 * m + 2)
                    nc.gpsimd.tensor_tensor(w_qkv[:, ds(m, 1), :], attn_sum[:, 0:1, :], attn_sum[:, 1:2, :],
                                            ALU.add).then_inc(attn_scaled, 1)
                else:
                    attn_scale(attn_sum[:, 2:3, :], m, 2, 3)
                    attn_scale(w_o[:, ds(m, 1), :], m, 3, 4)
                    counted(attn_scaled, 5 * m + 5)
                    nc.gpsimd.tensor_tensor(w_qkv[:, ds(m, 1), :], w_qkv[:, ds(m, 1), :], attn_sum[:, 2:3, :],
                                            ALU.add).then_inc(attn_scaled, 1)

            def make_nf4(k):
                for par in range(2):
                    nf4_scale(k + par, par)
                    A_down_chunk(k + par, par)

            for n in range(FIRST_UNITS):
                pool.wait_ge(first_loaded[n % SECTIONS], 32 * (n // SECTIONS) + 32)
                nc.gpsimd.tensor_tensor(raw_s[:, n % SECTIONS, :], raw_s[:, n % SECTIONS, :],
                                        base_s[:, n % SECTIONS, :], ALU.subtract).then_inc(diff_ready, 1)
            ffn_diff_at(2, 0)
            ffn_diff_at(2, 1)
            pool.wait_ge(scales_loaded, 16 * (2 + 4 + 1))
            nc.gpsimd.tensor_scalar(scale_trio[:, :, 0:16], scale_raw[:, :, :, :].rearrange("p c m b -> p c (m b)"),
                                    -NF4_STEP, 0.0, ALU.mult, ALU.add).then_inc(scales_ready, 1)
            for q in range(HC):
                nc.gpsimd.tensor_scalar(scale_trio[:, :, 16 + 2 * q:18 + 2 * q],
                                        scale_down_raw[:, q, :].rearrange("p (c b) -> p c b", b=2),
                                        -NF4_STEP, 0.0, ALU.mult, ALU.add).then_inc(scales_ready, 1)
            nc.gpsimd.tensor_scalar(scale_attn[:, :, 0:3, :], scale_attn_raw[:, :, 0:3, :],
                                    -NF4_STEP / 3.0, 0.0, ALU.mult, ALU.add).then_inc(scales_ready, 1)
            nc.gpsimd.tensor_scalar(scale_attn[:, :, 3, :], scale_attn_raw[:, :, 3, :],
                                    -NF4_STEP, 0.0, ALU.mult, ALU.add).then_inc(scales_ready, 1)
            pool.wait_ge(scales_ready, 3 + HC)
            nc.gpsimd.memset(ln[:, 4, 0:1], 0.0).then_inc(attn_scaled, 1)

            ffn_diff_at(3, 0)
            ffn_diff_at(3, 1)
            pool.wait_ge(y_done, TT)
            with pool.Fori(2, 5) as i:
                attn_begin(i - 2)
                ffn_diff_at(i + 2, 0)
                attn_finish(i - 2, 0)
                ffn_diff_at(i + 2, 1)
                attn_finish(i - 2, 1)
            attn_begin(3)
            attn_finish(3, 0)
            attn_finish(3, 1)
            pool.wait_ge(scan_abs, 3 * SCANS)
            nc.gpsimd.memset(x1[:, 4, :], 0.0).then_inc(B_nat_ready, 1)
            pool.wait_ge(fold_loaded, 16 * 5)
            pool.wait_ge(B_nat_ready, 1)
            nc.gpsimd.tensor_copy(B_qkv_nat[:, :, 0:48].rearrange("p j (w r) -> p j w r", w=3),
                                  B_attn_raw[:, :, 0:3, :]).then_inc(B_nat_ready, 1)
            nc.gpsimd.tensor_copy(B_o_nat[:, :, 48:64], B_attn_raw[:, :, 3, :]).then_inc(B_nat_ready, 1)
            for par in range(2):
                nf4_scale(par, par)

            for m in range(4):
                pool.wait_ge(qkv_hi, m + 1)
                nc.gpsimd.tensor_tensor(qkv_split[:, m, LO, :], w_qkv[:, m, :],
                                        qkv_split[:, m, HI, :].bitcast(f32), ALU.subtract).then_inc(qkv_lo, 1)
            pool.wait_ge(lora_loaded, 16 * 15)
            for n in range(2):
                for s in (1, 3):
                    pool.wait_ge(lora_hi, 2 + 2 * n + 2)
                    nc.gpsimd.tensor_tensor(B_gu_nat[n][:, :, :, s, :],
                                            B_gu_raw[:, n * HALF_CHUNKS:(n + 1) * HALF_CHUNKS, :, :],
                                            B_gu_nat[n][:, :, :, 0, :], ALU.subtract).then_inc(lora_lo, 1)
            for s in (1, 3):
                pool.wait_ge(lora_hi, 8)
                nc.gpsimd.tensor_tensor(B_down_nat[:, :, s, :], B_down_raw, B_down_nat[:, :, 0, :],
                                        ALU.subtract).then_inc(lora_lo, 1)
            pool.wait_ge(A_low, 3)
            pool.wait_ge(lora_zero, 3)
            A_down_chunk(0, 0)
            A_down_chunk(1, 1)
            with pool.Fori(0, PAIRS - 1) as i:
                make_nf4(2 * i + 2)
            for t in range(TT):
                pool.wait_ge(x_last, 16 * 4)
                pool.wait_ge(gated, t + 1)
                nc.gpsimd.tensor_tensor(y[:, t, :], y[:, t, :], last_x(t), ALU.add).then_inc(out_ready, 1)

        @block.scalar
        def _(act):
            act.wait_ge(ln_step, TT + 1)
            nc.scalar.activation(ln[:, 1, :], ln[:, 0, :], ACT.Sqrt).then_inc(root_done, 1)

            def x_high(t):
                act.wait_ge(xT_tr, t + 1)
                nc.scalar.activation(xT[:, HI, :, t * P:(t + 1) * P],
                                     tr_ps[:, t % 2, :].rearrange("p (c t) -> p c t", c=HC), ACT.Copy
                                     ).then_inc(xT_hi, 1)

            def scan_sum(k):
                m, part = k // SCANS, k % SCANS
                act.wait_ge(scan_diff, k + 1)
                nc.scalar.activation(scan[:, k % SCAN_SLOTS, 0, :], scan[:, k % SCAN_SLOTS, 0, :], ACT.Abs,
                                     accum_out=abs_sums[:, SUMS * m + part:SUMS * m + part + 1]).then_inc(scan_abs, 1)

            def first_sum(n):
                column = SUMS * (n // FIRST) + SCANS + n % FIRST
                act.wait_ge(diff_ready, n + 1)
                if n > 0:
                    act.wait_ge(first_abs, n)
                nc.scalar.activation(abs_out, raw_s[:, n % SECTIONS, :], ACT.Abs,
                                     accum_out=abs_sums[:, column:column + 1]).then_inc(first_abs, 1)

            def first_sign(n):
                nc.scalar.activation(raw_s[:, n % SECTIONS, :], raw_s[:, n % SECTIONS, :], ACT.Sign
                                     ).then_inc(sign_ready, 1)

            def first_high(n):
                act.wait_ge(tr_done, n + 1)
                nc.scalar.activation(first_w(n)[:, HI, :], tr_ps[:, n % 2, :], ACT.Copy).then_inc(w_hi, 1)

            def first_silu(c, th):
                act.wait_ge(gate_done, 2 * c + th + 1)
                nc.scalar.activation(silu_first[c][:, th * HALF:(th + 1) * HALF], gate_ps[:, th, :], ACT.Silu
                                     ).then_inc(silu_done, 1)

            def first_h_high(c, th):
                act.wait_ge(h_done, 2 * c + th + 1)
                nc.scalar.activation(first_h(c, HI, 4 * th, 4 * th + 4),
                                     up_ps[:, th, :].rearrange("p (t n) -> p t n", n=P), ACT.Copy).then_inc(h_hi, 1)

            def ffn_sign(c, par):
                act.wait_ge(diff_ready, FIRST_UNITS + c - FIRST + 1)
                nc.scalar.activation(raw[:, par, :], raw[:, par, :], ACT.Sign).then_inc(sign_ready, 1)

            def w_high(block_no, c, par, kind):
                act.wait_ge(tr_done, unit_index(block_no, c, kind) + 1)
                dst = downT[:, par, HI, :] if kind == DOWN else guT[:, par, kind, HI, :]
                nc.scalar.activation(dst, tr_ps[:, (3 * par + kind) % 2, :], ACT.Copy
                                     ).then_inc(w_hi, 1)

            def silu(n, th):
                act.wait_ge(gate_done, 2 * n + th + 1)
                act.wait_ge(h_done, 2 * n + th - 1)
                nc.scalar.activation(silu_gate[:, th * HALF:(th + 1) * HALF], gate_ps[:, th, :], ACT.Silu
                                     ).then_inc(silu_done, 1)

            def h_high(n, par, th):
                act.wait_ge(h_done, 2 * n + th + 1)
                sl = slice(th * HALF, (th + 1) * HALF)
                nc.scalar.activation(h_split[:, par, HI, sl], up_ps[:, th, :], ACT.Copy).then_inc(h_hi, 1)

            def nf4_begin(k, par):
                act.wait_ge(chunk_loaded[par], 96 * (PAIRS - 2) + 16 * (k - par) + 32)
                if isinstance(k, int) and k < 2:
                    act.wait_ge(ffn_weight, 3 * (CHUNKS - 2 + k) + 3)
                else:
                    act.wait_ge(nf4_weight, k - 1)
                nc.scalar.activation(base[:, par, :], raw[:, par, :].bitcast(i32), ACT.Copy, bias=NF4_OFFSET,
                                     scale=-1.0).then_inc(nf4_start, 1)

            def nf4_ramp_step(k, step):
                par, j = step // RAMPS, step % RAMPS
                slope, start, _ = NF4_RAMPS[j]
                r = RAMPS * k + step
                if j == 0:
                    nf4_begin(k + par, par)
                if not (isinstance(k, int) and r < 2):
                    act.wait_ge(nf4_sum, r - 1)
                nc.scalar.activation(ramp[:, (step % 2) * TRIO:(step % 2 + 1) * TRIO],
                                     raw[:, par, :].bitcast(i32), ACT.Relu, bias=ramp_bias[:, j:j + 1], scale=slope
                                     ).then_inc(nf4_ramp, 1)

            def attn_ramp_step(m, step):
                half, j = step // RAMPS, step % RAMPS
                slope, start, _ = NF4_RAMPS[j]
                if step == 0:
                    act.wait_ge(attn_start, m + 1)
                act.wait_ge(attn_acc, 2 * RAMPS * m + step + 1)
                nc.scalar.activation(ramp[:, (step % 2) * TRIO:(step % 2) * TRIO + 2 * HID],
                                     attn_codes[:, 2 * half:2 * half + 2, :].bitcast(i32).rearrange("p w h -> p (w h)"),
                                     ACT.Relu, bias=ramp_bias[:, j:j + 1], scale=slope).then_inc(attn_ramp, 1)

            def make(step, i, make_ffn, attn, make_nf4):
                if make_ffn and step == 6:
                    ffn_sign(2 * i + 4, 0)
                if attn is not None:
                    attn_ramp_step(attn, step)
                if make_nf4 is not None:
                    nf4_ramp_step(2 * make_nf4, step)

            def iteration(block_no, i, make_ffn=False, attn=None, make_nf4=None, last=False):
                n, a, b = CHUNKS * block_no + 2 * i, 2 * i, 2 * i + 1
                bg = (i, make_ffn, attn, make_nf4)
                w_high(block_no, a, 0, DOWN)
                make(0, *bg)
                make(1, *bg)
                silu(n, 0)
                w_high(block_no, b, 1, GATE)
                make(2, *bg)
                silu(n, 1)
                w_high(block_no, b, 1, UP)
                make(3, *bg)
                make(4, *bg)
                h_high(n, 0, 0)
                w_high(block_no, b, 1, DOWN)
                h_high(n, 0, 1)
                make(5, *bg)
                silu(n + 1, 0)
                make(6, *bg)
                silu(n + 1, 1)
                make(7, *bg)
                h_high(n + 1, 1, 0)
                make(8, *bg)
                h_high(n + 1, 1, 1)
                make(9, *bg)
                if not last:
                    w_high(block_no, a + 2, 0, GATE)
                if make_ffn:
                    ffn_sign(b + 4, 1)
                if not last:
                    w_high(block_no, a + 2, 0, UP)

            x_high(0)
            x_high(1)
            x_high(2)
            x_high(3)
            scan_sum(0)
            x_high(4)
            x_high(5)
            scan_sum(1)
            first_sum(0)
            x_high(6)
            x_high(7)
            first_sum(1)
            first_sign(0)
            first_sign(1)
            scan_sum(2)
            scan_sum(3)
            first_sum(2)
            first_sum(3)
            first_sign(2)
            first_sign(3)
            first_high(0)
            first_high(1)
            scan_sum(4)
            scan_sum(5)
            first_silu(0, 0)
            first_sum(4)
            first_silu(0, 1)
            first_high(2)
            first_sum(5)
            first_sign(4)
            first_sign(5)
            scan_sum(6)
            first_silu(1, 0)
            first_silu(1, 1)
            first_high(3)
            scan_sum(7)
            first_silu(2, 0)
            first_sum(6)
            first_sum(7)
            first_silu(2, 1)
            first_sign(6)
            first_sign(7)
            scan_sum(8)
            first_silu(3, 0)
            first_high(4)
            first_silu(3, 1)
            first_high(5)
            scan_sum(9)
            first_sum(8)
            first_h_high(0, 0)
            first_sum(9)
            scan_sum(10)
            first_h_high(0, 1)
            first_high(6)
            scan_sum(11)
            first_h_high(1, 0)
            first_h_high(1, 1)
            first_sum(10)
            first_sum(11)
            first_sign(8)
            first_high(7)
            first_sign(9)
            first_h_high(2, 0)
            first_sign(10)
            first_h_high(2, 1)
            first_sign(11)
            first_high(8)
            first_high(9)
            first_h_high(3, 0)
            first_high(10)
            first_high(11)
            first_h_high(3, 1)
            ffn_sign(4, 0)
            ffn_sign(5, 1)
            w_high(0, 4, 0, GATE)
            ffn_sign(6, 0)
            w_high(0, 4, 0, UP)
            ffn_sign(7, 1)
            with act.Fori(2, 5) as i:
                iteration(0, i, make_ffn=True, attn=i - 2)
            iteration(0, 5, attn=3)
            act.wait_ge(attn_acc, 2 + 8 * RAMPS)
            iteration(0, 6, make_nf4=0, last=True)

            act.wait_ge(B_tr, 2)
            nc.scalar.activation(B_qkvT[0:64, :], tr_ps[0:64, 0, :], ACT.Copy, scale=1.0 / 3.0).then_inc(B_T_ready, 1)
            nc.scalar.activation(B_oT[0:64, :], tr_ps[0:64, 1, :], ACT.Copy).then_inc(B_T_ready, 1)
            for m in range(4):
                act.wait_ge(qkv_full, m + 1)
                nc.scalar.activation(qkv_split[:, m, HI, :], w_qkv[:, m, :], ACT.Copy).then_inc(qkv_hi, 1)
                act.wait_ge(oT_tr, m + 1)
                nc.scalar.activation(oT_split[:, HI, :, m * P:(m + 1) * P],
                                     tr_ps[:, m % 2, :].rearrange("p (c o) -> p c o", c=4), ACT.Copy
                                     ).then_inc(oT_hi, 1)
            act.wait_ge(lora_loaded, 16 * 15)
            act.wait_ge(lora_zero, 2)
            for m in range(2):
                rows = slice(64 * m, 64 * m + 64)
                nc.scalar.activation(A_gu[rows, m, :], A_gu_raw[rows, :], ACT.Copy).then_inc(lora_hi, 1)
            act.wait_ge(h_done, 4 * PAIRS)
            for n in range(2):
                for s in (0, 2):
                    nc.scalar.activation(B_gu_nat[n][:, :, :, s, :].bitcast(f32r),
                                         B_gu_raw[:, n * HALF_CHUNKS:(n + 1) * HALF_CHUNKS, :, :], ACT.Copy
                                         ).then_inc(lora_hi, 1)
            for s in (0, 2):
                nc.scalar.activation(B_down_nat[:, :, s, :].bitcast(f32r), B_down_raw, ACT.Copy).then_inc(lora_hi, 1)
            act.wait_ge(qkv_hi, 4)
            act.wait_ge(qkv_lo, 4)
            nc.scalar.activation(A_down[0:64, :], A_down_raw[0:64, :], ACT.Copy).then_inc(lora_hi, 1)
            for c in range(HC):
                act.wait_ge(MT_done, c + 1)
                nc.scalar.activation(MT[:, HI, c, :], four_ps[c], ACT.Copy).then_inc(MT_hi, 1)
            for n in range(5):
                act.wait_ge(lora_tr, n + 1)
                if n < 4:
                    w = min(4, CHUNKS - 4 * n) * P
                    nc.scalar.activation(B_guT[:, 4 * n * P:4 * n * P + w], tr_ps[:, n % 2, 0:w], ACT.Copy
                                         ).then_inc(lora_T, 1)
                else:
                    nc.scalar.activation(B_downT[0:64, :], tr_ps[0:64, n % 2, :], ACT.Copy).then_inc(lora_T, 1)
            for t in range(TT):
                act.wait_ge(x1_tr, t + 1)
                nc.scalar.activation(xT[:, HI, :, t * P:(t + 1) * P],
                                     tr_ps[:, t % 2, :].rearrange("p (c t) -> p c t", c=HC), ACT.Copy
                                     ).then_inc(x1_hi, 1)
            for kind in (GATE, UP):
                w_high(1, 0, 0, kind)
            act.wait_ge(y_done, TT * GROUPS)
            nc.scalar.activation(y[:, :, :].rearrange("p t h -> p (t h)"), y[:, :, :].rearrange("p t h -> p (t h)"),
                                 ACT.Silu).then_inc(ffn_silu, 1)
            with act.Fori(0, 6) as i:
                iteration(1, i, make_nf4=i + 1)
            iteration(1, 6, last=True)

        @block.vector
        def _(dve):
            for j, (_, start, _) in enumerate(NF4_RAMPS):
                nc.vector.memset(ramp_bias[:, j:j + 1], start)
            for t in range(TT):
                dve.wait_ge(x_loaded[t // 4], 16)
                nc.vector.bn_stats(stats[:, t, :], y[:, t, :]).then_inc(ln_step, 1)
            dve.wait_ge(ln_step, TT)
            for t in range(TT):
                last = nc.vector.bn_aggr(moments[:, t, :], stats[:, t, :])
            last.then_inc(xn_ready, 1)
            dve.wait_ge(xn_ready, 1)
            nc.vector.tensor_scalar(ln[:, 0, :], moments[:, :, 1], EPS, None, ALU.add).then_inc(ln_step, 1)
            dve.wait_ge(root_done, 1)
            nc.vector.reciprocal(ln[:, 2, :], ln[:, 1, :]).then_inc(xn_ready, 1)
            dve.wait_ge(xn_ready, 2)
            nc.vector.tensor_tensor(ln[:, 2, :], ln[:, 2, :], ln[:, 0, :], ALU.mult).then_inc(xn_ready, 1)
            dve.wait_ge(xn_ready, 3)
            nc.vector.tensor_tensor(ln[:, 2, :], ln[:, 2, :], ln[:, 1, :], ALU.add).then_inc(xn_ready, 1)
            dve.wait_ge(xn_ready, 4)
            nc.vector.tensor_scalar(ln[:, 3, :], ln[:, 2, :], 0.5, None, ALU.mult).then_inc(xn_ready, 1)
            dve.wait_ge(xn_ready, 5)
            nc.vector.reciprocal(inv_std[:, :], ln[:, 3, :]).then_inc(xn_ready, 1)
            dve.wait_ge(xn_ready, 6)

            def normalise(buf, t, done):
                nc.vector.tensor_scalar(buf[:, t, :], buf[:, t, :], moments[:, t, 0:1], inv_std[:, t:t + 1],
                                        ALU.subtract, ALU.mult).then_inc(done, 1)

            def scan_subtract(k):
                dve.wait_ge(scan_loaded[k % SCAN_SLOTS], 32 * (k // SCAN_SLOTS) + 32)
                nc.vector.tensor_tensor(scan[:, k % SCAN_SLOTS, 0, :], scan[:, k % SCAN_SLOTS, 0, :],
                                        scan[:, k % SCAN_SLOTS, 1, :], ALU.subtract).then_inc(scan_diff, 1)

            for t in range(TT):
                normalise(y, t, xn_ready)

            def x_low(t):
                dve.wait_ge(xT_hi, t + 1)
                nc.vector.tensor_tensor(xT[:, LO, :, t * P:(t + 1) * P],
                                        tr_ps[:, t % 2, :].rearrange("p (c t) -> p c t", c=HC),
                                        xT[:, HI, :, t * P:(t + 1) * P].bitcast(f32), ALU.subtract
                                        ).then_inc(xT_lo, 1)

            def take_coeff(m):
                dve.wait_ge(scan_abs, SCANS * (m + 1))
                dve.wait_ge(first_abs, FIRST * (m + 1))
                nc.vector.tensor_reduce(abs_part[:, m:m + 1], abs_sums[:, SUMS * m:SUMS * (m + 1)],
                                        axis=AX.X, op=ALU.add).then_inc(part_ready, 1)
                dve.wait_ge(total_ready, m + 1)
                nc.vector.tensor_scalar(coeff[:, m:m + 1], sum_ps[:, 0, m:m + 1], 1.0 / (INTER * HID), None, ALU.mult
                                        ).then_inc(coeff_ready, 1)
                dve.wait_ge(coeff_ready, m + 1)

            def first_make(n):
                kind, k = n // FIRST, n % SECTIONS
                dve.wait_ge(sign_ready, n + 1)
                if n >= SECTIONS:
                    dve.wait_ge(tr_done, n - SECTIONS + 1)
                nc.vector.scalar_tensor_tensor(weight_s[:, k, :], raw_s[:, k, :], coeff[:, kind:kind + 1],
                                               base_s[:, k, :], ALU.mult, ALU.add).then_inc(ffn_weight, 1)

            def first_low(n):
                dve.wait_ge(w_hi, n + 1)
                nc.vector.tensor_tensor(first_w(n)[:, LO, :], tr_ps[:, n % 2, :], first_w(n)[:, HI, :].bitcast(f32),
                                        ALU.subtract).then_inc(w_lo, 1)

            def first_h_make(c, th):
                dve.wait_ge(silu_done, 2 * FIRST)
                dve.wait_ge(up_done, 2 * c + th + 1)
                nc.vector.tensor_tensor(up_ps[:, th, :], silu_first[c][:, th * HALF:(th + 1) * HALF], up_ps[:, th, :],
                                        ALU.mult).then_inc(h_done, 1)

            def first_h_low(c, th):
                dve.wait_ge(h_hi, 2 * c + th + 1)
                nc.vector.tensor_tensor(first_h(c, LO, 4 * th, 4 * th + 4),
                                        up_ps[:, th, :].rearrange("p (t n) -> p t n", n=P),
                                        first_h(c, HI, 4 * th, 4 * th + 4).bitcast(f32), ALU.subtract
                                        ).then_inc(h_lo, 1)

            def ffn_make(c, par, kind):
                dve.wait_ge(sign_ready, FIRST_UNITS + c - FIRST + 1)
                dve.wait_ge(tr_done, 3 * c - 3)
                sl = slice(kind * HID, (kind + 1) * HID)
                nc.vector.scalar_tensor_tensor(weight[:, par, sl], raw[:, par, sl], coeff[:, kind:kind + 1],
                                               base[:, par, sl], ALU.mult, ALU.add).then_inc(ffn_weight, 1)

            def w_low(block_no, c, par, kind):
                dve.wait_ge(w_hi, unit_index(block_no, c, kind) + 1)
                buf = downT[:, par] if kind == DOWN else guT[:, par, kind]
                nc.vector.tensor_tensor(buf[:, LO, :], tr_ps[:, (3 * par + kind) % 2, :],
                                        buf[:, HI, :].bitcast(f32), ALU.subtract).then_inc(w_lo, 1)

            def h_make(n, th):
                dve.wait_ge(silu_done, 2 * n + th + 1)
                dve.wait_ge(up_done, 2 * n + th + 1)
                nc.vector.tensor_tensor(up_ps[:, th, :], silu_gate[:, th * HALF:(th + 1) * HALF], up_ps[:, th, :],
                                        ALU.mult).then_inc(h_done, 1)

            def h_low(n, par, th):
                dve.wait_ge(h_hi, 2 * n + th + 1)
                sl = slice(th * HALF, (th + 1) * HALF)
                nc.vector.tensor_tensor(h_split[:, par, LO, sl], up_ps[:, th, :],
                                        h_split[:, par, HI, sl].bitcast(f32), ALU.subtract).then_inc(h_lo, 1)

            def nf4_add(k, step):
                par, j = step // RAMPS, step % RAMPS
                r = RAMPS * k + step
                dve.wait_ge(nf4_ramp, r + 1)
                if not (isinstance(k, int) and r < 1):
                    dve.wait_ge(nf4_sum, r)
                nc.vector.scalar_tensor_tensor(base[:, par, :], ramp[:, (step % 2) * TRIO:(step % 2 + 1) * TRIO],
                                               NF4_RAMPS[j][2], base[:, par, :], ALU.min, ALU.add
                                               ).then_inc(nf4_sum, 1)

            def attn_add(m, step):
                half, j = step // RAMPS, step % RAMPS
                dve.wait_ge(attn_ramp, 2 * RAMPS * m + step + 1)
                dve.wait_ge(attn_acc, 2 * RAMPS * m + step + 2)
                dst = attn_sum[:, 2 * half:2 * half + 2, :].rearrange("p w h -> p (w h)")
                nc.vector.scalar_tensor_tensor(dst, ramp[:, (step % 2) * TRIO:(step % 2) * TRIO + 2 * HID],
                                               NF4_RAMPS[j][2], dst, ALU.min, ALU.add).then_inc(attn_acc, 1)

            def y_add(block_no, i, t, last=False):
                done = TT * (PAIRS * block_no + i - 1) + t
                dve.wait_ge(down_done, done + 1)
                if block_no == 0:
                    dve.wait_ge(y_done, done - TT + 1)
                    nc.vector.tensor_tensor(y[:, t, :], y[:, t, :], down_ps[t], ALU.add).then_inc(y_done, 1)
                else:
                    if isinstance(i, int) and i == 0:
                        dve.wait_ge(x1_ready, t + 1)
                    else:
                        dve.wait_ge(y_done, done - TT + 1)
                    nc.vector.tensor_tensor(x1[:, t, :], x1[:, t, :], down_ps[t], ALU.add
                                            ).then_inc(y_done, 1)
                    if last:
                        dve.wait_ge(y_done, done + 1)
                        if t == 0:
                            dve.wait_ge(ffn_silu, 1)
                        nc.vector.tensor_tensor(y[:, t, :], x1[:, t, :], y[:, t, :], ALU.mult).then_inc(gated, 1)

            def make(step, i, make_ffn, attn, make_nf4):
                if make_ffn and step % RAMPS == 0:
                    for kind in (GATE, UP, DOWN):
                        ffn_make(2 * i + 2 + step // RAMPS, step // RAMPS, kind)
                if attn is not None:
                    attn_add(attn, step)
                if make_nf4 is not None:
                    nf4_add(2 * make_nf4, step)

            def iteration(block_no, i, make_ffn=False, attn=None, make_nf4=None, last=False):
                n, a, b = CHUNKS * block_no + 2 * i, 2 * i, 2 * i + 1
                bg = (i, make_ffn, attn, make_nf4)
                w_low(block_no, a, 0, DOWN)
                make(0, *bg)
                make(1, *bg)
                w_low(block_no, b, 1, GATE)
                make(2, *bg)
                w_low(block_no, b, 1, UP)
                make(3, *bg)
                h_make(n, 0)
                make(4, *bg)
                w_low(block_no, b, 1, DOWN)
                h_low(n, 0, 0)
                h_make(n, 1)
                make(5, *bg)
                h_low(n, 0, 1)
                make(6, *bg)
                h_make(n + 1, 0)
                h_low(n + 1, 1, 0)
                make(7, *bg)
                h_make(n + 1, 1)
                for t in range(TT):
                    y_add(block_no, i, t, last=last and block_no == 1)
                    if t == 0:
                        h_low(n + 1, 1, 1)
                    if t == 1:
                        make(8, *bg)
                    if t == 3 and not last:
                        w_low(block_no, a + 2, 0, GATE)
                    if t == 3:
                        make(9, *bg)
                    if t == 5 and not last:
                        w_low(block_no, a + 2, 0, UP)

            x_low(0)
            x_low(1)
            scan_subtract(0)
            x_low(2)
            x_low(3)
            scan_subtract(1)
            x_low(4)
            x_low(5)
            x_low(6)
            x_low(7)
            scan_subtract(2)
            scan_subtract(3)
            take_coeff(GATE)
            first_make(0)
            first_make(1)
            first_low(0)
            first_low(1)
            first_make(2)
            first_make(3)
            scan_subtract(4)
            scan_subtract(5)
            scan_subtract(6)
            first_low(2)
            scan_subtract(7)
            first_low(3)
            take_coeff(UP)
            first_make(4)
            first_make(5)
            scan_subtract(8)
            first_make(6)
            first_make(7)
            first_low(4)
            first_low(5)
            scan_subtract(9)
            first_h_make(0, 0)
            scan_subtract(10)
            first_h_low(0, 0)
            first_h_make(0, 1)
            scan_subtract(11)
            first_h_low(0, 1)
            first_low(6)
            first_h_make(1, 0)
            first_h_low(1, 0)
            first_h_make(1, 1)
            first_h_low(1, 1)
            take_coeff(DOWN)
            first_low(7)
            first_make(8)
            first_h_make(2, 0)
            first_make(9)
            first_h_low(2, 0)
            first_h_make(2, 1)
            first_make(10)
            first_h_low(2, 1)
            first_make(11)
            first_low(8)
            first_low(9)
            first_h_make(3, 0)
            first_h_low(3, 0)
            first_low(10)
            first_low(11)
            first_h_make(3, 1)
            first_h_low(3, 1)
            for k in range(2):
                nc.vector.memset(ln[:, 2, k:k + 1], 0.0).then_inc(attn_acc, 1)
            for t in range(TT):
                dve.wait_ge(down_done, t + 1)
                nc.vector.tensor_copy(y[:, t, :], down_ps[t]).then_inc(y_done, 1)
                if t == 1:
                    for kind in (GATE, UP, DOWN):
                        ffn_make(4, 0, kind)
                if t == 3:
                    w_low(0, 4, 0, GATE)
                if t == 5:
                    w_low(0, 4, 0, UP)
                    for kind in (GATE, UP, DOWN):
                        ffn_make(5, 1, kind)
            with dve.Fori(2, 5) as i:
                iteration(0, i, make_ffn=True, attn=i - 2)
            iteration(0, 5, make_ffn=True, attn=3)
            iteration(0, 6, make_nf4=0, last=True)

            for m in range(4):
                dve.wait_ge(lora_qkv, m + 1)
                dve.wait_ge(attn_scaled, 5 * 4 + 1)
                nc.vector.tensor_tensor(w_qkv[:, m, :], w_qkv[:, m, :], four_ps[m], ALU.add).then_inc(qkv_full, 1)
                dve.wait_ge(oT_hi, m + 1)
                nc.vector.tensor_tensor(oT_split[:, LO, :, m * P:(m + 1) * P],
                                        tr_ps[:, m % 2, :].rearrange("p (c o) -> p c o", c=4),
                                        oT_split[:, HI, :, m * P:(m + 1) * P].bitcast(f32), ALU.subtract
                                        ).then_inc(oT_lo, 1)
            for t in range(TT):
                dve.wait_ge(x_again[t // 4], 16)
                normalise(x1, t, xn_again)
            dve.wait_ge(oT_tr, 4)
            dve.wait_ge(qkv_lo, 4)
            nc.vector.memset(A_down[64:128, :].bitcast(f32), 0.0).then_inc(lora_zero, 1)
            for m in range(2):
                rows = slice(64 * m + 32, 64 * m + 64)
                dve.wait_ge(lora_hi, m + 1)
                nc.vector.tensor_tensor(A_gu[rows, m, :], A_gu_raw[rows, :], A_gu[rows, m, :].bitcast(f32),
                                        ALU.subtract).then_inc(A_low, 1)
            dve.wait_ge(lora_hi, 9)
            nc.vector.tensor_tensor(A_down[32:64, :], A_down_raw[32:64, :], A_down[32:64, :].bitcast(f32),
                                    ALU.subtract).then_inc(A_low, 1)
            for c in range(HC):
                dve.wait_ge(MT_hi, c + 1)
                nc.vector.tensor_tensor(MT[:, LO, c, :], four_ps[c], MT[:, HI, c, :].bitcast(f32), ALU.subtract
                                        ).then_inc(MT_lo, 1)
            for t in range(TT + 1):
                if t < TT:
                    dve.wait_ge(x1_sum, t + 1)
                    dve.wait_ge(xn_again, t + 1)
                    nc.vector.tensor_tensor(x1[:, t, :], x1[:, t, :], sum_ps[:, t % 2, :], ALU.add
                                            ).then_inc(x1_ready, 1)
                if t > 0:
                    u = t - 1
                    dve.wait_ge(x1_hi, u + 1)
                    nc.vector.tensor_tensor(xT[:, LO, :, u * P:(u + 1) * P],
                                            tr_ps[:, u % 2, :].rearrange("p (c t) -> p c t", c=HC),
                                            xT[:, HI, :, u * P:(u + 1) * P].bitcast(f32), ALU.subtract
                                            ).then_inc(x1_lo, 1)
            for kind in (GATE, UP):
                w_low(1, 0, 0, kind)
            with dve.Fori(0, 6) as i:
                iteration(1, i, make_nf4=i + 1)
            iteration(1, 6, last=True)

        @block.tensor
        def _(pe):
            def transpose4(bank, src, accumulate=False):
                for c in range(HC):
                    last = nc.tensor.matmul(tr_ps[:, bank, c * P:(c + 1) * P], src(c), ident[:], is_transpose=True,
                                            start=(c == 0), stop=(c == HC - 1 and not accumulate))
                return last

            pe.wait_ge(const_ready, 3)
            for t in range(TT):
                pe.wait_ge(xn_ready, 6 + t + 1)
                if t >= 2:
                    pe.wait_ge(xT_lo, t - 1)
                transpose4(t % 2, lambda c: y[:, t, c * P:(c + 1) * P]).then_inc(xT_tr, 1)
            pe.wait_ge(xT_lo, TT)

            def total(m):
                pe.wait_ge(part_ready, m + 1)
                nc.tensor.matmul(sum_ps[:, 0, m:m + 1], ones[:], abs_part[:, m:m + 1], start=True, stop=True
                                 ).then_inc(total_ready, 1)

            def first_unit(n):
                if n >= 2:
                    pe.wait_ge(w_lo, n - 1)
                pe.wait_ge(ffn_weight, n + 1)
                transpose4(n % 2, lambda q: weight_s[:, n % SECTIONS, q * P:(q + 1) * P]).then_inc(tr_done, 1)

            def first_project(kind, c):
                n = FIRST * kind + c
                pe.wait_ge(w_lo, n + 1)
                for th in range(2):
                    if c > 0:
                        pe.wait_ge(silu_done if kind == GATE else h_lo, 2 * c + th - 1)
                    ps = (gate_ps if kind == GATE else up_ps)[:, th, :]
                    for hc in range(HC):
                        for w_part, x_part in PASSES:
                            last = nc.tensor.matmul(ps, first_w(n)[:, w_part, hc * P:(hc + 1) * P],
                                                    xT[:, x_part, hc, th * HALF:(th + 1) * HALF],
                                                    start=(hc == 0 and w_part == x_part == HI),
                                                    stop=(hc == HC - 1 and w_part == LO))
                    last.then_inc(gate_done if kind == GATE else up_done, 1)

            def first_down(t):
                if t == 0:
                    pe.wait_ge(coeff_ready, 3)
                    pe.wait_ge(w_lo, FIRST_UNITS)
                    pe.wait_ge(h_lo, 2 * FIRST - 1)
                    pe.wait_ge(silu_done, 2 * FIRST)
                if t == TT // 2:
                    pe.wait_ge(h_lo, 2 * FIRST)
                if t in (4, 5):
                    pe.wait_ge(y_done, t - 3)
                for c in range(FIRST):
                    for h_part, w_part in PASSES:
                        last = nc.tensor.matmul(down_ps[t], first_h(c, h_part, t, t + 1).rearrange("p t n -> p (t n)"),
                                                first_w(2 * FIRST + c)[:, w_part, :],
                                                start=(c == 0 and h_part == w_part == HI),
                                                stop=(c == FIRST - 1 and h_part == LO))
                last.then_inc(down_done, 1)

            def unit(block_no, c, par, kind):
                index = unit_index(block_no, c, kind)
                bank = (3 * par + kind) % 2
                pe.wait_ge(w_hi, index - 1)
                pe.wait_ge(w_lo, index - 1)
                if block_no == 0:
                    pe.wait_ge(ffn_weight, index + 1)
                else:
                    pe.wait_ge(nf4_weight, c + 1)
                last = transpose4(bank, lambda n: weight[:, par, kind * HID + n * P:kind * HID + (n + 1) * P],
                                  accumulate=block_no == 1)
                if block_no == 1 and kind == DOWN:
                    pe.wait_ge(A_down_ready, c + 1)
                    last = nc.tensor.matmul(tr_ps[:, bank, :], A_down_now[:, par, :], B_downT[:, :],
                                            start=False, stop=True)
                elif block_no == 1:
                    for n in range(HC):
                        last = nc.tensor.matmul(tr_ps[:, bank, n * P:(n + 1) * P], A_gu[:, kind, n * P:(n + 1) * P],
                                                B_guT[:, ds(c * P, P)], start=False, stop=(n == HC - 1))
                last.then_inc(tr_done, 1)

            def project(block_no, c, par, kind, th):
                n = CHUNKS * block_no + c
                if th == 0:
                    pe.wait_ge(w_lo, unit_index(block_no, c, kind) + 1)
                if par == 1:
                    pe.wait_ge(silu_done if kind == GATE else h_lo, 2 * n + th - 1)
                else:
                    pe.wait_ge(y_done, TT // 2 * n + (3 if kind == GATE else 7) + th - 2 * TT)
                ps = (gate_ps if kind == GATE else up_ps)[:, th, :]
                for hc in range(HC):
                    for w_part, x_part in PASSES:
                        last = nc.tensor.matmul(ps, guT[:, par, kind, w_part, hc * P:(hc + 1) * P],
                                                xT[:, x_part, hc, th * HALF:(th + 1) * HALF],
                                                start=(hc == 0 and w_part == x_part == HI),
                                                stop=(hc == HC - 1 and w_part == LO))
                last.then_inc(gate_done if kind == GATE else up_done, 1)

            def down(block_no, i, t):
                q = PAIRS * block_no + i
                done = TT * (q - 1) + t
                if t == 0:
                    pe.wait_ge(w_lo, 6 * q + 6)
                    pe.wait_ge(h_lo, 4 * q + 3)
                if t == TT // 2:
                    pe.wait_ge(h_lo, 4 * q + 4)
                if t in (2, 3):
                    pe.wait_ge(silu_done, 4 * q + 1 + t)
                elif t < 6:
                    pe.wait_ge(y_done, done - 3)
                for par in range(2):
                    for h_part, w_part in PASSES:
                        last = nc.tensor.matmul(down_ps[t], h_split[:, par, h_part, t * P:(t + 1) * P],
                                                downT[:, par, w_part, :],
                                                start=(par == 0 and h_part == w_part == HI),
                                                stop=(par == 1 and h_part == LO))
                last.then_inc(down_done, 1)

            def iteration(block_no, i, last=False):
                a, b = 2 * i, 2 * i + 1
                unit(block_no, a, 0, DOWN)
                project(block_no, a, 0, GATE, 0)
                unit(block_no, b, 1, GATE)
                project(block_no, a, 0, GATE, 1)
                unit(block_no, b, 1, UP)
                project(block_no, a, 0, UP, 0)
                unit(block_no, b, 1, DOWN)
                project(block_no, a, 0, UP, 1)
                for kind in (GATE, UP):
                    for th in range(2):
                        project(block_no, b, 1, kind, th)
                for t in range(TT):
                    down(block_no, i, t)
                    if t == 3 and not last:
                        unit(block_no, a + 2, 0, GATE)
                    if t == 5 and not last:
                        unit(block_no, a + 2, 0, UP)

            total(GATE)
            first_unit(0)
            first_unit(1)
            first_project(GATE, 0)
            first_unit(2)
            first_project(GATE, 1)
            first_unit(3)
            first_project(GATE, 2)
            total(UP)
            first_project(GATE, 3)
            first_unit(4)
            first_unit(5)
            first_project(UP, 0)
            first_unit(6)
            first_project(UP, 1)
            first_unit(7)
            total(DOWN)
            first_project(UP, 2)
            first_unit(8)
            first_unit(9)
            first_project(UP, 3)
            first_unit(10)
            first_unit(11)
            for t in range(TT):
                first_down(t)
                if t == 3:
                    unit(0, 4, 0, GATE)
                if t == 5:
                    unit(0, 4, 0, UP)
            with pe.Fori(2, 6) as i:
                iteration(0, i)
            iteration(0, 6, last=True)

            pe.wait_ge(w_lo, 3 * CHUNKS)
            pe.wait_ge(B_nat_ready, 3)
            for bank, nat in enumerate((B_qkv_nat, B_o_nat)):
                for j in range(4):
                    last = nc.tensor.matmul(tr_ps[0:64, bank, j * P:(j + 1) * P], nat[:, j, :], ident[:],
                                            is_transpose=True, start=(j == 0), stop=(j == 3))
                last.then_inc(B_tr, 1)
            pe.wait_ge(B_T_ready, 2)
            pe.wait_ge(silu_done, 2 * CHUNKS)
            pe.wait_ge(h_lo, 2 * CHUNKS)
            pe.wait_ge(fold_loaded, 16 * 5)
            pe.wait_ge(y_done, TT * GROUPS)
            for m in range(4):
                nc.tensor.matmul(four_ps[m], B_qkvT[0:64, m * P:(m + 1) * P], A_attn[0:64, :], start=True, stop=True
                                 ).then_inc(lora_qkv, 1)
            pe.wait_ge(attn_scaled, 5 * 4 + 1)
            for j in range(4):
                if j >= 2:
                    pe.wait_ge(oT_lo, j - 1)
                transpose4(j % 2, lambda c: w_o[:, j, c * P:(c + 1) * P], accumulate=True)
                for c in range(4):
                    last = nc.tensor.matmul(tr_ps[:, j % 2, c * P:(c + 1) * P], A_attn[0:64, c * P:(c + 1) * P],
                                            B_oT[0:64, j * P:(j + 1) * P], start=False, stop=(c == 3))
                last.then_inc(oT_tr, 1)
            pe.wait_ge(qkv_full, 4)
            pe.wait_ge(qkv_lo, 4)
            pe.wait_ge(oT_lo, 4)
            for hc in range(HC):
                for m in range(4):
                    for a_part, b_part in PASSES:
                        last = nc.tensor.matmul(four_ps[hc], qkv_split[:, m, a_part, hc * P:(hc + 1) * P],
                                                oT_split[:, b_part, m, :],
                                                start=(m == 0 and a_part == b_part == HI),
                                                stop=(m == 3 and a_part == LO))
                last.then_inc(MT_done, 1)
            for n in range(5):
                if n < 4:
                    pe.wait_ge(lora_lo, 2 if 4 * n + 4 <= HALF_CHUNKS else 4)
                else:
                    pe.wait_ge(lora_lo, 6)
                if n >= 2:
                    pe.wait_ge(lora_T, n - 1)
                if n < 4:
                    chunks = range(4 * n, min(4 * n + 4, CHUNKS))
                    for c in chunks:
                        nat = B_gu_nat[c // HALF_CHUNKS][:, c % HALF_CHUNKS, :, :, :].rearrange("p m s r -> p (m s r)")
                        last = nc.tensor.matmul(tr_ps[:, n % 2, (c - 4 * n) * P:(c - 4 * n + 1) * P], nat, ident[:],
                                                is_transpose=True, start=(c == 4 * n), stop=(c == chunks[-1]))
                else:
                    for j in range(4):
                        last = nc.tensor.matmul(tr_ps[0:64, n % 2, j * P:(j + 1) * P],
                                                B_down_nat[:, j, :, :].rearrange("p s r -> p (s r)"), ident[:],
                                                is_transpose=True, start=(j == 0), stop=(j == 3))
                last.then_inc(lora_tr, 1)
            pe.wait_ge(MT_lo, HC)
            pe.wait_ge(y_done, TT * GROUPS)

            def x1_transpose(t):
                pe.wait_ge(x1_ready, t + 1)
                if t < 2:
                    pe.wait_ge(lora_T, 5)
                else:
                    pe.wait_ge(x1_lo, t - 1)
                transpose4(t % 2, lambda c: x1[:, t, c * P:(c + 1) * P]).then_inc(x1_tr, 1)

            for t in range(TT):
                if t >= 2:
                    pe.wait_ge(x1_ready, t - 1)
                for hc in range(HC):
                    for x_part, m_part in PASSES:
                        last = nc.tensor.matmul(sum_ps[:, t % 2, :], xT[:, x_part, hc, t * P:(t + 1) * P],
                                                MT[:, m_part, hc, :],
                                                start=(hc == 0 and x_part == m_part == HI),
                                                stop=(hc == HC - 1 and x_part == LO))
                last.then_inc(x1_sum, 1)
                if t > 0:
                    x1_transpose(t - 1)
            x1_transpose(TT - 1)
            pe.wait_ge(x1_lo, TT)
            pe.wait_ge(A_low, 2)
            unit(1, 0, 0, GATE)
            unit(1, 0, 0, UP)
            with pe.Fori(0, 6) as i:
                iteration(1, i)
            iteration(1, 6, last=True)


_INS = ["L0_attn_x", "L0_attn_codes_attn", "L0_attn_scales_attn", "L0_attn_codes_gu", "L0_attn_scales_gu",
        "L0_attn_codes_down", "L0_attn_scales_down", "L0_attn_lora_A_h", "L0_attn_lora_A_down",
        "L0_attn_lora_B_attn", "L0_attn_lora_B_gu", "L0_attn_lora_B_down",
        "L0_ffn_w1", "L0_ffn_mean_w1", "L0_ffn_w2", "L0_ffn_mean_w2", "L0_ffn_w3", "L0_ffn_mean_w3"]


def kernel(**inputs):
    import numpy as np
    import concourse.bacc as bacc
    from concourse.bass_utils import run_bass_kernel_spmd

    nc = bacc.Bacc("TRN2", target_bir_lowering=False, num_devices=1)
    arrays, args = {}, []
    for name in _INS:
        a = np.ascontiguousarray(inputs[name])
        arrays[name] = a
        args.append(nc.dram_tensor(name, a.shape, mybir.dt.from_np(a.dtype), kind="ExternalInput").ap())
    shape = inputs["L0_attn_x"].shape
    args.append(nc.dram_tensor("out", shape, mybir.dt.float32, kind="ExternalOutput").ap())
    block_kernel(nc, *args)
    result = run_bass_kernel_spmd(nc, [arrays], core_ids=[0])
    return result.results[0]["out"]
```

```python
import concourse.bass as bass
from concourse import mybir
from contextlib import ExitStack

P = 128
TOKENS, HID, INTER, RANK = 1024, 512, 1792, 16
BLOCK = 64
EPS = 1e-5
CHUNKS = INTER // P
HC = HID // P
TT = TOKENS // P
HALF = TOKENS // 2
TRIO = 3 * HID
PAIRS = CHUNKS // 2
FIRST = 4
FIRST_UNITS = 3 * FIRST
SECTIONS = 6
SCAN = INTER - FIRST * P
SCANS = HID // P
SUMS = SCANS + FIRST
SCAN_SLOTS = 4
POOL_TILES = 2
GROUPS = PAIRS - 1

NF4_STEP = 0.30380719900131226
NF4_OFFSET = 3.2915611267089844
NF4_RAMPS = [
    (0.4722318649291992, -0.5077152252197266, 6.19162654876709),
    (0.16412925720214844, -0.3930339813232422, 1.7030200958251953),
    (0.05514240264892578, -0.24013614654541016, 0.39171409606933594),
    (0.02811431884765625, -0.18800067901611328, 0.09946441650390625),
    (0.036876678466796875, -0.27657508850097656, 0.031052589416503906),
]
RAMPS = len(NF4_RAMPS)
GATE, UP, DOWN = 0, 1, 2
HI, LO = 0, 1
PASSES = [(HI, HI), (HI, LO), (LO, HI)]


def block_kernel(nc, x, codes_attn, scales_attn, codes_gu, scales_gu, codes_down, scales_down,
                 lora_A_h, lora_A_down, lora_B_attn, lora_B_gu, lora_B_down,
                 w1, mean_w1, w2, mean_w2, w3, mean_w3, out):
    f32, f32r, i32 = mybir.dt.float32, mybir.dt.float32r, mybir.dt.int32
    ALU, ACT, AX = mybir.AluOpType, mybir.ActivationFunctionType, mybir.AxisListType
    ds = bass.ds

    x_v = x.rearrange("b s h -> (b s) h").rearrange("(t p) h -> p t h", p=P)
    out_v = out.rearrange("b s h -> (b s) h").rearrange("(t p) h -> p t h", p=P)
    w2_v, mean_w2_v = (m.rearrange("(q p) i -> p q i", p=P) for m in (w2, mean_w2))
    scan_v = [m[FIRST * P:, :].rearrange("(p a) n -> p (a n)", p=P).rearrange("p (k s) -> p k s", s=SCAN)
              for m in (w1, mean_w1, w3, mean_w3)] + [m[:, :, FIRST * P:] for m in (w2_v, mean_w2_v)]
    codes_gu_v = codes_gu.rearrange("m i h -> i m h")
    codes_down_v = codes_down.rearrange("(q p) i -> p q i", p=P)
    codes_attn_v = codes_attn.rearrange("w o h -> o w h")

    ctx = ExitStack()
    with ctx:
        def sb(name, shape, dt=f32):
            return ctx.enter_context(nc.sbuf_tensor(name, shape, dt))

        def sem(name):
            return ctx.enter_context(nc.semaphore(name))

        ident = sb("ident", [P, P])
        ones = sb("ones", [P, P])
        stats = sb("stats", [P, TT, 6])
        moments = sb("moments", [P, TT, 2])
        ln = sb("ln", [P, 5, TT])
        inv_std = sb("inv_std", [P, TT])
        ramp_bias = sb("ramp_bias", [P, RAMPS])
        abs_sums = sb("abs_sums", [P, 3 * SUMS])
        abs_part = sb("abs_part", [P, 3])
        coeff = sb("coeff", [P, 3])
        xT = sb("xT", [P, 2, HC, TOKENS], f32r)
        h_split = sb("h_split", [P, 2, 2, TOKENS], f32r)
        staging = sb("staging", [P, TOKENS])
        downT = sb("downT", [P, 2, 2, HID], f32r)
        guT = sb("guT", [P, 2, 2, 2, HID], f32r)
        raw = sb("raw", [P, 2, TRIO])
        base = sb("base", [P, 2, TRIO])
        weight = sb("weight", [P, 2, TRIO])
        ramp = sb("ramp", [P, 2 * TRIO])
        silu_gate = sb("silu_gate", [P, TOKENS])
        with nc.sbuf_tensor("y", [P, TT, HID], f32) as y:
            pass
        h_more = sb("h_more", [P, TT, HID], f32r)
        scale_raw = sb("scale_raw", [P, CHUNKS, 2, 8])
        scale_down_raw = sb("scale_down_raw", [P, HC, 2 * CHUNKS])
        scale_trio = sb("scale_trio", [P, CHUNKS, 24])
        scale_attn_raw = sb("scale_attn_raw", [P, 4, 4, 8])
        scale_attn = sb("scale_attn", [P, 4, 4, 8])
        A_gu = sb("A_gu", [P, 2, HID], f32r)
        B_downT = sb("B_downT", [P, HID], f32r)
        A_down_now = sb("A_down_now", [P, 2, P], f32r)
        with nc.sbuf_tensor("scan", [P, SCAN_SLOTS, 2, SCAN], f32) as scan:
            pass
        with nc.sbuf_tensor("attn_codes", [P, 4, HID], f32) as attn_codes, \
                nc.sbuf_tensor("attn_sum", [P, 4, HID], f32) as attn_sum, \
                nc.sbuf_tensor("w_qkv", [P, 4, HID], f32) as w_qkv, \
                nc.sbuf_tensor("w_o", [P, 4, HID], f32) as w_o, \
                nc.sbuf_tensor("x1", [P, TT, HID], f32) as x1:
            pass
        with nc.sbuf_tensor("downT_more_space", [P, 4, HID], f32), \
                nc.sbuf_tensor("downT_more", [P, 2, 2, HID], f32r) as downT_more:
            pass
        MT = sb("MT", [P, 2, HC, HID], f32r)
        A_down = sb("A_down", [P, INTER], f32r)
        B_guT = sb("B_guT", [P, INTER], f32r)
        sb("x1_space", [P, 4 * 4 * HID - 2 * HC * HID - 2 * INTER + TT * HID])
        A_attn = x1[:, 0, :]
        B_qkvT = x1[:, 1, :]
        B_oT = x1[:, 2, :]
        B_attn_raw = x1[:, 3, 0:256].rearrange("p (j w r) -> p j w r", j=4, w=4)
        B_qkv_nat = x1[:, 4, 0:256].rearrange("p (j r) -> p j r", j=4)
        B_o_nat = x1[:, 4, 256:512].rearrange("p (j r) -> p j r", j=4)
        qkv_split = h_split[:, :, :, :].rearrange("p a b t -> p (a b t)").rearrange(
            "p (m s h) -> p m s h", m=4, s=2)
        oT_split = guT[:, :, :, :, :].rearrange("p a b c h -> p (a b c h)").rearrange(
            "p (s m h) -> p s m h", s=2, m=4)
        B_down_nat = ramp[:, 0:256].rearrange("p (j s r) -> p j s r", j=4, s=4)
        B_down_raw = ramp[:, 256:320].rearrange("p (j r) -> p j r", j=4)
        B_gu_raw = ramp[:, 320:768].rearrange("p (c m r) -> p c m r", c=CHUNKS, m=2)
        A_gu_raw = ramp[:, 768:1280]
        A_down_raw = ramp[:, 1280:1280 + INTER]
        HALF_CHUNKS = CHUNKS // 2
        B_gu_nat = [t[:, 0:HALF_CHUNKS * P].rearrange("p (c m s r) -> p c m s r", c=HALF_CHUNKS, m=2, s=4)
                    for t in (silu_gate, staging)]

        raw_s, base_s, weight_s = (t[:, :, :].rearrange("p a (k h) -> p (a k) h", h=HID) for t in (raw, base, weight))
        silu_first = [silu_gate[:, :], staging[:, :], ramp[:, 0:TOKENS], ramp[:, TOKENS:2 * TOKENS]]
        abs_out = ramp[:, 2 * TOKENS:2 * TOKENS + HID]

        def first_w(n):
            if n < 2 * FIRST:
                return guT[:, n % FIRST // 2, n % 2]
            c = n - 2 * FIRST
            return downT[:, c] if c < 2 else downT_more[:, c - 2]

        signT = downT[:, 0, HI, :]

        def first_h(c, part, t0, t1):
            if c < 2:
                return h_split[:, c, part, t0 * P:t1 * P].rearrange("p (t n) -> p t n", n=P)
            k = 2 * (c - 2) + part
            return h_more[:, t0:t1, k * P:(k + 1) * P]

        def pb(name):
            return ctx.enter_context(nc.psum_tensor(name, [P, 2, HALF], f32))

        gate_ps, up_ps, tr_ps, sum_ps = pb("gate_ps"), pb("up_ps"), pb("tr_ps"), pb("sum_ps")
        down_ps = [sum_ps[:, 0, :], sum_ps[:, 1, :], gate_ps[:, 0, :], gate_ps[:, 1, :],
                   sum_ps[:, 0, :], sum_ps[:, 1, :], up_ps[:, 0, :], up_ps[:, 1, :]]
        four_ps = [gate_ps[:, 0, :], gate_ps[:, 1, :], up_ps[:, 0, :], up_ps[:, 1, :]]
        xT_ps = [tr_ps[:, 0, :], tr_ps[:, 1, :]] + four_ps + [tr_ps[:, 0, :], tr_ps[:, 1, :]]
        fold_ps = [tr_ps[:, 0, :], tr_ps[:, 1, :], gate_ps[:, 0, :], gate_ps[:, 1, :]]

        x_loaded = [sem("x_loaded0"), sem("x_loaded1")]
        const_ready = sem("const_ready")
        ln_step = sem("ln_step")
        root_done = sem("root_done")
        xn_ready = sem("xn_ready")
        xT_tr = sem("xT_tr")
        xT_hi = sem("xT_hi")
        xT_lo = sem("xT_lo")
        scan_loaded = [sem(f"scan_loaded{n}") for n in range(SCAN_SLOTS)]
        scan_diff = sem("scan_diff")
        scan_diff_pool = sem("scan_diff_pool")
        scan_abs = sem("scan_abs")
        first_loaded = [sem(f"first_loaded{n}") for n in range(SECTIONS)]
        first_abs = sem("first_abs")
        sign_T = sem("sign_T")
        early_part = sem("early_part")
        early_gate = sem("early_gate")
        part_ready = sem("part_ready")
        total_ready = sem("total_ready")
        coeff_ready = sem("coeff_ready")
        scales_loaded = sem("scales_loaded")
        scales_ready = sem("scales_ready")
        chunk_loaded = [sem("chunk_loaded0"), sem("chunk_loaded1")]
        diff_ready = sem("diff_ready")
        sign_ready = sem("sign_ready")
        ffn_weight = sem("ffn_weight")
        nf4_ramp = sem("nf4_ramp")
        nf4_sum = sem("nf4_sum")
        nf4_weight = sem("nf4_weight")
        A_down_ready = sem("A_down_ready")
        tr_done = sem("tr_done")
        w_hi = sem("w_hi")
        w_lo = sem("w_lo")
        gate_done = sem("gate_done")
        up_done = sem("up_done")
        silu_done = sem("silu_done")
        h_done = sem("h_done")
        h_hi = sem("h_hi")
        h_lo = sem("h_lo")
        down_done = sem("down_done")
        y_done = sem("y_done")
        attn_loaded = sem("attn_loaded")
        gpsimd_passed = sem("gpsimd_passed")
        attn_start = sem("attn_start")
        attn_ramp = sem("attn_ramp")
        attn_acc = sem("attn_acc")
        attn_scaled = sem("attn_scaled")
        fold_loaded = sem("fold_loaded")
        B_nat_ready = sem("B_nat_ready")
        B_tr = sem("B_tr")
        B_T_ready = sem("B_T_ready")
        lora_qkv = sem("lora_qkv")
        qkv_full = sem("qkv_full")
        qkv_hi = sem("qkv_hi")
        qkv_lo = sem("qkv_lo")
        oT_tr = sem("oT_tr")
        oT_hi = sem("oT_hi")
        oT_lo = sem("oT_lo")
        MT_done = sem("MT_done")
        MT_hi = sem("MT_hi")
        MT_lo = sem("MT_lo")
        x_again = [sem("x_again0"), sem("x_again1")]
        xn_again = sem("xn_again")
        x1_sum = sem("x1_sum")
        x1_ready = sem("x1_ready")
        x1_tr = sem("x1_tr")
        x1_hi = sem("x1_hi")
        x1_lo = sem("x1_lo")
        lora_loaded = sem("lora_loaded")
        lora_zero = sem("lora_zero")
        lora_hi = sem("lora_hi")
        lora_lo = sem("lora_lo")
        A_low = sem("A_low")
        lora_tr = sem("lora_tr")
        lora_T = sem("lora_T")
        ffn_silu = sem("ffn_silu")
        x_last = sem("x_last")
        gated = sem("gated")
        out_ready = sem("out_ready")
        out_stored = sem("out_stored")

        block = ctx.enter_context(nc.Block())

        def unit_index(block_no, c, kind):
            return 3 * (CHUNKS * block_no + c) + kind

        @block.sync
        def _(sp):
            for n in range(2):
                sp.dma_start(y[:, 4 * n:4 * n + 4, :], x_v[:, 4 * n:4 * n + 4, :]).then_inc(x_loaded[n], 16)

            def load_scan(k):
                m, part = k // SCANS, k % SCANS
                if k >= SCAN_SLOTS:
                    sp.wait_ge(scan_abs, k - SCAN_SLOTS + 1)
                for which in range(2):
                    sp.dma_start(scan[:, k % SCAN_SLOTS, which, :], scan_v[2 * m + which][:, part, :]
                                 ).then_inc(scan_loaded[k % SCAN_SLOTS], 16)

            def load_first(n):
                kind, c = n // FIRST, n % FIRST
                if n >= SECTIONS:
                    sp.wait_ge(ffn_weight, n - SECTIONS + 1)
                for dst, src in ((raw_s, (w1, w3, w2_v)[kind]), (base_s, (mean_w1, mean_w3, mean_w2_v)[kind])):
                    if kind == DOWN:
                        sp.dma_start(dst[:, n % SECTIONS, :].rearrange("p (q i) -> p q i", q=HC),
                                     src[:, :, c * P:(c + 1) * P]).then_inc(first_loaded[n % SECTIONS], 16)
                    else:
                        sp.dma_start(dst[:, n % SECTIONS, :], src[c * P:(c + 1) * P, :]
                                     ).then_inc(first_loaded[n % SECTIONS], 16)

            def load_ffn(c, par):
                sp.wait_ge(ffn_weight, 3 * c - 3)
                for dst, gate, up, down in ((raw, w1, w3, w2_v), (base, mean_w1, mean_w3, mean_w2_v)):
                    sp.dma_start(dst[:, par, 0:HID], gate[ds(c * P, P), :]).then_inc(chunk_loaded[par], 16)
                    sp.dma_start(dst[:, par, HID:2 * HID], up[ds(c * P, P), :]).then_inc(chunk_loaded[par], 16)
                    sp.dma_start(dst[:, par, 2 * HID:].rearrange("p (q i) -> p q i", q=HC),
                                 down[:, :, ds(c * P, P)]).then_inc(chunk_loaded[par], 16)

            def load_nf4(k, par):
                if isinstance(k, int) and k < 2:
                    sp.wait_ge(ffn_weight, 3 * (CHUNKS - 2 + k) + 3)
                else:
                    sp.wait_ge(nf4_ramp, RAMPS * (k - 1))
                sp.dma_start(raw[:, par, 0:2 * HID].bitcast(i32).rearrange("p (m h) -> p m h", m=2),
                             codes_gu_v[ds(k * P, P), :, :]).then_inc(chunk_loaded[par], 16)
                sp.dma_start(raw[:, par, 2 * HID:].bitcast(i32).rearrange("p (q i) -> p q i", q=HC),
                             codes_down_v[:, :, ds(k * P, P)]).then_inc(chunk_loaded[par], 16)

            def load_attn(m):
                if not isinstance(m, int):
                    sp.wait_ge(attn_ramp, 2 * RAMPS * m)
                sp.dma_start(attn_codes[:, :, :].bitcast(i32), codes_attn_v[ds(m * P, P), :, :]
                             ).then_inc(attn_loaded, 16)

            load_first(0)
            for m in range(3):
                for half in range(2):
                    for k in range(2):
                        load_scan(SCANS * m + 2 * half + k)
                    for n in range(FIRST * m + 2 * half, FIRST * m + 2 * half + 2):
                        if n > 0:
                            load_first(n)
            for m in range(2):
                sp.dma_start(scale_raw[:, :, m, :], scales_gu[m].rearrange("(c p) b -> p c b", p=P)
                             ).then_inc(scales_loaded, 16)
            sp.dma_start(scale_down_raw[:, :, :], scales_down.rearrange("(q p) b -> p q b", p=P)
                         ).then_inc(scales_loaded, 16)
            for m in range(4):
                sp.dma_start(scale_attn_raw[:, m, :, :],
                             scales_attn[:, m * P:(m + 1) * P, :].rearrange("w p b -> p w b")
                             ).then_inc(scales_loaded, 16)
            load_ffn(4, 0)
            load_ffn(5, 1)
            sp.wait_ge(scan_abs, 3 * SCANS)
            load_attn(0)
            sp.dma_start(A_attn[0:4 * RANK, :], lora_A_h[0:4].rearrange("w r h -> (w r) h")
                         ).then_inc(fold_loaded, 16)
            for j in range(4):
                sp.dma_start(B_attn_raw[:, j, :, :],
                             lora_B_attn[:, j * P:(j + 1) * P, :].rearrange("w p r -> p w r")
                             ).then_inc(fold_loaded, 16)
            load_ffn(6, 0)
            load_ffn(7, 1)
            with sp.Fori(2, 5) as i:
                load_ffn(2 * i + 4, 0)
                load_ffn(2 * i + 5, 1)
                load_attn(i - 1)
            load_nf4(0, 0)
            load_nf4(1, 1)
            sp.wait_ge(nf4_sum, 2 * RAMPS)
            for m in range(2):
                for copy in range(4):
                    sp.dma_start(A_gu_raw[64 * m + 16 * copy:64 * m + 16 * copy + 16, :], lora_A_h[4 + m]
                                 ).then_inc(lora_loaded, 16)
                sp.dma_start(B_gu_raw[:, :, m, :], lora_B_gu[m].rearrange("(c p) r -> p c r", p=P)
                             ).then_inc(lora_loaded, 16)
            for copy in range(4):
                sp.dma_start(A_down_raw[16 * copy:16 * copy + 16, :], lora_A_down).then_inc(lora_loaded, 16)
            sp.dma_start(B_down_raw, lora_B_down.rearrange("(j p) r -> p j r", p=P)).then_inc(lora_loaded, 16)
            load_nf4(2, 0)
            load_nf4(3, 1)
            sp.wait_ge(oT_tr, 4)
            sp.wait_ge(lora_qkv, 4)
            for n in range(2):
                sp.dma_start(x1[:, 4 * n:4 * n + 4, :], x_v[:, 4 * n:4 * n + 4, :]).then_inc(x_again[n], 16)
            with sp.Fori(1, 6) as i:
                load_nf4(2 * i + 2, 0)
                load_nf4(2 * i + 3, 1)
            sp.wait_ge(nf4_sum, RAMPS * CHUNKS)
            sp.wait_ge(nf4_weight, CHUNKS)
            for n in range(2):
                for which, dst in enumerate((raw, base)):
                    t = 4 * n + 2 * which
                    sp.dma_start(dst[:, n, 0:2 * HID].rearrange("p (t h) -> p t h", t=2), x_v[:, t:t + 2, :]
                                 ).then_inc(x_last, 16)
            for t in range(TT):
                sp.wait_ge(out_ready, t + 1)
                sp.dma_start(out_v[:, t, :], y[:, t, :]).then_inc(out_stored, 16)
            sp.wait_ge(out_stored, 16 * TT)

        def last_x(t):
            buf = (raw, base)[(t % 4) // 2]
            return buf[:, t // 4, (t % 2) * HID:(t % 2 + 1) * HID]

        @block.gpsimd
        def _(pool):
            nc.gpsimd.memset(ident[:], 0.0).then_inc(const_ready, 1)
            nc.gpsimd.memset(ones[:], 1.0).then_inc(const_ready, 1)
            pool.wait_ge(const_ready, 2)
            nc.gpsimd.affine_select(out=ident[:], in_=ident[:], compare_op=ALU.not_equal, fill=1.0, base=0,
                                    pattern=[[-1, P]], channel_multiplier=1).then_inc(const_ready, 1)
            nc.gpsimd.memset(A_gu[:, :, :].bitcast(f32), 0.0).then_inc(lora_zero, 1)
            nc.gpsimd.memset(B_downT[:, :].bitcast(f32), 0.0).then_inc(lora_zero, 1)
            def counted(semaphore, count):
                pool.wait_ge(semaphore, count)
                pool.sem_inc(gpsimd_passed, 1)

            def ffn_diff_at(i, par):
                counted(chunk_loaded[par], 96 * i - 96)
                nc.gpsimd.tensor_tensor(raw[:, par, :], raw[:, par, :], base[:, par, :], ALU.subtract
                                        ).then_inc(diff_ready, 1)

            def nf4_scale(k, par):
                counted(nf4_sum, RAMPS * k + RAMPS)
                counted(tr_done, 3 * (CHUNKS + k) - 3)
                nc.gpsimd.tensor_tensor(
                    weight[:, par, :].rearrange("p (b n) -> p b n", n=BLOCK),
                    base[:, par, :].rearrange("p (b n) -> p b n", n=BLOCK),
                    scale_trio[:, ds(k, 1), :].rearrange("p a b -> p (a b)").unsqueeze(2).to_broadcast([P, 24, BLOCK]),
                    ALU.mult).then_inc(nf4_weight, 1)

            def A_down_chunk(k, par):
                counted(tr_done, 3 * (CHUNKS + k) - 3)
                nc.gpsimd.tensor_copy(A_down_now[:, par, :], A_down[:, ds(k * P, P)].bitcast(f32)
                                      ).then_inc(A_down_ready, 1)

            def attn_begin(m):
                counted(attn_loaded, 16 * m + 16)
                counted(attn_scaled, 5 * m + 1)
                nc.gpsimd.tensor_scalar(attn_sum[:, :, :], attn_codes[:, :, :].bitcast(i32), -1.0, NF4_OFFSET,
                                        ALU.mult, ALU.add).then_inc(attn_start, 1)

            def attn_scale(dst, m, w0, w1_):
                n = (w1_ - w0) * HID // BLOCK
                nc.gpsimd.tensor_tensor(
                    dst.rearrange("p w (b n) -> p (w b) n", n=BLOCK),
                    attn_sum[:, w0:w1_, :].rearrange("p w (b n) -> p (w b) n", n=BLOCK),
                    scale_attn[:, ds(m, 1), w0:w1_, :].rearrange("p a w b -> p (a w b)").unsqueeze(2)
                    .to_broadcast([P, n, BLOCK]), ALU.mult).then_inc(attn_scaled, 1)

            def attn_finish(m, half):
                counted(attn_acc, 2 + 2 * RAMPS * m + RAMPS * (half + 1))
                if half == 0:
                    attn_scale(attn_sum[:, 0:2, :], m, 0, 2)
                    counted(attn_scaled, 5 * m + 2)
                    nc.gpsimd.tensor_tensor(w_qkv[:, ds(m, 1), :], attn_sum[:, 0:1, :], attn_sum[:, 1:2, :],
                                            ALU.add).then_inc(attn_scaled, 1)
                else:
                    attn_scale(attn_sum[:, 2:3, :], m, 2, 3)
                    attn_scale(w_o[:, ds(m, 1), :], m, 3, 4)
                    counted(attn_scaled, 5 * m + 5)
                    nc.gpsimd.tensor_tensor(w_qkv[:, ds(m, 1), :], w_qkv[:, ds(m, 1), :], attn_sum[:, 2:3, :],
                                            ALU.add).then_inc(attn_scaled, 1)

            def make_nf4(k):
                for par in range(2):
                    nf4_scale(k + par, par)
                    A_down_chunk(k + par, par)

            for n in range(FIRST_UNITS):
                pool.wait_ge(first_loaded[n % SECTIONS], 32 * (n // SECTIONS) + 32)
                nc.gpsimd.tensor_tensor(raw_s[:, n % SECTIONS, :], raw_s[:, n % SECTIONS, :],
                                        base_s[:, n % SECTIONS, :], ALU.subtract).then_inc(diff_ready, 1)
                if n == 0:
                    for k in range(POOL_TILES):
                        pool.wait_ge(scan_loaded[k], 32)
                        nc.gpsimd.tensor_tensor(scan[:, k, 0, :], scan[:, k, 0, :], scan[:, k, 1, :], ALU.subtract
                                                ).then_inc(scan_diff_pool, 1)
            ffn_diff_at(2, 0)
            ffn_diff_at(2, 1)
            pool.wait_ge(scales_loaded, 16 * (2 + 4 + 1))
            nc.gpsimd.tensor_scalar(scale_trio[:, :, 0:16], scale_raw[:, :, :, :].rearrange("p c m b -> p c (m b)"),
                                    -NF4_STEP, 0.0, ALU.mult, ALU.add).then_inc(scales_ready, 1)
            for q in range(HC):
                nc.gpsimd.tensor_scalar(scale_trio[:, :, 16 + 2 * q:18 + 2 * q],
                                        scale_down_raw[:, q, :].rearrange("p (c b) -> p c b", b=2),
                                        -NF4_STEP, 0.0, ALU.mult, ALU.add).then_inc(scales_ready, 1)
            nc.gpsimd.tensor_scalar(scale_attn[:, :, 0:3, :], scale_attn_raw[:, :, 0:3, :],
                                    -NF4_STEP / 3.0, 0.0, ALU.mult, ALU.add).then_inc(scales_ready, 1)
            nc.gpsimd.tensor_scalar(scale_attn[:, :, 3, :], scale_attn_raw[:, :, 3, :],
                                    -NF4_STEP, 0.0, ALU.mult, ALU.add).then_inc(scales_ready, 1)
            pool.wait_ge(scales_ready, 3 + HC)
            nc.gpsimd.memset(ln[:, 4, 0:1], 0.0).then_inc(attn_scaled, 1)

            ffn_diff_at(3, 0)
            ffn_diff_at(3, 1)
            pool.wait_ge(y_done, TT)
            with pool.Fori(2, 5) as i:
                attn_begin(i - 2)
                ffn_diff_at(i + 2, 0)
                attn_finish(i - 2, 0)
                ffn_diff_at(i + 2, 1)
                attn_finish(i - 2, 1)
            attn_begin(3)
            attn_finish(3, 0)
            attn_finish(3, 1)
            pool.wait_ge(scan_abs, 3 * SCANS)
            nc.gpsimd.memset(x1[:, 4, :], 0.0).then_inc(B_nat_ready, 1)
            pool.wait_ge(fold_loaded, 16 * 5)
            pool.wait_ge(B_nat_ready, 1)
            nc.gpsimd.tensor_copy(B_qkv_nat[:, :, 0:48].rearrange("p j (w r) -> p j w r", w=3),
                                  B_attn_raw[:, :, 0:3, :]).then_inc(B_nat_ready, 1)
            nc.gpsimd.tensor_copy(B_o_nat[:, :, 48:64], B_attn_raw[:, :, 3, :]).then_inc(B_nat_ready, 1)
            for par in range(2):
                nf4_scale(par, par)

            pool.wait_ge(lora_loaded, 16 * 15)
            for n in range(2):
                for s in (1, 3):
                    pool.wait_ge(lora_hi, 2 + 2 * n + 2)
                    nc.gpsimd.tensor_tensor(B_gu_nat[n][:, :, :, s, :],
                                            B_gu_raw[:, n * HALF_CHUNKS:(n + 1) * HALF_CHUNKS, :, :],
                                            B_gu_nat[n][:, :, :, 0, :], ALU.subtract).then_inc(lora_lo, 1)
            for s in (1, 3):
                pool.wait_ge(lora_hi, 8)
                nc.gpsimd.tensor_tensor(B_down_nat[:, :, s, :], B_down_raw, B_down_nat[:, :, 0, :],
                                        ALU.subtract).then_inc(lora_lo, 1)
            pool.wait_ge(A_low, 3)
            pool.wait_ge(lora_zero, 3)
            A_down_chunk(0, 0)
            A_down_chunk(1, 1)
            with pool.Fori(0, PAIRS - 1) as i:
                make_nf4(2 * i + 2)
            for t in range(TT):
                pool.wait_ge(x_last, 16 * 4)
                pool.wait_ge(gated, t + 1)
                nc.gpsimd.tensor_tensor(y[:, t, :], y[:, t, :], last_x(t), ALU.add).then_inc(out_ready, 1)

        @block.scalar
        def _(act):
            act.wait_ge(ln_step, TT + 1)
            nc.scalar.activation(ln[:, 1, :], ln[:, 0, :], ACT.Sqrt).then_inc(root_done, 1)
            nc.scalar.activation(stats[:, 0, :], ln[:, 0, 0:6], ACT.Silu)

            def x_high(t):
                act.wait_ge(xT_tr, t + 1)
                nc.scalar.activation(xT[:, HI, :, t * P:(t + 1) * P],
                                     xT_ps[t].rearrange("p (c t) -> p c t", c=HC), ACT.Copy
                                     ).then_inc(xT_hi, 1)

            def scan_sum(k):
                m, part = k // SCANS, k % SCANS
                if k < POOL_TILES:
                    act.wait_ge(scan_diff_pool, k + 1)
                else:
                    act.wait_ge(scan_diff, k - POOL_TILES + 1)
                nc.scalar.activation(scan[:, k % SCAN_SLOTS, 0, :], scan[:, k % SCAN_SLOTS, 0, :], ACT.Abs,
                                     accum_out=abs_sums[:, SUMS * m + part:SUMS * m + part + 1]).then_inc(scan_abs, 1)

            def first_sum(n):
                column = SUMS * (n // FIRST) + SCANS + n % FIRST
                act.wait_ge(diff_ready, n + 1)
                if n > 0:
                    act.wait_ge(first_abs, n)
                nc.scalar.activation(abs_out, raw_s[:, n % SECTIONS, :], ACT.Abs,
                                     accum_out=abs_sums[:, column:column + 1]).then_inc(first_abs, 1)

            def first_sign(n):
                nc.scalar.activation(raw_s[:, n % SECTIONS, :], raw_s[:, n % SECTIONS, :], ACT.Sign
                                     ).then_inc(sign_ready, 1)

            def first_high(n):
                act.wait_ge(tr_done, n + 1)
                nc.scalar.activation(first_w(n)[:, HI, :], tr_ps[:, n % 2, :], ACT.Copy).then_inc(w_hi, 1)

            def early_high():
                act.wait_ge(tr_done, 1)
                nc.scalar.activation(signT[:, :], sum_ps[:, 1, :], ACT.Copy).then_inc(sign_T, 1)
                nc.scalar.activation(first_w(0)[:, HI, :], sum_ps[:, 0, :], ACT.Copy).then_inc(w_hi, 1)

            def first_silu(c, th):
                if c == 0:
                    act.wait_ge(early_gate, th + 1)
                else:
                    act.wait_ge(gate_done, 2 * c + th + 1)
                nc.scalar.activation(silu_first[c][:, th * HALF:(th + 1) * HALF], gate_ps[:, th, :], ACT.Silu
                                     ).then_inc(silu_done, 1)

            def first_h_high(c, th):
                act.wait_ge(h_done, 2 * c + th + 1)
                nc.scalar.activation(first_h(c, HI, 4 * th, 4 * th + 4),
                                     up_ps[:, th, :].rearrange("p (t n) -> p t n", n=P), ACT.Copy).then_inc(h_hi, 1)

            def ffn_sign(c, par):
                act.wait_ge(diff_ready, FIRST_UNITS + c - FIRST + 1)
                nc.scalar.activation(raw[:, par, :], raw[:, par, :], ACT.Sign).then_inc(sign_ready, 1)

            def w_high(block_no, c, par, kind):
                act.wait_ge(tr_done, unit_index(block_no, c, kind) + 1)
                dst = downT[:, par, HI, :] if kind == DOWN else guT[:, par, kind, HI, :]
                nc.scalar.activation(dst, tr_ps[:, (3 * par + kind) % 2, :], ACT.Copy
                                     ).then_inc(w_hi, 1)

            def silu(n, th):
                act.wait_ge(gate_done, 2 * n + th + 1)
                act.wait_ge(h_done, 2 * n + th - 1)
                nc.scalar.activation(silu_gate[:, th * HALF:(th + 1) * HALF], gate_ps[:, th, :], ACT.Silu
                                     ).then_inc(silu_done, 1)

            def h_high(n, par, th):
                act.wait_ge(h_done, 2 * n + th + 1)
                sl = slice(th * HALF, (th + 1) * HALF)
                nc.scalar.activation(h_split[:, par, HI, sl], up_ps[:, th, :], ACT.Copy).then_inc(h_hi, 1)

            def nf4_begin(k, par):
                act.wait_ge(chunk_loaded[par], 96 * (PAIRS - 2) + 16 * (k - par) + 32)
                if isinstance(k, int) and k < 2:
                    act.wait_ge(ffn_weight, 3 * (CHUNKS - 2 + k) + 3)
                else:
                    act.wait_ge(nf4_weight, k - 1)
                nc.scalar.activation(base[:, par, :], raw[:, par, :].bitcast(i32), ACT.Copy, bias=NF4_OFFSET,
                                     scale=-1.0)

            def nf4_ramp_step(k, step):
                par, j = step // RAMPS, step % RAMPS
                slope, start, _ = NF4_RAMPS[j]
                r = RAMPS * k + step
                if not (isinstance(k, int) and r < 2):
                    act.wait_ge(nf4_sum, r - 1)
                nc.scalar.activation(ramp[:, (step % 2) * TRIO:(step % 2 + 1) * TRIO],
                                     raw[:, par, :].bitcast(i32), ACT.Relu, bias=ramp_bias[:, j:j + 1], scale=slope
                                     ).then_inc(nf4_ramp, 1)

            def attn_ramp_step(m, step):
                half, j = step // RAMPS, step % RAMPS
                slope, start, _ = NF4_RAMPS[j]
                if step == 0:
                    act.wait_ge(attn_start, m + 1)
                act.wait_ge(attn_acc, 2 * RAMPS * m + step + 1)
                nc.scalar.activation(ramp[:, (step % 2) * TRIO:(step % 2) * TRIO + 2 * HID],
                                     attn_codes[:, 2 * half:2 * half + 2, :].bitcast(i32).rearrange("p w h -> p (w h)"),
                                     ACT.Relu, bias=ramp_bias[:, j:j + 1], scale=slope).then_inc(attn_ramp, 1)

            def make(step, i, make_ffn, attn, make_nf4):
                if make_ffn and step == 6:
                    ffn_sign(2 * i + 4, 0)
                if attn is not None:
                    attn_ramp_step(attn, step)
                if make_nf4 is not None:
                    nf4_ramp_step(2 * make_nf4, step)

            def ffn_iteration(i, make_ffn=False, attn=None, begin_nf4=None):
                n, a, b = 2 * i, 2 * i, 2 * i + 1
                bg = (i, make_ffn, attn, None)
                w_high(0, a, 0, DOWN)
                make(0, *bg)
                make(1, *bg)
                silu(n, 0)
                w_high(0, b, 1, GATE)
                make(2, *bg)
                silu(n, 1)
                w_high(0, b, 1, UP)
                make(3, *bg)
                make(4, *bg)
                h_high(n, 0, 0)
                w_high(0, b, 1, DOWN)
                h_high(n, 0, 1)
                make(5, *bg)
                silu(n + 1, 0)
                make(6, *bg)
                silu(n + 1, 1)
                make(7, *bg)
                h_high(n + 1, 1, 0)
                make(8, *bg)
                h_high(n + 1, 1, 1)
                make(9, *bg)
                w_high(0, a + 2, 0, GATE)
                if begin_nf4 is not None:
                    nf4_begin(begin_nf4, 0)
                if make_ffn:
                    ffn_sign(b + 4, 1)
                w_high(0, a + 2, 0, UP)

            def iteration(block_no, i, make_nf4=None, begin_nf4=None, last=False):
                n, a, b = CHUNKS * block_no + 2 * i, 2 * i, 2 * i + 1
                bg = (i, False, None, make_nf4)
                if make_nf4 is not None:
                    make(0, *bg)
                w_high(block_no, a, 0, DOWN)
                make(1, *bg)
                make(2, *bg)
                silu(n, 0)
                w_high(block_no, b, 1, GATE)
                make(3, *bg)
                silu(n, 1)
                w_high(block_no, b, 1, UP)
                make(4, *bg)
                if make_nf4 is not None:
                    nf4_begin(2 * make_nf4 + 1, 1)
                h_high(n, 0, 0)
                w_high(block_no, b, 1, DOWN)
                make(5, *bg)
                h_high(n, 0, 1)
                make(6, *bg)
                make(7, *bg)
                silu(n + 1, 0)
                make(8, *bg)
                silu(n + 1, 1)
                h_high(n + 1, 1, 0)
                make(9, *bg)
                h_high(n + 1, 1, 1)
                if not last:
                    w_high(block_no, a + 2, 0, GATE)
                if begin_nf4 is not None:
                    nf4_begin(begin_nf4, 0)
                if not last:
                    w_high(block_no, a + 2, 0, UP)

            first_sum(0)
            first_sign(0)
            for t in range(4):
                x_high(t)
            early_high()
            x_high(4)
            x_high(5)
            scan_sum(0)
            x_high(6)
            x_high(7)
            scan_sum(1)
            first_sum(1)
            first_sign(1)
            scan_sum(2)
            scan_sum(3)
            first_sum(2)
            first_sum(3)
            first_sign(2)
            first_sign(3)
            first_high(1)
            first_silu(0, 0)
            first_high(2)
            first_silu(0, 1)
            scan_sum(4)
            first_sum(4)
            first_silu(1, 0)
            scan_sum(5)
            first_sum(5)
            first_silu(1, 1)
            first_sign(4)
            first_high(3)
            first_sign(5)
            scan_sum(6)
            scan_sum(7)
            first_silu(2, 0)
            first_sum(6)
            first_sum(7)
            first_silu(2, 1)
            first_sign(6)
            first_sign(7)
            scan_sum(8)
            first_silu(3, 0)
            first_high(4)
            first_silu(3, 1)
            first_high(5)
            scan_sum(9)
            first_sum(8)
            first_h_high(0, 0)
            first_sum(9)
            scan_sum(10)
            first_h_high(0, 1)
            first_high(6)
            scan_sum(11)
            first_h_high(1, 0)
            first_sum(10)
            first_sum(11)
            first_h_high(1, 1)
            first_sign(8)
            first_high(7)
            first_sign(9)
            first_h_high(2, 0)
            first_sign(10)
            first_h_high(2, 1)
            first_sign(11)
            first_high(8)
            first_high(9)
            first_h_high(3, 0)
            first_high(10)
            first_high(11)
            first_h_high(3, 1)
            ffn_sign(4, 0)
            ffn_sign(5, 1)
            w_high(0, 4, 0, GATE)
            w_high(0, 4, 0, UP)
            ffn_sign(6, 0)
            ffn_sign(7, 1)
            with act.Fori(2, 5) as i:
                ffn_iteration(i, make_ffn=True, attn=i - 2)
            ffn_iteration(5, attn=3, begin_nf4=0)
            act.wait_ge(attn_acc, 2 + 8 * RAMPS)
            iteration(0, 6, make_nf4=0, last=True)

            act.wait_ge(B_tr, 2)
            nc.scalar.activation(B_qkvT[0:64, :], tr_ps[0:64, 0, :], ACT.Copy, scale=1.0 / 3.0).then_inc(B_T_ready, 1)
            nc.scalar.activation(B_oT[0:64, :], tr_ps[0:64, 1, :], ACT.Copy).then_inc(B_T_ready, 1)
            act.wait_ge(down_done, TT * GROUPS)
            for m in range(4):
                act.wait_ge(qkv_full, m + 1)
                nc.scalar.activation(qkv_split[:, m, HI, :], w_qkv[:, m, :], ACT.Copy).then_inc(qkv_hi, 1)

            def oT_high(m):
                act.wait_ge(oT_tr, m + 1)
                nc.scalar.activation(oT_split[:, HI, :, m * P:(m + 1) * P],
                                     fold_ps[m].rearrange("p (c o) -> p c o", c=4), ACT.Copy).then_inc(oT_hi, 1)

            oT_high(0)
            oT_high(1)
            act.wait_ge(lora_loaded, 16 * 15)
            act.wait_ge(lora_zero, 2)
            for m in range(2):
                rows = slice(64 * m, 64 * m + 64)
                nc.scalar.activation(A_gu[rows, m, :], A_gu_raw[rows, :], ACT.Copy).then_inc(lora_hi, 1)
            act.wait_ge(h_done, 4 * PAIRS)
            for n in range(2):
                for s in (0, 2):
                    nc.scalar.activation(B_gu_nat[n][:, :, :, s, :].bitcast(f32r),
                                         B_gu_raw[:, n * HALF_CHUNKS:(n + 1) * HALF_CHUNKS, :, :], ACT.Copy
                                         ).then_inc(lora_hi, 1)
            oT_high(2)
            oT_high(3)
            for s in (0, 2):
                nc.scalar.activation(B_down_nat[:, :, s, :].bitcast(f32r), B_down_raw, ACT.Copy).then_inc(lora_hi, 1)
            act.wait_ge(qkv_lo, 4)
            for n in range(5):
                act.wait_ge(lora_tr, n + 1)
                if n < 4:
                    w = min(4, CHUNKS - 4 * n) * P
                    nc.scalar.activation(B_guT[:, 4 * n * P:4 * n * P + w], tr_ps[:, n % 2, 0:w], ACT.Copy
                                         ).then_inc(lora_T, 1)
                else:
                    nc.scalar.activation(B_downT[0:64, :], tr_ps[0:64, n % 2, :], ACT.Copy).then_inc(lora_T, 1)
            nc.scalar.activation(A_down[0:64, :], A_down_raw[0:64, :], ACT.Copy).then_inc(lora_hi, 1)
            for c in range(HC):
                act.wait_ge(MT_done, c + 1)
                nc.scalar.activation(MT[:, HI, c, :], four_ps[c], ACT.Copy).then_inc(MT_hi, 1)
            for kind in (GATE, UP):
                w_high(1, 0, 0, kind)
            act.wait_ge(y_done, TT * GROUPS)
            for t in range(TT):
                nc.scalar.activation(y[:, t, :], y[:, t, :], ACT.Silu).then_inc(ffn_silu, 1)
                act.wait_ge(x1_tr, t + 1)
                nc.scalar.activation(xT[:, HI, :, t * P:(t + 1) * P],
                                     tr_ps[:, t % 2, :].rearrange("p (c t) -> p c t", c=HC), ACT.Copy
                                     ).then_inc(x1_hi, 1)
            nf4_begin(2, 0)
            with act.Fori(0, 5) as i:
                iteration(1, i, make_nf4=i + 1, begin_nf4=2 * i + 4)
            iteration(1, 5, make_nf4=6)
            iteration(1, 6, last=True)

        @block.vector
        def _(dve):
            for j, (_, start, _) in enumerate(NF4_RAMPS):
                nc.vector.memset(ramp_bias[:, j:j + 1], start)
            for t in range(TT):
                dve.wait_ge(x_loaded[t // 4], 16)
                nc.vector.bn_stats(stats[:, t, :], y[:, t, :]).then_inc(ln_step, 1)
            dve.wait_ge(ln_step, TT)
            for t in range(TT):
                last = nc.vector.bn_aggr(moments[:, t, :], stats[:, t, :])
            last.then_inc(xn_ready, 1)
            dve.wait_ge(xn_ready, 1)
            nc.vector.tensor_scalar(ln[:, 0, :], moments[:, :, 1], EPS, None, ALU.add).then_inc(ln_step, 1)
            dve.wait_ge(root_done, 1)
            nc.vector.reciprocal(ln[:, 2, :], ln[:, 1, :]).then_inc(xn_ready, 1)
            dve.wait_ge(xn_ready, 2)
            nc.vector.tensor_tensor(ln[:, 2, :], ln[:, 2, :], ln[:, 0, :], ALU.mult).then_inc(xn_ready, 1)
            dve.wait_ge(xn_ready, 3)
            nc.vector.tensor_tensor(ln[:, 2, :], ln[:, 2, :], ln[:, 1, :], ALU.add).then_inc(xn_ready, 1)
            dve.wait_ge(xn_ready, 4)
            nc.vector.tensor_scalar(ln[:, 3, :], ln[:, 2, :], 0.5, None, ALU.mult).then_inc(xn_ready, 1)
            dve.wait_ge(xn_ready, 5)
            nc.vector.reciprocal(inv_std[:, :], ln[:, 3, :]).then_inc(xn_ready, 1)
            dve.wait_ge(xn_ready, 6)

            def normalise(buf, t, done):
                nc.vector.tensor_scalar(buf[:, t, :], buf[:, t, :], moments[:, t, 0:1], inv_std[:, t:t + 1],
                                        ALU.subtract, ALU.mult).then_inc(done, 1)

            def scan_subtract(k):
                dve.wait_ge(scan_loaded[k % SCAN_SLOTS], 32 * (k // SCAN_SLOTS) + 32)
                nc.vector.tensor_tensor(scan[:, k % SCAN_SLOTS, 0, :], scan[:, k % SCAN_SLOTS, 0, :],
                                        scan[:, k % SCAN_SLOTS, 1, :], ALU.subtract).then_inc(scan_diff, 1)

            for t in range(TT):
                normalise(y, t, xn_ready)

            def x_low(t):
                dve.wait_ge(xT_hi, t + 1)
                nc.vector.tensor_tensor(xT[:, LO, :, t * P:(t + 1) * P],
                                        xT_ps[t].rearrange("p (c t) -> p c t", c=HC),
                                        xT[:, HI, :, t * P:(t + 1) * P].bitcast(f32), ALU.subtract
                                        ).then_inc(xT_lo, 1)

            def take_coeff(m):
                dve.wait_ge(scan_abs, SCANS * (m + 1))
                dve.wait_ge(first_abs, FIRST * (m + 1))
                nc.vector.tensor_reduce(abs_part[:, m:m + 1], abs_sums[:, SUMS * m:SUMS * (m + 1)],
                                        axis=AX.X, op=ALU.add).then_inc(part_ready, 1)
                dve.wait_ge(total_ready, m + 1)
                nc.vector.tensor_scalar(coeff[:, m:m + 1], sum_ps[:, 0, m:m + 1], 1.0 / (INTER * HID), None, ALU.mult
                                        ).then_inc(coeff_ready, 1)
                dve.wait_ge(coeff_ready, m + 1)

            def first_make(n):
                kind, k = n // FIRST, n % SECTIONS
                dve.wait_ge(sign_ready, n + 1)
                if n >= SECTIONS:
                    dve.wait_ge(tr_done, n - SECTIONS + 1)
                nc.vector.scalar_tensor_tensor(weight_s[:, k, :], raw_s[:, k, :], coeff[:, kind:kind + 1],
                                               base_s[:, k, :], ALU.mult, ALU.add).then_inc(ffn_weight, 1)

            def early_low():
                dve.wait_ge(w_hi, 1)
                nc.vector.tensor_tensor(first_w(0)[:, LO, :], sum_ps[:, 0, :], first_w(0)[:, HI, :].bitcast(f32),
                                        ALU.subtract).then_inc(w_lo, 1)
                nc.vector.memset(ln[:, 2, 2:3], 0.0).then_inc(ffn_weight, 1)

            def early_sum(th):
                dve.wait_ge(gate_done, th + 1)
                part = silu_first[0][:, th * HALF:(th + 1) * HALF]
                nc.vector.tensor_scalar(part, up_ps[:, th, :], coeff[:, GATE:GATE + 1], None, ALU.mult
                                        ).then_inc(early_part, 1)
                dve.wait_ge(early_part, th + 1)
                nc.vector.tensor_tensor(gate_ps[:, th, :], gate_ps[:, th, :], part, ALU.add).then_inc(early_gate, 1)

            def first_low(n):
                dve.wait_ge(w_hi, n + 1)
                nc.vector.tensor_tensor(first_w(n)[:, LO, :], tr_ps[:, n % 2, :], first_w(n)[:, HI, :].bitcast(f32),
                                        ALU.subtract).then_inc(w_lo, 1)

            def first_h_make(c, th):
                dve.wait_ge(silu_done, 2 * FIRST)
                dve.wait_ge(up_done, 2 * c + th + 1)
                nc.vector.tensor_tensor(up_ps[:, th, :], silu_first[c][:, th * HALF:(th + 1) * HALF], up_ps[:, th, :],
                                        ALU.mult).then_inc(h_done, 1)

            def first_h_low(c, th):
                dve.wait_ge(h_hi, 2 * c + th + 1)
                nc.vector.tensor_tensor(first_h(c, LO, 4 * th, 4 * th + 4),
                                        up_ps[:, th, :].rearrange("p (t n) -> p t n", n=P),
                                        first_h(c, HI, 4 * th, 4 * th + 4).bitcast(f32), ALU.subtract
                                        ).then_inc(h_lo, 1)

            def ffn_make(c, par, kind):
                dve.wait_ge(sign_ready, FIRST_UNITS + c - FIRST + 1)
                dve.wait_ge(tr_done, 3 * c - 3)
                sl = slice(kind * HID, (kind + 1) * HID)
                nc.vector.scalar_tensor_tensor(weight[:, par, sl], raw[:, par, sl], coeff[:, kind:kind + 1],
                                               base[:, par, sl], ALU.mult, ALU.add).then_inc(ffn_weight, 1)

            def w_low(block_no, c, par, kind):
                dve.wait_ge(w_hi, unit_index(block_no, c, kind) + 1)
                buf = downT[:, par] if kind == DOWN else guT[:, par, kind]
                nc.vector.tensor_tensor(buf[:, LO, :], tr_ps[:, (3 * par + kind) % 2, :],
                                        buf[:, HI, :].bitcast(f32), ALU.subtract).then_inc(w_lo, 1)

            def h_make(n, th):
                dve.wait_ge(silu_done, 2 * n + th + 1)
                dve.wait_ge(up_done, 2 * n + th + 1)
                nc.vector.tensor_tensor(up_ps[:, th, :], silu_gate[:, th * HALF:(th + 1) * HALF], up_ps[:, th, :],
                                        ALU.mult).then_inc(h_done, 1)

            def h_low(n, par, th):
                dve.wait_ge(h_hi, 2 * n + th + 1)
                sl = slice(th * HALF, (th + 1) * HALF)
                nc.vector.tensor_tensor(h_split[:, par, LO, sl], up_ps[:, th, :],
                                        h_split[:, par, HI, sl].bitcast(f32), ALU.subtract).then_inc(h_lo, 1)

            def nf4_add(k, step):
                par, j = step // RAMPS, step % RAMPS
                r = RAMPS * k + step
                dve.wait_ge(nf4_ramp, r + 1)
                if not (isinstance(k, int) and r < 1):
                    dve.wait_ge(nf4_sum, r)
                nc.vector.scalar_tensor_tensor(base[:, par, :], ramp[:, (step % 2) * TRIO:(step % 2 + 1) * TRIO],
                                               NF4_RAMPS[j][2], base[:, par, :], ALU.min, ALU.add
                                               ).then_inc(nf4_sum, 1)

            def attn_add(m, step):
                half, j = step // RAMPS, step % RAMPS
                dve.wait_ge(attn_ramp, 2 * RAMPS * m + step + 1)
                dve.wait_ge(attn_acc, 2 * RAMPS * m + step + 2)
                dst = attn_sum[:, 2 * half:2 * half + 2, :].rearrange("p w h -> p (w h)")
                nc.vector.scalar_tensor_tensor(dst, ramp[:, (step % 2) * TRIO:(step % 2) * TRIO + 2 * HID],
                                               NF4_RAMPS[j][2], dst, ALU.min, ALU.add).then_inc(attn_acc, 1)

            def y_add(block_no, i, t, last=False):
                done = TT * (PAIRS * block_no + i - 1) + t
                dve.wait_ge(down_done, done + 1)
                if block_no == 0:
                    dve.wait_ge(y_done, done - TT + 1)
                    nc.vector.tensor_tensor(y[:, t, :], y[:, t, :], down_ps[t], ALU.add).then_inc(y_done, 1)
                else:
                    if isinstance(i, int) and i == 0:
                        dve.wait_ge(x1_ready, t + 1)
                    else:
                        dve.wait_ge(y_done, done - TT + 1)
                    nc.vector.tensor_tensor(x1[:, t, :], x1[:, t, :], down_ps[t], ALU.add
                                            ).then_inc(y_done, 1)
                    if last:
                        dve.wait_ge(y_done, done + 1)
                        if t == 0:
                            dve.wait_ge(ffn_silu, TT)
                        nc.vector.tensor_tensor(y[:, t, :], x1[:, t, :], y[:, t, :], ALU.mult).then_inc(gated, 1)

            def make(step, i, make_ffn, attn, make_nf4):
                if make_ffn and step % RAMPS == 0:
                    for kind in (GATE, UP, DOWN):
                        ffn_make(2 * i + 2 + step // RAMPS, step // RAMPS, kind)
                if attn is not None:
                    attn_add(attn, step)
                if make_nf4 is not None:
                    nf4_add(2 * make_nf4, step)

            def ffn_iteration(i, make_ffn=False, attn=None):
                n, a, b = 2 * i, 2 * i, 2 * i + 1
                bg = (i, make_ffn, attn, None)
                w_low(0, a, 0, DOWN)
                make(0, *bg)
                make(1, *bg)
                w_low(0, b, 1, GATE)
                make(2, *bg)
                w_low(0, b, 1, UP)
                make(3, *bg)
                h_make(n, 0)
                make(4, *bg)
                w_low(0, b, 1, DOWN)
                h_low(n, 0, 0)
                h_make(n, 1)
                h_low(n, 0, 1)
                make(5, *bg)
                make(6, *bg)
                h_make(n + 1, 0)
                h_low(n + 1, 1, 0)
                make(7, *bg)
                h_make(n + 1, 1)
                for t in range(TT):
                    y_add(0, i, t)
                    if t == 0:
                        h_low(n + 1, 1, 1)
                    if t == 1:
                        make(8, *bg)
                    if t == 2:
                        make(9, *bg)
                    if t == 3:
                        w_low(0, a + 2, 0, GATE)
                    if t == 5:
                        w_low(0, a + 2, 0, UP)

            def iteration(block_no, i, make_nf4=None, last=False):
                n, a, b = CHUNKS * block_no + 2 * i, 2 * i, 2 * i + 1
                bg = (i, False, None, make_nf4)
                if make_nf4 is not None:
                    make(0, *bg)
                w_low(block_no, a, 0, DOWN)
                make(1, *bg)
                w_low(block_no, b, 1, GATE)
                make(2, *bg)
                make(3, *bg)
                w_low(block_no, b, 1, UP)
                make(4, *bg)
                h_make(n, 0)
                w_low(block_no, b, 1, DOWN)
                h_low(n, 0, 0)
                h_make(n, 1)
                make(5, *bg)
                h_low(n, 0, 1)
                make(6, *bg)
                make(7, *bg)
                h_make(n + 1, 0)
                h_low(n + 1, 1, 0)
                make(8, *bg)
                h_make(n + 1, 1)
                for t in range(TT):
                    y_add(block_no, i, t, last=last and block_no == 1)
                    if t == 0:
                        h_low(n + 1, 1, 1)
                    if t == 1:
                        make(9, *bg)
                    if t == 3 and not last:
                        w_low(block_no, a + 2, 0, GATE)
                    if t == 5 and not last:
                        w_low(block_no, a + 2, 0, UP)
                    if t == 5 and last and block_no == 0:
                        dve.wait_ge(attn_scaled, 5 * 4 + 1)
                        for m in range(4):
                            dve.wait_ge(lora_qkv, m + 1)
                            nc.vector.tensor_tensor(w_qkv[:, m, :], w_qkv[:, m, :], fold_ps[m], ALU.add
                                                    ).then_inc(qkv_full, 1)

            for t in range(4):
                x_low(t)
            early_low()
            for t in range(4, TT):
                x_low(t)
            scan_subtract(2)
            scan_subtract(3)
            take_coeff(GATE)
            first_make(1)
            early_sum(0)
            first_make(2)
            first_low(1)
            early_sum(1)
            first_low(2)
            first_make(3)
            scan_subtract(4)
            scan_subtract(5)
            scan_subtract(6)
            scan_subtract(7)
            first_low(3)
            take_coeff(UP)
            first_make(4)
            first_make(5)
            scan_subtract(8)
            first_make(6)
            first_make(7)
            first_low(4)
            first_low(5)
            scan_subtract(9)
            first_h_make(0, 0)
            scan_subtract(10)
            first_h_low(0, 0)
            first_h_make(0, 1)
            scan_subtract(11)
            first_h_low(0, 1)
            first_low(6)
            first_h_make(1, 0)
            first_h_low(1, 0)
            first_h_make(1, 1)
            first_h_low(1, 1)
            first_low(7)
            take_coeff(DOWN)
            first_make(8)
            first_h_make(2, 0)
            first_make(9)
            first_h_low(2, 0)
            first_h_make(2, 1)
            first_make(10)
            first_h_low(2, 1)
            first_make(11)
            first_low(8)
            first_low(9)
            first_h_make(3, 0)
            first_h_low(3, 0)
            first_low(10)
            first_low(11)
            first_h_make(3, 1)
            first_h_low(3, 1)
            for k in range(2):
                nc.vector.memset(ln[:, 2, k:k + 1], 0.0).then_inc(attn_acc, 1)
            for t in range(TT):
                dve.wait_ge(down_done, t + 1)
                nc.vector.tensor_copy(y[:, t, :], down_ps[t]).then_inc(y_done, 1)
                if t == 1:
                    for kind in (GATE, UP, DOWN):
                        ffn_make(4, 0, kind)
                if t == 3:
                    w_low(0, 4, 0, GATE)
                if t == 2:
                    for kind in (GATE, UP, DOWN):
                        ffn_make(5, 1, kind)
                if t == 5:
                    w_low(0, 4, 0, UP)
            with dve.Fori(2, 5) as i:
                ffn_iteration(i, make_ffn=True, attn=i - 2)
            ffn_iteration(5, make_ffn=True, attn=3)
            iteration(0, 6, make_nf4=0, last=True)

            for m in range(4):
                dve.wait_ge(qkv_hi, m + 1)
                nc.vector.tensor_tensor(qkv_split[:, m, LO, :], w_qkv[:, m, :],
                                        qkv_split[:, m, HI, :].bitcast(f32), ALU.subtract).then_inc(qkv_lo, 1)
            for m in range(4):
                dve.wait_ge(oT_hi, m + 1)
                nc.vector.tensor_tensor(oT_split[:, LO, :, m * P:(m + 1) * P],
                                        fold_ps[m].rearrange("p (c o) -> p c o", c=4),
                                        oT_split[:, HI, :, m * P:(m + 1) * P].bitcast(f32), ALU.subtract
                                        ).then_inc(oT_lo, 1)

            def MT_low(c):
                dve.wait_ge(MT_hi, c + 1)
                nc.vector.tensor_tensor(MT[:, LO, c, :], four_ps[c], MT[:, HI, c, :].bitcast(f32), ALU.subtract
                                        ).then_inc(MT_lo, 1)

            for m in range(2):
                rows = slice(64 * m + 32, 64 * m + 64)
                dve.wait_ge(lora_hi, m + 1)
                nc.vector.tensor_tensor(A_gu[rows, m, :], A_gu_raw[rows, :], A_gu[rows, m, :].bitcast(f32),
                                        ALU.subtract).then_inc(A_low, 1)
            dve.wait_ge(oT_tr, 4)
            dve.wait_ge(qkv_lo, 4)
            nc.vector.memset(A_down[64:128, :].bitcast(f32), 0.0).then_inc(lora_zero, 1)
            for t in range(TT):
                dve.wait_ge(x_again[t // 4], 16)
                normalise(x1, t, xn_again)
                if t == TT // 2 - 1:
                    MT_low(0)
            MT_low(1)
            dve.wait_ge(lora_hi, 9)
            nc.vector.tensor_tensor(A_down[32:64, :], A_down_raw[32:64, :], A_down[32:64, :].bitcast(f32),
                                    ALU.subtract).then_inc(A_low, 1)
            MT_low(2)
            MT_low(3)
            for kind in (GATE, UP):
                w_low(1, 0, 0, kind)
            for t in range(TT + 1):
                if t < TT:
                    dve.wait_ge(x1_sum, t + 1)
                    dve.wait_ge(xn_again, t + 1)
                    nc.vector.tensor_tensor(x1[:, t, :], x1[:, t, :], sum_ps[:, t % 2, :], ALU.add
                                            ).then_inc(x1_ready, 1)
                if t > 0:
                    u = t - 1
                    dve.wait_ge(x1_hi, u + 1)
                    nc.vector.tensor_tensor(xT[:, LO, :, u * P:(u + 1) * P],
                                            tr_ps[:, u % 2, :].rearrange("p (c t) -> p c t", c=HC),
                                            xT[:, HI, :, u * P:(u + 1) * P].bitcast(f32), ALU.subtract
                                            ).then_inc(x1_lo, 1)
            with dve.Fori(0, 6) as i:
                iteration(1, i, make_nf4=i + 1)
            iteration(1, 6, last=True)

        @block.tensor
        def _(pe):
            def transpose4(bank, src, accumulate=False):
                for c in range(HC):
                    last = nc.tensor.matmul(bank[:, c * P:(c + 1) * P], src(c), ident[:], is_transpose=True,
                                            start=(c == 0), stop=(c == HC - 1 and not accumulate))
                return last

            pe.wait_ge(const_ready, 3)
            for t in range(TT):
                pe.wait_ge(xn_ready, 6 + t + 1)
                if t >= 6:
                    pe.wait_ge(xT_lo, t - 5)
                transpose4(xT_ps[t], lambda c: y[:, t, c * P:(c + 1) * P]).then_inc(xT_tr, 1)
                if t == 3:
                    pe.wait_ge(sign_ready, 1)
                    transpose4(sum_ps[:, 1, :], lambda q: raw_s[:, 0, q * P:(q + 1) * P])
                    pe.wait_ge(first_loaded[0], 32)
                    transpose4(sum_ps[:, 0, :], lambda q: base_s[:, 0, q * P:(q + 1) * P]).then_inc(tr_done, 1)
            pe.wait_ge(xT_lo, TT)

            def total(m):
                pe.wait_ge(part_ready, m + 1)
                nc.tensor.matmul(sum_ps[:, 0, m:m + 1], ones[:], abs_part[:, m:m + 1], start=True, stop=True
                                 ).then_inc(total_ready, 1)

            def first_unit(n):
                if n >= 2:
                    pe.wait_ge(w_lo, n - 1)
                pe.wait_ge(ffn_weight, n + 1)
                transpose4(tr_ps[:, n % 2, :], lambda q: weight_s[:, n % SECTIONS, q * P:(q + 1) * P]).then_inc(tr_done, 1)

            def first_project(kind, c, halves=(0, 1)):
                n = FIRST * kind + c
                pe.wait_ge(w_lo, n + 1)
                for th in halves:
                    if c > 0:
                        pe.wait_ge(silu_done if kind == GATE else h_lo, 2 * c + th - 1)
                    ps = (gate_ps if kind == GATE else up_ps)[:, th, :]
                    for hc in range(HC):
                        for w_part, x_part in PASSES:
                            last = nc.tensor.matmul(ps, first_w(n)[:, w_part, hc * P:(hc + 1) * P],
                                                    xT[:, x_part, hc, th * HALF:(th + 1) * HALF],
                                                    start=(hc == 0 and w_part == x_part == HI),
                                                    stop=(hc == HC - 1 and w_part == LO))
                    last.then_inc(gate_done if kind == GATE else up_done, 1)

            def early_mean(th):
                pe.wait_ge(w_lo, 1)
                for hc in range(HC):
                    for w_part, x_part in PASSES:
                        nc.tensor.matmul(gate_ps[:, th, :], first_w(0)[:, w_part, hc * P:(hc + 1) * P],
                                         xT[:, x_part, hc, th * HALF:(th + 1) * HALF],
                                         start=(hc == 0 and w_part == x_part == HI),
                                         stop=(hc == HC - 1 and w_part == LO))

            def early_sign(th):
                pe.wait_ge(sign_T, 1)
                for hc in range(HC):
                    for x_part in (HI, LO):
                        last = nc.tensor.matmul(up_ps[:, th, :], signT[:, hc * P:(hc + 1) * P],
                                                xT[:, x_part, hc, th * HALF:(th + 1) * HALF],
                                                start=(hc == 0 and x_part == HI), stop=(hc == HC - 1 and x_part == LO))
                last.then_inc(gate_done, 1)

            def first_down(t):
                if t == 0:
                    pe.wait_ge(coeff_ready, 3)
                    pe.wait_ge(w_lo, FIRST_UNITS)
                    pe.wait_ge(h_lo, 2 * FIRST - 1)
                    pe.wait_ge(silu_done, 2 * FIRST)
                if t == TT // 2:
                    pe.wait_ge(h_lo, 2 * FIRST)
                if t in (4, 5):
                    pe.wait_ge(y_done, t - 3)
                for c in range(FIRST):
                    for h_part, w_part in PASSES:
                        last = nc.tensor.matmul(down_ps[t], first_h(c, h_part, t, t + 1).rearrange("p t n -> p (t n)"),
                                                first_w(2 * FIRST + c)[:, w_part, :],
                                                start=(c == 0 and h_part == w_part == HI),
                                                stop=(c == FIRST - 1 and h_part == LO))
                last.then_inc(down_done, 1)

            def unit(block_no, c, par, kind):
                index = unit_index(block_no, c, kind)
                bank = (3 * par + kind) % 2
                pe.wait_ge(w_hi, index - 1)
                pe.wait_ge(w_lo, index - 1)
                if block_no == 0:
                    pe.wait_ge(ffn_weight, index + 1)
                else:
                    pe.wait_ge(nf4_weight, c + 1)
                last = transpose4(tr_ps[:, bank, :], lambda n: weight[:, par, kind * HID + n * P:kind * HID + (n + 1) * P],
                                  accumulate=block_no == 1)
                if block_no == 1 and kind == DOWN:
                    pe.wait_ge(A_down_ready, c + 1)
                    last = nc.tensor.matmul(tr_ps[:, bank, :], A_down_now[:, par, :], B_downT[:, :],
                                            start=False, stop=True)
                elif block_no == 1:
                    for n in range(HC):
                        last = nc.tensor.matmul(tr_ps[:, bank, n * P:(n + 1) * P], A_gu[:, kind, n * P:(n + 1) * P],
                                                B_guT[:, ds(c * P, P)], start=False, stop=(n == HC - 1))
                last.then_inc(tr_done, 1)

            def project(block_no, c, par, kind, th):
                n = CHUNKS * block_no + c
                if th == 0:
                    pe.wait_ge(w_lo, unit_index(block_no, c, kind) + 1)
                if par == 1:
                    pe.wait_ge(silu_done if kind == GATE else h_lo, 2 * n + th - 1)
                else:
                    pe.wait_ge(y_done, TT // 2 * n + (3 if kind == GATE else 7) + th - 2 * TT)
                ps = (gate_ps if kind == GATE else up_ps)[:, th, :]
                for hc in range(HC):
                    for w_part, x_part in PASSES:
                        last = nc.tensor.matmul(ps, guT[:, par, kind, w_part, hc * P:(hc + 1) * P],
                                                xT[:, x_part, hc, th * HALF:(th + 1) * HALF],
                                                start=(hc == 0 and w_part == x_part == HI),
                                                stop=(hc == HC - 1 and w_part == LO))
                last.then_inc(gate_done if kind == GATE else up_done, 1)

            def down(block_no, i, t):
                q = PAIRS * block_no + i
                done = TT * (q - 1) + t
                if t == 0:
                    pe.wait_ge(w_lo, 6 * q + 6)
                    pe.wait_ge(h_lo, 4 * q + 3)
                if t == TT // 2:
                    pe.wait_ge(h_lo, 4 * q + 4)
                if t in (2, 3):
                    pe.wait_ge(silu_done, 4 * q + 1 + t)
                elif t < 6:
                    pe.wait_ge(y_done, done - 3)
                for par in range(2):
                    for h_part, w_part in PASSES:
                        last = nc.tensor.matmul(down_ps[t], h_split[:, par, h_part, t * P:(t + 1) * P],
                                                downT[:, par, w_part, :],
                                                start=(par == 0 and h_part == w_part == HI),
                                                stop=(par == 1 and h_part == LO))
                last.then_inc(down_done, 1)

            def fold_transposes():
                pe.wait_ge(w_lo, 3 * CHUNKS)
                pe.wait_ge(B_nat_ready, 3)
                for bank, nat in enumerate((B_qkv_nat, B_o_nat)):
                    for j in range(4):
                        last = nc.tensor.matmul(tr_ps[0:64, bank, j * P:(j + 1) * P], nat[:, j, :], ident[:],
                                                is_transpose=True, start=(j == 0), stop=(j == 3))
                    last.then_inc(B_tr, 1)

            def fold_lora():
                pe.wait_ge(B_T_ready, 2)
                pe.wait_ge(fold_loaded, 16 * 5)
                for m in range(4):
                    if m >= 2:
                        pe.wait_ge(y_done, TT * GROUPS - TT + m + 1)
                    nc.tensor.matmul(fold_ps[m], B_qkvT[0:64, m * P:(m + 1) * P], A_attn[0:64, :],
                                     start=True, stop=True).then_inc(lora_qkv, 1)

            def iteration(block_no, i, last=False):
                a, b = 2 * i, 2 * i + 1
                unit(block_no, a, 0, DOWN)
                project(block_no, a, 0, GATE, 0)
                unit(block_no, b, 1, GATE)
                project(block_no, a, 0, GATE, 1)
                unit(block_no, b, 1, UP)
                project(block_no, a, 0, UP, 0)
                unit(block_no, b, 1, DOWN)
                project(block_no, a, 0, UP, 1)
                for kind in (GATE, UP):
                    for th in range(2):
                        project(block_no, b, 1, kind, th)
                for t in range(TT):
                    down(block_no, i, t)
                    if last and block_no == 0 and t == 2:
                        fold_transposes()
                    if last and block_no == 0 and t == 5:
                        fold_lora()
                    if t == 3 and not last:
                        unit(block_no, a + 2, 0, GATE)
                    if t == 5 and not last:
                        unit(block_no, a + 2, 0, UP)

            for th in range(2):
                early_mean(th)
            early_sign(0)
            total(GATE)
            early_sign(1)
            first_unit(1)
            first_unit(2)
            first_project(GATE, 1)
            first_unit(3)
            first_project(GATE, 2)
            first_project(GATE, 3, (0,))
            total(UP)
            first_project(GATE, 3, (1,))
            first_unit(4)
            first_unit(5)
            first_project(UP, 0)
            first_unit(6)
            first_project(UP, 1)
            first_unit(7)
            first_project(UP, 2, (0,))
            total(DOWN)
            first_project(UP, 2, (1,))
            first_unit(8)
            first_unit(9)
            first_project(UP, 3, (0,))
            first_unit(10)
            first_unit(11)
            first_project(UP, 3, (1,))
            for t in range(TT):
                first_down(t)
                if t == 3:
                    unit(0, 4, 0, GATE)
                if t == 5:
                    unit(0, 4, 0, UP)
            with pe.Fori(2, 6) as i:
                iteration(0, i)
            iteration(0, 6, last=True)

            pe.wait_ge(attn_scaled, 5 * 4 + 1)
            for j in range(4):
                pe.wait_ge(qkv_full, j + 1)
                transpose4(fold_ps[j], lambda c: w_o[:, j, c * P:(c + 1) * P], accumulate=True)
                for c in range(4):
                    last = nc.tensor.matmul(fold_ps[j][:, c * P:(c + 1) * P], A_attn[0:64, c * P:(c + 1) * P],
                                            B_oT[0:64, j * P:(j + 1) * P], start=False, stop=(c == 3))
                last.then_inc(oT_tr, 1)
            for n in range(5):
                if n < 4:
                    pe.wait_ge(lora_lo, 2 if 4 * n + 4 <= HALF_CHUNKS else 4)
                else:
                    pe.wait_ge(lora_lo, 6)
                if n >= 2:
                    pe.wait_ge(lora_T, n - 1)
                else:
                    pe.wait_ge(oT_lo, n + 1)
                if n < 4:
                    chunks = range(4 * n, min(4 * n + 4, CHUNKS))
                    for c in chunks:
                        nat = B_gu_nat[c // HALF_CHUNKS][:, c % HALF_CHUNKS, :, :, :].rearrange("p m s r -> p (m s r)")
                        last = nc.tensor.matmul(tr_ps[:, n % 2, (c - 4 * n) * P:(c - 4 * n + 1) * P], nat, ident[:],
                                                is_transpose=True, start=(c == 4 * n), stop=(c == chunks[-1]))
                else:
                    for j in range(4):
                        last = nc.tensor.matmul(tr_ps[0:64, n % 2, j * P:(j + 1) * P],
                                                B_down_nat[:, j, :, :].rearrange("p s r -> p (s r)"), ident[:],
                                                is_transpose=True, start=(j == 0), stop=(j == 3))
                last.then_inc(lora_tr, 1)
            pe.wait_ge(y_done, TT * GROUPS)
            pe.wait_ge(qkv_full, 4)
            pe.wait_ge(qkv_lo, 4)
            pe.wait_ge(oT_lo, 4)
            for hc in range(HC):
                for m in range(4):
                    for a_part, b_part in PASSES:
                        last = nc.tensor.matmul(four_ps[hc], qkv_split[:, m, a_part, hc * P:(hc + 1) * P],
                                                oT_split[:, b_part, m, :],
                                                start=(m == 0 and a_part == b_part == HI),
                                                stop=(m == 3 and a_part == LO))
                last.then_inc(MT_done, 1)
            pe.wait_ge(lora_T, 5)
            pe.wait_ge(A_low, 2)
            unit(1, 0, 0, GATE)
            unit(1, 0, 0, UP)

            def x1_transpose(t):
                pe.wait_ge(x1_ready, t + 1)
                if t < 2:
                    pe.wait_ge(w_lo, 3 * CHUNKS + t + 1)
                else:
                    pe.wait_ge(x1_lo, t - 1)
                transpose4(tr_ps[:, t % 2, :], lambda c: x1[:, t, c * P:(c + 1) * P]).then_inc(x1_tr, 1)

            pe.wait_ge(MT_lo, HC)
            for t in range(TT):
                if t >= 2:
                    pe.wait_ge(x1_ready, t - 1)
                for hc in range(HC):
                    for x_part, m_part in PASSES:
                        last = nc.tensor.matmul(sum_ps[:, t % 2, :], xT[:, x_part, hc, t * P:(t + 1) * P],
                                                MT[:, m_part, hc, :],
                                                start=(hc == 0 and x_part == m_part == HI),
                                                stop=(hc == HC - 1 and x_part == LO))
                last.then_inc(x1_sum, 1)
                if t > 0:
                    x1_transpose(t - 1)
            x1_transpose(TT - 1)
            pe.wait_ge(x1_lo, TT)
            with pe.Fori(0, 6) as i:
                iteration(1, i)
            iteration(1, 6, last=True)


_INS = ["L0_attn_x", "L0_attn_codes_attn", "L0_attn_scales_attn", "L0_attn_codes_gu", "L0_attn_scales_gu",
        "L0_attn_codes_down", "L0_attn_scales_down", "L0_attn_lora_A_h", "L0_attn_lora_A_down",
        "L0_attn_lora_B_attn", "L0_attn_lora_B_gu", "L0_attn_lora_B_down",
        "L0_ffn_w1", "L0_ffn_mean_w1", "L0_ffn_w2", "L0_ffn_mean_w2", "L0_ffn_w3", "L0_ffn_mean_w3"]


def kernel(**inputs):
    import numpy as np
    import concourse.bacc as bacc
    from concourse.bass_utils import run_bass_kernel_spmd

    nc = bacc.Bacc("TRN2", target_bir_lowering=False, num_devices=1)
    arrays, args = {}, []
    for name in _INS:
        a = np.ascontiguousarray(inputs[name])
        arrays[name] = a
        args.append(nc.dram_tensor(name, a.shape, mybir.dt.from_np(a.dtype), kind="ExternalInput").ap())
    shape = inputs["L0_attn_x"].shape
    args.append(nc.dram_tensor("out", shape, mybir.dt.float32, kind="ExternalOutput").ap())
    block_kernel(nc, *args)
    result = run_bass_kernel_spmd(nc, [arrays], core_ids=[0])
    return result.results[0]["out"]
```
